# Optimizing a Trainium2 kernel written in Bass

```python
import numpy as np
import jax
import jax.numpy as jnp

def _softmax(x, axis=-1):
    return jax.nn.softmax(x, axis=axis)

def _gelu(x):
    return jax.nn.gelu(x, approximate=True)

def _silu(x):
    return jax.nn.silu(x)

def _sigmoid(x):
    return jax.nn.sigmoid(x)

def _layernorm(x, axis=-1, eps=1e-05):
    m = jnp.mean(x, axis=axis, keepdims=True)
    v = jnp.var(x, axis=axis, keepdims=True)
    return (x - m) / jnp.sqrt(v + eps)

def _scatter_add(tgt, idx, src, axis=0):
    return tgt.at[idx].add(src)

def _segment_sum(src, seg, n):
    return jax.ops.segment_sum(src, seg, n)
kernel_name = 'mk_decoder_postln_d1_seqx_r8_c2f9c2'

def setup_inputs(seed: int=0):
    np.random.seed(seed)
    _w = jnp.asarray

    def _rec_inputs():
        import jax
        import jax.numpy as jnp
        _rk = jax.random.key(seed)
        x = -0.0002928 + 1 * jax.random.normal(jax.random.fold_in(_rk, 1), (4, 256, 128), jnp.float32)
        _lenS = 256 - jax.random.randint(jax.random.fold_in(_rk, 7), (4,), 0, max(1, 256 // 4) + 1, jnp.int32)
        _lenS2 = 512 - jax.random.randint(jax.random.fold_in(_rk, 8), (4,), 0, max(1, 512 // 4) + 1, jnp.int32)
        _ctx_1024P = jax.random.normal(jax.random.fold_in(_rk, 11), (4, 16, 128), jnp.float32)
        _ctx_1024c = jax.random.dirichlet(jax.random.fold_in(_rk, 511), 0.3 * jnp.ones((16,), jnp.float32), (4, 512))
        _ctx_1024t = jnp.einsum('bsk,bkd->bsd', _ctx_1024c, _ctx_1024P)
        _ctx_1024t = _ctx_1024t * jax.lax.rsqrt(jnp.mean(jnp.square(_ctx_1024t)) + 1e-12) * 0.953939
        ctx_1024 = -1.39393e-06 + 0.999914 * (_ctx_1024t + 0.3 * jax.random.normal(jax.random.fold_in(_rk, 611), (4, 512, 128), jnp.float32))
        _validS = jnp.arange(256)[None, :] < _lenS[:, None]
        _validS2 = jnp.arange(512)[None, :] < _lenS2[:, None]
        _causal = jnp.tril(jnp.ones((256, 256), dtype=bool))
        mask_1x1xSxS2_bk1 = jnp.broadcast_to(_validS2[0:1, None, None, :], (1, 1, 256, 512))
        return (x, ctx_1024, mask_1x1xSxS2_bk1)
    x, ctx_1024, mask_1x1xSxS2_bk1 = _rec_inputs()

    def _L0_attn_setup():
        import jax, jax.numpy as jnp
        import numpy as np
        NUM_HEADS, D_HEAD, D_MODEL, N_CTX = (16, 64, 128, 256)
        BATCH, SEQ = (4, 256)
        key = jax.random.key(seed)
        kx, kq, kk, kv, ko = jax.random.split(key, 5)
        x = jax.random.normal(kx, (BATCH, SEQ, D_MODEL), dtype=jnp.float32)
        Q = jax.random.normal(kq, (NUM_HEADS, D_HEAD, D_MODEL), dtype=jnp.float32) / np.sqrt(D_MODEL)
        K = jax.random.normal(kk, (NUM_HEADS, D_HEAD, D_MODEL), dtype=jnp.float32) / np.sqrt(D_MODEL)
        V = jax.random.normal(kv, (NUM_HEADS, D_HEAD, D_MODEL), dtype=jnp.float32) / np.sqrt(D_MODEL)
        O = jax.random.normal(ko, (D_MODEL, NUM_HEADS * D_HEAD), dtype=jnp.float32) / np.sqrt(NUM_HEADS * D_HEAD)
        return {'x': x, 'Q': Q, 'K': K, 'V': V, 'O': O}
    _L0_attn_all = _L0_attn_setup()
    _L0_attn_in = {k: v for k, v in _L0_attn_all.items() if k in ('Q', 'K', 'V', 'O')}
    del _L0_attn_all

    def _L0_xattn_setup():
        import jax, jax.numpy as jnp
        import numpy as np
        B, S, D, H = (2, 256, 128, 16)
        DH = D // H

        def _rope(x):
            s, dh = (x.shape[2], x.shape[3])
            inv = jnp.exp(jnp.arange(0, dh, 2, dtype=jnp.float32) * (-(4.0 * jnp.log(jnp.float32(10.0))) / dh))
            pos = jnp.arange(s, dtype=jnp.float32)[:, None]
            sin = jnp.sin(pos * inv)
            cos = jnp.cos(pos * inv)
            x1 = x[..., 0::2]
            x2 = x[..., 1::2]
            out = jnp.stack([x1 * sin - x2 * cos, -x1 * cos - x2 * sin], axis=-1)
            return out.reshape(x.shape)
        key = jax.random.key(seed)
        ks = jax.random.split(key, 12)
        f = lambda k, sh: jax.random.normal(k, sh, dtype=jnp.float32)
        inp = {'q': f(ks[0], (B, S, D)), 'k': f(ks[1], (B, S, D)), 'v': f(ks[2], (B, S, D))}
        scale = 1.0 / np.sqrt(D)
        names = ['q', 'k', 'v', 'o']
        for i, n in enumerate(names):
            inp['W' + n] = f(ks[3 + i], (D, D)) * scale
            inp['b' + n] = f(ks[7 + i], (D,)) * scale
        inp['mask'] = jnp.triu(jnp.ones((S, S), dtype=bool), k=1)[None, None]
        return inp
    _L0_xattn_all = _L0_xattn_setup()
    _L0_xattn_in = {k: v for k, v in _L0_xattn_all.items() if k in ('Wq', 'bq', 'Wk', 'bk', 'Wv', 'bv', 'Wo', 'bo')}
    del _L0_xattn_all

    def _L0_ffn_setup():
        import jax, jax.numpy as jnp
        import numpy as np
        D_MODEL, HIDDEN, N_EXPERTS, TOP_K = (128, 256, 8, 2)
        RMS_EPS = 1e-06
        key = jax.random.key(seed)
        ks = jax.random.split(key, 6)
        B, S = (4, 256)
        return {'x': jax.random.normal(ks[0], (B, S, D_MODEL), jnp.float32), 'norm_weight': jnp.ones((D_MODEL,), jnp.float32), 'gate_w': jax.random.normal(ks[1], (N_EXPERTS, D_MODEL), jnp.float32) * 0.02, 'w1': jax.random.normal(ks[2], (N_EXPERTS, HIDDEN, D_MODEL), jnp.float32) * 0.02, 'b1': jnp.zeros((N_EXPERTS, HIDDEN), jnp.float32), 'w2': jax.random.normal(ks[3], (N_EXPERTS, D_MODEL, HIDDEN), jnp.float32) * 0.02, 'b2': jnp.zeros((N_EXPERTS, D_MODEL), jnp.float32)}
    _L0_ffn_all = _L0_ffn_setup()
    _L0_ffn_in = {k: v for k, v in _L0_ffn_all.items() if k in ('norm_weight', 'gate_w', 'w1', 'b1', 'w2', 'b2')}
    del _L0_ffn_all
    return {'x': x, 'ctx_1024': ctx_1024, 'mask_1x1xSxS2_bk1': mask_1x1xSxS2_bk1, 'L0_attn_Q': _L0_attn_in['Q'], 'L0_attn_K': _L0_attn_in['K'], 'L0_attn_V': _L0_attn_in['V'], 'L0_attn_O': _L0_attn_in['O'], 'L0_xattn_Wq': _L0_xattn_in['Wq'], 'L0_xattn_bq': _L0_xattn_in['bq'], 'L0_xattn_Wk': _L0_xattn_in['Wk'], 'L0_xattn_bk': _L0_xattn_in['bk'], 'L0_xattn_Wv': _L0_xattn_in['Wv'], 'L0_xattn_bv': _L0_xattn_in['bv'], 'L0_xattn_Wo': _L0_xattn_in['Wo'], 'L0_xattn_bo': _L0_xattn_in['bo'], 'L0_ffn_norm_weight': _L0_ffn_in['norm_weight'], 'L0_ffn_gate_w': _L0_ffn_in['gate_w'], 'L0_ffn_w1': _L0_ffn_in['w1'], 'L0_ffn_b1': _L0_ffn_in['b1'], 'L0_ffn_w2': _L0_ffn_in['w2'], 'L0_ffn_b2': _L0_ffn_in['b2']}

def reference(x, ctx_1024, mask_1x1xSxS2_bk1, L0_attn_Q, L0_attn_K, L0_attn_V, L0_attn_O, L0_xattn_Wq, L0_xattn_bq, L0_xattn_Wk, L0_xattn_bk, L0_xattn_Wv, L0_xattn_bv, L0_xattn_Wo, L0_xattn_bo, L0_ffn_norm_weight, L0_ffn_gate_w, L0_ffn_w1, L0_ffn_b1, L0_ffn_w2, L0_ffn_b2):
    import jax
    import jax.numpy as jnp

    def _L0_attn_ref(x, Q, K, V, O):
        import jax, jax.numpy as jnp
        import numpy as np
        NUM_HEADS, D_HEAD, D_MODEL, N_CTX = (16, 64, 128, 256)
        BATCH, SEQ = (4, 256)
        q = jnp.einsum('nhm,btm->bnth', Q, x)
        k = jnp.einsum('nhm,btm->bnth', K, x)
        v = jnp.einsum('nhm,btm->bnth', V, x)
        scores = jnp.einsum('bnqh,bnkh->bnqk', q, k)
        s = x.shape[1]
        causal = jnp.tril(jnp.ones((s, s), dtype=bool))
        masked = jnp.where(causal, scores, jnp.float32(-10000000000.0))
        attn = jax.nn.softmax(masked, axis=-1)
        z = jnp.einsum('bnqk,bnkh->bnqh', attn, v)
        z = jnp.transpose(z, (0, 2, 1, 3)).reshape(x.shape[0], s, -1)
        return jnp.einsum('ma,bqa->bqm', O, z)

    def _L0_xattn_ref(q, k, v, Wq, bq, Wk, bk, Wv, bv, Wo, bo, mask):
        import jax, jax.numpy as jnp
        import numpy as np
        B, S, D, H = (2, 256, 128, 16)
        DH = D // H

        def _rope(x):
            s, dh = (x.shape[2], x.shape[3])
            inv = jnp.exp(jnp.arange(0, dh, 2, dtype=jnp.float32) * (-(4.0 * jnp.log(jnp.float32(10.0))) / dh))
            pos = jnp.arange(s, dtype=jnp.float32)[:, None]
            sin = jnp.sin(pos * inv)
            cos = jnp.cos(pos * inv)
            x1 = x[..., 0::2]
            x2 = x[..., 1::2]
            out = jnp.stack([x1 * sin - x2 * cos, -x1 * cos - x2 * sin], axis=-1)
            return out.reshape(x.shape)
        b, s, d = q.shape
        h, dh = (H, DH)

        def proj(x, W, bias):
            return (x @ W.T + bias).reshape(b, -1, h, dh).transpose(0, 2, 1, 3)
        Q = proj(q, Wq, bq)
        K = proj(k, Wk, bk)
        V = proj(v, Wv, bv)
        PQ = _rope(Q)
        PK = _rope(K)
        scores = jnp.einsum('bhqd,bhkd->bhqk', PQ, PK)
        neg = jnp.finfo(scores.dtype).min
        scores = jnp.where(mask, neg, scores)
        p = jax.nn.softmax(scores, axis=-1)
        p = jnp.where(mask, jnp.float32(0.0), p)
        out = jnp.einsum('bhqk,bhkd->bhqd', p, V)
        out = out.transpose(0, 2, 1, 3).reshape(b, s, d)
        return out @ Wo.T + bo

    def _L0_ffn_ref(x, norm_weight, gate_w, w1, b1, w2, b2):
        import jax, jax.numpy as jnp
        import numpy as np
        D_MODEL, HIDDEN, N_EXPERTS, TOP_K = (128, 256, 8, 2)
        RMS_EPS = 1e-06
        B, S, D = x.shape
        E = gate_w.shape[0]
        t = x * jax.lax.rsqrt(jnp.mean(x * x, axis=-1, keepdims=True) + RMS_EPS) * norm_weight
        tokens = t.reshape(-1, D)
        T = tokens.shape[0]
        gate_logits = tokens @ gate_w.T
        gate_scores, expert_idx = jax.lax.top_k(gate_logits, TOP_K)
        routing_weights = jax.nn.softmax(gate_scores, axis=-1)
        combine = jnp.zeros((T, E), tokens.dtype).at[jnp.arange(T)[:, None], expert_idx].add(routing_weights)

        def body(acc, params):
            W1, B1, W2, B2, c = params
            h = jax.nn.gelu(tokens @ W1.T + B1, approximate=False)
            o = h @ W2.T + B2
            return (acc + c[:, None] * o, None)
        out, _ = jax.lax.scan(body, jnp.zeros_like(tokens), (w1, b1, w2, b2, combine.T))
        return x + out.reshape(B, S, D)
    x = _layernorm(x + _L0_attn_ref(x, L0_attn_Q, L0_attn_K, L0_attn_V, L0_attn_O), axis=-1)
    x = _layernorm(x + _L0_xattn_ref(x, ctx_1024, ctx_1024, L0_xattn_Wq, L0_xattn_bq, L0_xattn_Wk, L0_xattn_bk, L0_xattn_Wv, L0_xattn_bv, L0_xattn_Wo, L0_xattn_bo, mask_1x1xSxS2_bk1), axis=-1)
    x = _layernorm(x + _L0_ffn_ref(x, L0_ffn_norm_weight, L0_ffn_gate_w, L0_ffn_w1, L0_ffn_b1, L0_ffn_w2, L0_ffn_b2), axis=-1)
    return x

_drawn_inputs = setup_inputs


def setup_inputs(seed=0):
    import zlib

    import numpy as np

    out = dict(_drawn_inputs(seed))
    spreads = {'L0_ffn_norm_weight': (1.0, 0.6), 'L0_ffn_b1': (0.0, 0.8), 'L0_ffn_b2': (0.0, 0.1)}
    factors = {'L0_ffn_w1': 4.199, 'L0_ffn_w2': 3.825}
    for name, (base, spread) in spreads.items():
        noise = np.random.default_rng([zlib.crc32(name.encode()), seed]).standard_normal(out[name].shape)
        drawn = base * np.exp(spread * noise) if base else spread * noise
        out[name] = jnp.asarray(drawn.astype(out[name].dtype))
    for name, factor in factors.items():
        out[name] = (out[name] * factor).astype(out[name].dtype)
    return out
```

```python
from contextlib import ExitStack

import concourse.bass as bass
from concourse import mybir

F32 = mybir.dt.float32
BF16 = mybir.dt.bfloat16
U8 = mybir.dt.uint8
U32 = mybir.dt.uint32
ALU = mybir.AluOpType
ACT = mybir.ActivationFunctionType

B, S, D = 4, 256, 128
SK = 512
H, DH = 16, 64
XH, XD = 16, 8
E, F = 8, 256
P = 128
QT = S // P
KT = SK // P
TILES = B * QT
TOK = B * S
NEG_CAUSAL = -1.0e10
NEG_MASK = -1.0e30
SHIFT_MAX = 1.0e15
TINY = 1.0e-30
LN_EPS = 1e-5
RMS_EPS = 1e-6
PARTS = 3
SROWS = 96
TROWS = SROWS + PARTS


def wait_alone(eng, passed, sem, value):
    eng.wait_ge(sem, value)
    eng.sem_inc(passed, 1)


class Steps:

    def __init__(self, eng, sem, i=0, per=0, base=0):
        self.eng, self.sem, self.i, self.per, self.base, self.n = eng, sem, i, per, base, 0

    def link(self, ins, passed=None):
        ins.then_inc(self.sem, 1)
        self.n += 1
        value = self.i * self.per + self.base + self.n
        if passed is None:
            self.eng.wait_ge(self.sem, value)
        else:
            wait_alone(self.eng, passed, self.sem, value)

    def done(self):
        assert self.n == self.per, (self.n, self.per)


def build(nc, x, ctx_in, mask, aQ, aK, aV, aO, Wq, bq, Wk, bk, Wv, bv, Wo, bo, norm_w, gate_w,
          w1, b1, w2, b2, c_ident, c_causal, c_rope, c_fill, c_iota, out):
    with ExitStack() as top:
        def sb(name, shape, dt=F32, scope=top):
            return scope.enter_context(nc.sbuf_tensor(name, shape, dt))

        def sem(name):
            return top.enter_context(nc.semaphore(name))

        x_n = sb("x_n", [P, TILES, D])
        x1_n = sb("x1_n", [P, TILES, D])
        x2_n = sb("x2_n", [P, TILES, D])
        ident = sb("ident", [P, P])
        identb = sb("identb", [P, P], BF16)
        xw_T = sb("xw_T", [P, 4, D])
        xws_T = sb("xws_T", [P, 2, D])
        cols = sb("cols", [P, 27])
        cols_s = sb("cols_s", [P, 2])
        bv_bc = sb("bv_bc", [P, D])
        bo_bc = sb("bo_bc", [P, D])
        b2_n = sb("b2_n", [E, D])
        rope = sb("rope", [P, 2, SK])
        maskb = sb("maskb", [P, QT, SK], BF16)
        mask_T = sb("mask_T", [P, KT, S], BF16)
        v_aug = sb("v_aug", [P, B, KT, XH, XD + 1])
        w1_T = sb("w1_T", [P, 2 * E, P])
        w2_T = sb("w2_T", [P, 2 * E, D])
        neghalf = sb("neghalf", [P, TILES])
        iota = sb("iota", [P, E])
        ps = [top.enter_context(nc.psum_tensor(f"ps{i}", [P, 512], F32)) for i in range(2)]
        ps2 = [top.enter_context(nc.psum_tensor(f"pd{i}", [P, 1024], F32)) for i in range(2)]
        psx = [top.enter_context(nc.psum_tensor(f"px{i}", [P, 512], F32)) for i in range(2)]

        k_parts_d = nc.dram_tensor("k_parts_d", (B, PARTS, XH, XD, SK), BF16, kind="Internal").ap()
        q_parts_d = nc.dram_tensor("q_parts_d", (2, PARTS, XH, XD, 2 * S), BF16, kind="Internal").ap()

        passed = sem("passed")
        self_block(nc, top, sem, locals())
        cross_block(nc, top, sem, locals())
        moe_block(nc, top, sem, locals())


def self_block(nc, top, sem, g):
    passed = g["passed"]
    (x, ctx_in, mask, aQ, aK, aV, aO, Wq, bq, Wk, bk, Wv, bv, Wo, bo, norm_w, gate_w, w1, b1, w2, b2) = (
        g[k] for k in ("x", "ctx_in", "mask", "aQ", "aK", "aV", "aO", "Wq", "bq", "Wk", "bk", "Wv", "bv", "Wo",
                       "bo", "norm_w", "gate_w", "w1", "b1", "w2", "b2"))
    (x_n, x1_n, ident, identb, xw_T, xws_T, cols, cols_s, bv_bc, bo_bc, b2_n, rope, maskb, mask_T, v_aug, w1_T,
     w2_T, neghalf, iota, ps, ps2, psx, k_parts_d) = (
        g[k] for k in ("x_n", "x1_n", "ident", "identb", "xw_T", "xws_T", "cols", "cols_s", "bv_bc", "bo_bc",
                       "b2_n", "rope", "maskb", "mask_T", "v_aug", "w1_T", "w2_T", "neghalf", "iota", "ps",
                       "ps2", "psx", "k_parts_d"))
    c_ident, c_causal, c_rope, c_iota = (g[k] for k in ("c_ident", "c_causal", "c_rope", "c_iota"))

    with ExitStack() as st:
        def sb(name, shape, dt=F32):
            return st.enter_context(nc.sbuf_tensor(name, shape, dt))

        q_raw = sb("q_raw", [DH, H, D])
        k_raw = sb("k_raw", [DH, H, D])
        v_raw = sb("v_raw", [P, 8, D])
        o_raw = sb("o_raw", [P, H * DH])
        xw_raw = sb("xw_raw", [P, 4, D])
        rows = sb("rows", [27, D])
        rows_s = sb("rows_s", [2, D])
        mask_raw = sb("mask_raw", [P, QT, SK], U8)
        causal = sb("causal", [P, S])
        qk_T = sb("qk_T", [P, H, D])
        v_T = sb("v_T", [P, H * DH])
        o_T = sb("o_T", [P, 8, D])
        x_T = sb("x_T", [P, TOK])
        xb_T = sb("xb_T", [P, S])
        y_T = sb("y_T", [P, H, S])
        v_n = sb("v_n", [P, QT, H * DH])
        prob = sb("prob", [P, 4, 3 * P])
        prob_T = sb("prob_T", [P, 4, 3 * P])
        z_T = sb("z_T", [P, 8, S])
        nmax = sb("nmax", [P, 4, 2])
        rsum = sb("rsum", [P, 4, 2])
        rinv = sb("rinv", [P, 4, 2])
        res = sb("res", [P, QT, D])
        stats = sb("stats", [P, QT, 6])
        mv = sb("mv", [P, QT, 2])
        rstd = sb("rstd", [P, QT])
        ctx_n = sb("ctx_n", [P, KT, D])
        ctx_T = sb("ctx_T", [P, SK])
        e_raw = sb("e_raw", [P, 8, P])
        rot = sb("rot", [P, 2, SK])
        k_parts = sb("k_parts", [P, PARTS, SK], BF16)

        ld_x = sem("ld_x"); ld_qk = sem("ld_qk"); ld_v = sem("ld_v"); ld_o = sem("ld_o")
        ld_id = sem("ld_id"); ld_ca = sem("ld_ca"); ld_xw = sem("ld_xw"); ld_rows = sem("ld_rows")
        ld_mask = sem("ld_mask"); ld_tab = sem("ld_tab"); ld_bc = sem("ld_bc")
        ld_ctx = sem("ld_ctx"); ld_e = sem("ld_e")
        identb_ready = sem("identb_ready"); maskb_ready = sem("maskb_ready"); rows_s_ready = sem("rows_s_ready")
        consts_ready = sem("consts_ready"); setup_ready = sem("setup_ready")
        setup_dve = sem("setup_dve"); setup_act = sem("setup_act")
        xb_ready = sem("xb_ready"); proj_ready = sem("proj_ready"); proj_dve = sem("proj_dve")
        proj_act = sem("proj_act"); score_ready = sem("score_ready"); masked = sem("masked")
        exp_ready = sem("exp_ready"); rinv_ready = sem("rinv_ready"); prob_ready = sem("prob_ready")
        prob_T_ready = sem("prob_T_ready"); prob_T_copied = sem("prob_T_copied"); pv_ready = sem("pv_ready")
        z_copied = sem("z_copied"); var_ready = sem("var_ready"); rstd_ready = sem("rstd_ready")
        kparts_ready = sem("kparts_ready"); kparts_stored = sem("kparts_stored")
        dve_chain = sem("dve_chain"); pool_chain = sem("pool_chain")

        ITEMS = (["y0", "v0", "y1", "v1", "v2", "v3"] + [f"y{j}" for j in range(2, 8)]
                 + ["ctx", "k0", "k1", "cv", "w1", "w2", "o0", "o1"])
        BY = {n: ("act" if n[0] == "v" or n in ("ctx", "w1", "w2") else "dve") for n in ITEMS}
        NI = len(ITEMS)
        N_BY = {e: sum(BY[n] == e for n in ITEMS) for e in ("act", "dve")}
        AT = {n: ITEMS.index(n) for n in ITEMS}
        NTH = {n: sum(BY[m] == BY[n] for m in ITEMS[:AT[n]]) + 1 for n in ITEMS}
        assert NI % 2 == 0

        def emptied(b, name):
            return BY[name], (b + 1) * N_BY[BY[name]] + NTH[name]

        def wait_bank(pe, b, name):
            n = AT[name] - 2
            eng, v = emptied(b, ITEMS[n]) if n >= 0 else emptied(b - 1, ITEMS[n + NI])
            pe.wait_ge(proj_act if eng == "act" else proj_dve, v)

        psG = ps
        psS = [ps2[0][:, 0:512], ps2[0][:, 512:1024]]
        psT = [ps2[1][:, 0:512], ps2[1][:, 512:1024]]
        psZ = psx
        banks = [ps[0][:, :], ps[1][:, :]] + psS + psT + [psx[0][:, :], psx[1][:, :]]
        SETUP = ["x0", "x1", "qk0", "qk1", "qk2", "qk3", "v0", "v1", "o0", "o1", "xw", "cols", "mask"]

        block = st.enter_context(nc.Block())

        @block.sync
        def _(sp):
            sp.dma_start(ident[:, :], c_ident).then_inc(ld_id, 16)
            xv = x.rearrange("b (t p) m -> p (b t) m", p=P)
            sp.dma_start(x_n[:, 0:4, :], xv[:, 0:4, :]).then_inc(ld_x, 16)
            sp.dma_start(x_n[:, 4:8, :], xv[:, 4:8, :]).then_inc(ld_x, 16)
            sp.dma_start(v_raw[:, :, :], aV.rearrange("(j two) h m -> (two h) j m", two=2)).then_inc(ld_v, 16)
            sp.dma_start(o_raw[:, :], aO).then_inc(ld_o, 16)
            sp.dma_start(causal[:, :], g["c_causal"]).then_inc(ld_ca, 16)
            for n, w in enumerate((Wq, Wk, Wv, Wo)):
                sp.dma_start(xw_raw[:, n, :], w).then_inc(ld_xw, 16)
            sp.dma_start(mask_raw[:, :, :], mask.rearrange("a b (t p) k -> p (a b t) k", p=P)).then_inc(ld_mask, 16)
            sp.dma_start(rope[:, :, :], c_rope).then_inc(ld_tab, 16)

            def load_cross(b):
                sp.dma_start(ctx_n[:, :, :], ctx_in[b].rearrange("(t p) m -> p t m", p=P)).then_inc(ld_ctx, 16)

            def load_experts(b):
                for e in range(2):
                    sp.dma_start(e_raw[:, 2 * e:2 * e + 2, :],
                                 w1[2 * b + e].rearrange("(t p) d -> p t d", p=P)).then_inc(ld_e, 16)
                    sp.dma_start(e_raw[:, 4 + 2 * e:6 + 2 * e, :],
                                 w2[2 * b + e].rearrange("d (t p) -> d t p", p=P)).then_inc(ld_e, 16)

            def store_parts(b):
                sp.wait_ge(kparts_ready, b + 1)
                for c in range(PARTS):
                    sp.dma_start(k_parts_d[b, c].rearrange("h d k -> (h d) k"),
                                 k_parts[:, c, :]).then_inc(kparts_stored, 16)

            load_cross(0)
            load_experts(0)
            sp.sem_inc(kparts_stored, 1)
            with sp.Fori(0, B - 1) as b:
                sp.wait_ge(proj_ready, b * NI + AT["ctx"] + 1)
                load_cross(b + 1)
                store_parts(b)
                sp.wait_ge(proj_ready, b * NI + AT["w2"] + 1)
                load_experts(b + 1)
            store_parts(B - 1)
            sp.wait_ge(kparts_stored, 16 * PARTS * B + 1)

        @block.gpsimd
        def _(pool):
            pool.memset(neghalf[:, :], -0.5).then_inc(consts_ready, 1)
            pool.memset(v_aug[:, :, :, :, XD:XD + 1], 1.0).then_inc(consts_ready, 1)
            with pool.Fori(0, B) as b:
                for h in range(H):
                    s = h % 4
                    pool.wait_ge(rinv_ready, b * H + h + 1)
                    nc.gpsimd.tensor_tensor(prob[:, s, 0:P], prob[:, s, 0:P],
                                            rinv[:, s, 0:1].broadcast_to((P, P)), ALU.mult)
                    nc.gpsimd.tensor_tensor(prob[:, s, P:3 * P], prob[:, s, P:3 * P],
                                            rinv[:, s, 1:2].broadcast_to((P, S)), ALU.mult).then_inc(prob_ready, 1)
                ch = Steps(pool, pool_chain, b, 1)
                wait_alone(pool, passed, var_ready, b + 1)
                ch.link(nc.gpsimd.tensor_scalar(rstd[:, :], mv[:, :, 1], LN_EPS, None, ALU.add))
                nc.gpsimd.tensor_tensor(rstd[:, :], rstd[:, :], neghalf[:, 0:QT], ALU.pow).then_inc(rstd_ready, 1)
                ch.done()

        @block.scalar
        def _(act):
            act.dma_start(q_raw[:, :, :], aQ.rearrange("n h m -> h n m")).then_inc(ld_qk, 16)
            act.dma_start(k_raw[:, :, :], aK.rearrange("n h m -> h n m")).then_inc(ld_qk, 16)
            one = lambda v: v.rearrange("(a n) -> a n", a=1)
            for r0, n, v in ((0, 1, one(bq)), (1, 1, one(bk)), (2, 1, one(norm_w)), (3, E, gate_w),
                             (11, 2 * E, b1.rearrange("e (t p) -> (e t) p", p=P))):
                act.dma_start(rows[r0:r0 + n, :], v).then_inc(ld_rows, 16)
            act.dma_start(b2_n[:, :], b2).then_inc(ld_bc, 16)
            act.dma_start(bv_bc[:, :], one(bv).broadcast_to((P, D))).then_inc(ld_bc, 16)
            act.dma_start(bo_bc[:, :], one(bo).broadcast_to((P, D))).then_inc(ld_bc, 16)
            act.dma_start(iota[:, :], c_iota.broadcast_to((P, E))).then_inc(ld_bc, 16)

            def take(n, dst, src):
                act.wait_ge(setup_ready, n + 1)
                nc.scalar.activation(dst, src, ACT.Copy).then_inc(setup_act, 1)

            take(1, x_T[:, 512:1024], banks[1])
            take(3, qk_T[:, 4:8, :], banks[3].rearrange("p (a c) -> p a c", a=4))
            take(5, qk_T[:, 12:16, :], banks[5].rearrange("p (a c) -> p a c", a=4))
            take(7, v_T[:, 512:1024], banks[7])
            take(9, o_T[:, 4:8, :], banks[1].rearrange("p (a c) -> p a c", a=4))
            take(11, cols[:, :], banks[3][:, 0:27])
            nc.scalar.activation(cols_s[:, :], banks[3][:, 32:34], ACT.Copy).then_inc(setup_act, 1)

            act.sem_inc(proj_act, N_BY["act"])
            act.sem_inc(prob_T_copied, 2)
            act.sem_inc(z_copied, 2)
            with act.Fori(0, B) as b:
                def proj(name, dst, src):
                    act.wait_ge(proj_ready, b * NI + AT[name] + 1)
                    nc.scalar.activation(dst, src, ACT.Copy).then_inc(proj_act, 1)

                def v_copy(n):
                    proj(f"v{n}", v_n[:, n // 2, (n % 2) * 512:(n % 2) * 512 + 512], psG[AT[f"v{n}"] % 2][:, :])

                def exps(h):
                    s = h % 4
                    act.wait_ge(masked, b * H + h + 1 + 2)
                    nc.scalar.activation(prob[:, s, 0:P], prob[:, s, 0:P], ACT.Exp, scale=-1.0,
                                         bias=nmax[:, s, 0:1], accum_out=rsum[:, s, 0:1])
                    nc.scalar.activation(prob[:, s, P:3 * P], prob[:, s, P:3 * P], ACT.Exp, scale=-1.0,
                                         bias=nmax[:, s, 1:2], accum_out=rsum[:, s, 1:2]).then_inc(exp_ready, 1)

                def take_prob_T(h):
                    act.wait_ge(prob_T_ready, b * H + h + 1 + 4)
                    act.wait_ge(pv_ready, b * H + h + 1)
                    nc.scalar.activation(prob_T[:, h % 4, :], psT[h % 2][:, 0:3 * P],
                                         ACT.Copy).then_inc(prob_T_copied, 1)

                def take_z(j):
                    act.wait_ge(pv_ready, b * H + 2 * j + 2 + 4)
                    nc.scalar.activation(z_T[:, j, :], psZ[j % 2][:, 0:S], ACT.Copy).then_inc(z_copied, 1)

                for n in range(4):
                    v_copy(n)
                for t in range(H + 5):
                    if t < H:
                        exps(t)
                    if 0 <= t - 3 < H:
                        take_prob_T(t - 3)
                    if t >= 5 and (t - 5) % 2 == 1:
                        take_z((t - 5) // 2)
                proj("ctx", ctx_T[:, :], psG[AT["ctx"] % 2][:, :])
                proj("w1", w1_T[:, bass.ds(4 * b, 4), :], psG[AT["w1"] % 2][:, :].rearrange("p (a c) -> p a c", a=4))
                proj("w2", w2_T[:, bass.ds(4 * b, 4), :], psG[AT["w2"] % 2][:, :].rearrange("p (a c) -> p a c", a=4))

        @block.tensor
        def _(pe):
            def transposes(n, src, count=4):
                if n >= 8:
                    pe.wait_ge(setup_dve if n % 2 == 0 else setup_act, (n - 8) // 2 + 1)
                for c in range(count):
                    last = nc.tensor.transpose(banks[n % 8][:, c * P:(c + 1) * P], src(c), ident[:, :])
                last.then_inc(setup_ready, 1)

            pe.wait_ge(ld_id, 16)
            pe.wait_ge(ld_x, 32)
            for n in range(2):
                transposes(n, lambda c: x_n[:, 4 * n + c, :])
            pe.wait_ge(ld_qk, 32)
            for n in range(2, 6):
                for c in range(4):
                    h = 4 * (n - 2) + c
                    last = nc.tensor.matmul(banks[n][:, c * P:(c + 1) * P], q_raw[:, h, :], k_raw[:, h, :],
                                            start=True, stop=True)
                last.then_inc(setup_ready, 1)
            pe.wait_ge(ld_v, 16)
            for n in range(6, 8):
                transposes(n, lambda c: v_raw[:, 4 * (n - 6) + c, :])
            pe.wait_ge(ld_o, 16)
            for n in range(8, 10):
                transposes(n, lambda c: o_raw[:, (4 * (n - 8) + c) * P:(4 * (n - 8) + c + 1) * P])
            pe.wait_ge(ld_xw, 64)
            transposes(10, lambda c: xw_raw[:, c, :])
            pe.wait_ge(ld_rows, 80)
            pe.wait_ge(rows_s_ready, 2)
            pe.wait_ge(setup_act, 2)
            nc.tensor.transpose(banks[3][:, 0:27], rows[:, :], ident[0:27, 0:27])
            nc.tensor.transpose(banks[3][:, 32:34], rows_s[:, :], ident[0:2, 0:2]).then_inc(setup_ready, 1)
            pe.wait_ge(identb_ready, 1)
            pe.wait_ge(maskb_ready, 1)
            pe.wait_ge(setup_dve, 3)
            mbank = banks[4].bitcast(BF16).rearrange("p (k q) -> p k q", k=KT)
            for k in range(KT):
                for q in range(QT):
                    last = nc.tensor.transpose(mbank[:, k, q * P:(q + 1) * P], maskb[:, q, k * P:(k + 1) * P],
                                               identb[:, :])
            last.then_inc(setup_ready, 1)
            pe.wait_ge(setup_act, 7)
            pe.wait_ge(setup_dve, 7)

            pe.sem_inc(pv_ready, 4)
            pe.sem_inc(prob_T_ready, 4)
            with pe.Fori(0, B) as b:
                xcol = lambda n: x_T[:, bass.ds(b * S, n)]

                def y_proj(j):
                    wait_bank(pe, b, f"y{j}")
                    for i in range(2):
                        last = nc.tensor.matmul(psG[AT[f"y{j}"] % 2][:, i * S:(i + 1) * S], qk_T[:, 2 * j + i, :],
                                                xcol(S), start=True, stop=True)
                    last.then_inc(proj_ready, 1)

                def v_proj(n):
                    wait_bank(pe, b, f"v{n}")
                    if n == 0:
                        pe.wait_ge(xb_ready, b + 1)
                    nc.tensor.matmul(psG[AT[f"v{n}"] % 2][:, :], xb_T[:, (n // 2) * P:(n // 2 + 1) * P],
                                     v_T[:, (n % 2) * 512:(n % 2) * 512 + 512], start=True,
                                     stop=True).then_inc(proj_ready, 1)

                def scores(h):
                    pe.wait_ge(proj_dve, emptied(b, f"y{h // 2}")[1])
                    pe.wait_ge(masked, b * H + h + 1)
                    nc.tensor.matmul(psS[h % 2][:, 0:P], y_T[:, h, 0:P], xcol(P), start=True, stop=True)
                    nc.tensor.matmul(psS[h % 2][:, P:3 * P], y_T[:, h, P:2 * P], xcol(S), start=True,
                                     stop=True).then_inc(score_ready, 1)

                def turn(h):
                    pe.wait_ge(prob_ready, b * H + h + 1)
                    pe.wait_ge(prob_T_copied, b * H + h + 1)
                    for c in range(3):
                        last = nc.tensor.transpose(psT[h % 2][:, c * P:(c + 1) * P],
                                                   prob[:, h % 4, c * P:(c + 1) * P], ident[:, :])
                    last.then_inc(prob_T_ready, 1)

                def pv(h):
                    pe.wait_ge(prob_T_copied, b * H + h + 1 + 2)
                    if h == 0:
                        pe.wait_ge(proj_act, emptied(b, "v3")[1])
                    if h % 2 == 0:
                        pe.wait_ge(z_copied, b * (H // 2) + h // 2 + 1)
                    r = DH * (h % 2)
                    z = psZ[(h // 2) % 2]
                    v = lambda t: v_n[:, t, h * DH:(h + 1) * DH]
                    nc.tensor.matmul(z[r:r + DH, 0:P], v(0), prob_T[:, h % 4, 0:P], start=True, stop=True)
                    nc.tensor.matmul(z[r:r + DH, P:S], v(0), prob_T[:, h % 4, P:S], start=True, stop=False)
                    nc.tensor.matmul(z[r:r + DH, P:S], v(1), prob_T[:, h % 4, S:3 * P], start=False,
                                     stop=True).then_inc(pv_ready, 1)

                y_proj(0)
                v_proj(0)
                y_proj(1)
                v_proj(1)
                v_proj(2)
                v_proj(3)
                for t in range(H + 4):
                    if t % 2 == 0 and t // 2 + 2 < 8:
                        y_proj(t // 2 + 2)
                    if t < H:
                        scores(t)
                    if 0 <= t - 3 < H:
                        turn(t - 3)
                    if t >= 4:
                        pv(t - 4)

                wait_bank(pe, b, "ctx")
                pe.wait_ge(ld_ctx, 16 * (b + 1))
                for c in range(KT):
                    last = nc.tensor.transpose(psG[AT["ctx"] % 2][:, c * P:(c + 1) * P], ctx_n[:, c, :], ident[:, :])
                last.then_inc(proj_ready, 1)
                pe.wait_ge(proj_act, emptied(b, "ctx")[1])
                for n, w in (("k0", xw_T[:, 1, :]), ("k1", xws_T[:, 1, :])):
                    wait_bank(pe, b, n)
                    nc.tensor.matmul(psG[AT[n] % 2][:, :], w, ctx_T[:, :], start=True,
                                     stop=True).then_inc(proj_ready, 1)
                wait_bank(pe, b, "cv")
                for c in range(KT):
                    last = nc.tensor.matmul(psG[AT["cv"] % 2][:, c * P:(c + 1) * P], ctx_T[:, c * P:(c + 1) * P],
                                            xw_T[:, 2, :], start=True, stop=True)
                last.then_inc(proj_ready, 1)
                pe.wait_ge(ld_e, 64 * (b + 1))
                for n, o in (("w1", 0), ("w2", 4)):
                    wait_bank(pe, b, n)
                    for c in range(4):
                        last = nc.tensor.transpose(psG[AT[n] % 2][:, c * P:(c + 1) * P], e_raw[:, o + c, :],
                                                   ident[:, :])
                    last.then_inc(proj_ready, 1)
                pe.wait_ge(z_copied, (b + 1) * (H // 2) + 2)
                for q in range(QT):
                    wait_bank(pe, b, f"o{q}")
                    for j in range(8):
                        last = nc.tensor.matmul(psG[AT[f"o{q}"] % 2][:, 0:D], z_T[:, j, q * P:(q + 1) * P],
                                                o_T[:, j, :], start=(j == 0), stop=(j == 7))
                    last.then_inc(proj_ready, 1)

        @block.vector
        def _(dve):
            dve.wait_ge(ld_id, 16)
            nc.vector.tensor_copy(identb[:, :], ident[:, :]).then_inc(identb_ready, 1)

            def take(n, dst, src, swapped=None):
                dve.wait_ge(setup_ready, n + 1)
                nc.vector.tensor_copy(dst, src).then_inc(setup_dve, 1)

            take(0, x_T[:, 0:512], banks[0])
            take(2, qk_T[:, 0:4, :], banks[2].rearrange("p (a c) -> p a c", a=4))
            take(4, qk_T[:, 8:12, :], banks[4].rearrange("p (a c) -> p a c", a=4))
            take(6, v_T[:, 0:512], banks[6])
            take(8, o_T[:, 0:4, :], banks[0].rearrange("p (a c) -> p a c", a=4))
            dve.wait_ge(ld_rows, 80)
            pair = lambda v: v.rearrange("p (i two) -> p i two", two=2)
            for i in range(2):
                nc.vector.tensor_copy(pair(rows_s[:, :])[:, :, i], pair(rows[0:2, :])[:, :, 1 - i]).then_inc(rows_s_ready, 1)
            dve.wait_ge(ld_mask, 16)
            nc.vector.tensor_scalar(maskb[:, :, :], mask_raw[:, :, :], NEG_MASK, None, ALU.mult).then_inc(maskb_ready, 1)
            dve.wait_ge(setup_ready, 11)
            nc.vector.tensor_copy(xw_T[:, :, :], banks[2].rearrange("p (a c) -> p a c", a=4))
            four = lambda v: v.rearrange("p a (i two) -> p a i two", two=2)
            for i in range(2):
                last = nc.vector.tensor_copy(four(xws_T[:, :, :])[:, :, :, i],
                                             four(banks[2].rearrange("p (a c) -> p a c", a=4)[:, 0:2, :])[:, :, :, 1 - i])
            last.then_inc(setup_dve, 1)
            dve.wait_ge(setup_ready, 13)
            nc.vector.tensor_copy(mask_T[:, :, :], banks[4].bitcast(BF16).rearrange("p (k q) -> p k q", k=KT)
                                  ).then_inc(setup_dve, 1)
            dve.wait_ge(ld_ca, 16)
            dve.wait_ge(ld_tab, 16)
            dve.wait_ge(ld_bc, 64)
            dve.wait_ge(setup_act, 7)
            dve.wait_ge(consts_ready, 2)

            dve.sem_inc(proj_dve, N_BY["dve"])
            dve.sem_inc(masked, 2)
            with dve.Fori(0, B) as b:
                ch = Steps(dve, dve_chain, b, 6)

                def proj(name):
                    dve.wait_ge(proj_ready, b * NI + AT[name] + 1)
                    return psG[AT[name] % 2]

                def take_y(j):
                    nc.vector.tensor_copy(y_T[:, 2 * j:2 * j + 2, :],
                                          proj(f"y{j}")[:, :].rearrange("p (a c) -> p a c", a=2)).then_inc(proj_dve, 1)

                def mask_scores(h):
                    s = h % 4
                    dve.wait_ge(prob_T_ready, b * H + h + 1)
                    wait_alone(dve, passed, score_ready, b * H + h + 1)
                    nc.vector.tensor_tensor_reduce(prob[:, s, 0:P], psS[h % 2][:, 0:P], causal[:, P:2 * P], -1.0,
                                                   3.0e38, ALU.add, ALU.min, nmax[:, s, 0:1])
                    nc.vector.tensor_tensor_reduce(prob[:, s, P:3 * P], psS[h % 2][:, P:3 * P], causal[:, :], -1.0,
                                                   3.0e38, ALU.add, ALU.min, nmax[:, s, 1:2]).then_inc(masked, 1)

                def invert(h):
                    dve.wait_ge(exp_ready, b * H + h + 1)
                    nc.vector.reciprocal(rinv[:, h % 4, :], rsum[:, h % 4, :]).then_inc(rinv_ready, 1)

                nc.vector.tensor_copy(xb_T[:, :], x_T[:, bass.ds(b * S, S)]).then_inc(xb_ready, 1)
                take_y(0)
                take_y(1)
                for t in range(H + 1):
                    if t % 2 == 0 and t // 2 + 2 < 8:
                        take_y(t // 2 + 2)
                    if t < H:
                        mask_scores(t)
                    if t >= 1:
                        invert(t - 1)

                k = proj("k0")
                nc.vector.scalar_tensor_tensor(rot[:, 0, :], k[:, :], cols[:, 1:2], rope[:, 0, :], ALU.add,
                                               ALU.mult).then_inc(proj_dve, 1)
                k = proj("k1")
                nc.vector.scalar_tensor_tensor(rot[:, 1, :], k[:, :], cols_s[:, 1:2], rope[:, 1, :], ALU.add,
                                               ALU.mult).then_inc(proj_dve, 1)
                dve.wait_ge(proj_dve, emptied(b, "k1")[1])
                ch.link(nc.vector.tensor_tensor(rot[:, 0, :], rot[:, 0, :], rot[:, 1, :], ALU.add))
                dve.wait_ge(kparts_stored, b * (16 * PARTS) + 1)
                ch.link(nc.vector.tensor_copy(k_parts[:, 0, :], rot[:, 0, :]))
                ch.link(nc.vector.tensor_tensor(rot[:, 1, :], rot[:, 0, :], k_parts[:, 0, :], ALU.subtract))
                ch.link(nc.vector.tensor_copy(k_parts[:, 1, :], rot[:, 1, :]))
                nc.vector.tensor_tensor(k_parts[:, 2, :], rot[:, 1, :], k_parts[:, 1, :],
                                        ALU.subtract).then_inc(kparts_ready, 1)
                cv = proj("cv")
                nc.vector.tensor_tensor(v_aug[:, b, :, :, 0:XD].rearrange("p t h d -> p t h d"),
                                        cv[:, :].rearrange("p (t h d) -> p t h d", t=KT, h=XH),
                                        bv_bc[:, :].rearrange("p (a h d) -> p a h d", a=1, h=XH).broadcast_to((P, KT, XH, XD)),
                                        ALU.add).then_inc(proj_dve, 1)
                for q in range(QT):
                    o = proj(f"o{q}")
                    nc.vector.tensor_tensor(res[:, q, :], o[:, 0:D], x_n[:, 2 * b + q, :], ALU.add).then_inc(proj_dve, 1)
                    dve.wait_ge(proj_dve, emptied(b, f"o{q}")[1])
                    ch.link(nc.vector.bn_stats(stats[:, q, :], res[:, q, :]), passed=passed)
                    last = nc.vector.bn_aggr(mv[:, q, :], stats[:, q, :])
                last.then_inc(var_ready, 1)
                dve.wait_ge(rstd_ready, b + 1)
                for q in range(QT):
                    nc.vector.tensor_scalar(x1_n[:, 2 * b + q, :], res[:, q, :], mv[:, q, 0:1], rstd[:, q:q + 1],
                                            ALU.subtract, ALU.mult)
                ch.done()


def cross_block(nc, top, sem, g):
    passed = g["passed"]
    (x1_n, x2_n, ident, identb, xw_T, xws_T, cols, cols_s, bo_bc, rope, maskb, mask_T, v_aug, neghalf, ps, ps2,
     psx, k_parts_d, q_parts_d, c_fill) = (
        g[k] for k in ("x1_n", "x2_n", "ident", "identb", "xw_T", "xws_T", "cols", "cols_s", "bo_bc", "rope",
                       "maskb", "mask_T", "v_aug", "neghalf", "ps", "ps2", "psx", "k_parts_d", "q_parts_d",
                       "c_fill"))
    HALF = TOK // 2
    UNITS = 4 * KT
    SC = XH * QT

    with ExitStack() as st:
        def sb(name, shape, dt=F32):
            return st.enter_context(nc.sbuf_tensor(name, shape, dt))

        q_op = sb("q_op", [P, XH, TOK], BF16)
        k_op = sb("k_op", [P, B, XH, SK], BF16)
        x1_T = sb("x1_T", [P, 2, HALF])
        q_rot = sb("q_rot", [P, 2, HALF])
        q_parts = sb("q_parts", [P, 2, PARTS, HALF], BF16)
        junk = sb("junk", [P, 2, SK], BF16)
        nmax = sb("nmaxx", [P, QT, XH])
        nrest = sb("nrest", [P, QT, XH])
        m_parts = sb("m_parts", [P, QT, PARTS, XH], BF16)
        m_T = sb("m_T", [PARTS * XH, S], BF16)
        v_cur = sb("v_cur", [P, KT, XH, XD + 1])
        prob = sb("probx", [P, 4, 4 * S])
        z_aug = sb("z_aug", [P, 2, S])
        rsum = sb("rsumx", [P, QT, 4])
        z_n = sb("z_n", [P, QT, XH, XD])
        z_T = sb("z_Tx", [P, S])
        x1b = sb("x1b", [P, TILES, D])
        res = sb("resx", [P, QT, D])
        stats = sb("statsx", [P, QT, 6])
        mv = sb("mvx", [P, QT, 2])
        rstd = sb("rstdx", [P, QT])

        k_loaded = [sem(f"k_loaded{b}") for b in range(B)]
        fill_loaded = sem("fill_loaded"); q_stored = sem("q_stored")
        q_loaded = [sem(f"q_loaded{h}") for h in range(2)]
        x1t_ready = sem("x1t_ready"); x1t_copied = sem("x1t_copied"); q_proj = sem("q_proj")
        qparts_ready = sem("qparts_ready"); psum_zeroed = sem("psum_zeroed")
        row_scores = sem("row_scores"); row_max = sem("row_max"); mparts_ready = sem("mparts_ready")
        shift_turned = sem("shift_turned"); shift_copied = sem("shift_copied"); shift_loaded = sem("shift_loaded")
        v_ready = sem("v_ready"); col_scores = sem("col_scores"); probs = sem("probs"); pv_done = sem("pv_done")
        z_copied = sem("zx_copied"); z_turned = sem("z_turned"); z_normed = sem("z_normed")
        zn_turned = sem("zn_turned"); zn_copied = sem("zn_copied"); out_ready = sem("out_ready")
        out_taken = sem("out_taken"); x1b_ready = sem("x1b_ready"); var_ready = sem("varx_ready")
        rstd_ready = sem("rstdx_ready"); dve_chain = sem("dvex_chain"); dve_chain2 = sem("dvex_chain2")
        pool_chain = sem("poolx_chain"); pool_ln = sem("pool_ln")

        block = st.enter_context(nc.Block())

        def k_load(eng, b):
            for a in range(PARTS + 1):
                for c in range(PARTS):
                    r = XD * (PARTS * a + c)
                    eng.dma_start(k_op[r:r + XD, b, :, :],
                                  k_parts_d[b, c].rearrange("h d k -> d h k")).then_inc(k_loaded[b], 16)

        K_LOADS = PARTS * (PARTS + 1) * 16
        Q_LOADS = PARTS * PARTS * 16

        @block.sync
        def _(sp):
            ones_zeros = c_fill
            sp.dma_start(k_op[SROWS:TROWS, :, :, :].rearrange("p b h k -> p (b h k)"),
                         ones_zeros[1:2, :].broadcast_to((PARTS, B * XH * SK))).then_inc(fill_loaded, 16)
            sp.dma_start(q_op[72:SROWS, :, :].rearrange("p h k -> p (h k)"),
                         ones_zeros[0:1, 0:XH * TOK].broadcast_to((24, XH * TOK))).then_inc(fill_loaded, 16)
            k_load(sp, 0)
            for hf in range(2):
                sp.wait_ge(qparts_ready, hf + 1)
                for c in range(PARTS):
                    sp.dma_start(q_parts_d[hf, c].rearrange("h d k -> (h d) k"),
                                 q_parts[:, hf, c, :]).then_inc(q_stored, 16)
                sp.wait_ge(q_stored, 16 * PARTS * (hf + 1))
                for a in range(PARTS):
                    for c in range(PARTS):
                        r = XD * (PARTS * a + c)
                        sp.dma_start(q_op[r:r + XD, :, hf * HALF:(hf + 1) * HALF],
                                     q_parts_d[hf, a].rearrange("h d k -> d h k")).then_inc(q_loaded[hf], 16)
            k_load(sp, 2)
            sp.sem_inc(shift_loaded, 1)
            with sp.Fori(0, B) as b:
                sp.wait_ge(shift_copied, b + 1)
                for c in range(PARTS):
                    sp.dma_start(q_op[SROWS + c:SROWS + c + 1, :, bass.ds(b * S, S)],
                                 m_T[XH * c:XH * (c + 1), :]).then_inc(shift_loaded, 16)
            sp.wait_ge(shift_loaded, 16 * PARTS * B + 1)

        @block.gpsimd
        def _(pool):
            for t in range(TILES):
                last = nc.gpsimd.tensor_tensor(x1b[:, t, :], x1_n[:, t, :], bo_bc[:, :], ALU.add)
            last.then_inc(x1b_ready, 1)

            def shift_parts(b):
                ch = Steps(pool, pool_chain, b, 4)
                pool.wait_ge(shift_turned, b + 1)
                wait_alone(pool, passed, row_max, (b + 1) * SC + 2)
                ch.link(nc.gpsimd.tensor_scalar(nrest[:, :, :], nmax[:, :, :], SHIFT_MAX, None, ALU.min), passed=passed)
                ch.link(nc.gpsimd.tensor_copy(m_parts[:, :, 0, :], nrest[:, :, :]))
                ch.link(nc.gpsimd.tensor_tensor(nrest[:, :, :], nrest[:, :, :], m_parts[:, :, 0, :], ALU.subtract),
                        passed=passed)
                ch.link(nc.gpsimd.tensor_copy(m_parts[:, :, 1, :], nrest[:, :, :]))
                nc.gpsimd.tensor_tensor(m_parts[:, :, 2, :], nrest[:, :, :], m_parts[:, :, 1, :],
                                        ALU.subtract).then_inc(mparts_ready, 1)
                ch.done()

            def layer_norm(b):
                ch = Steps(pool, pool_ln, b, 1)
                wait_alone(pool, passed, var_ready, b + 1)
                ch.link(nc.gpsimd.tensor_scalar(rstd[:, :], mv[:, :, 1], LN_EPS, None, ALU.add))
                nc.gpsimd.tensor_tensor(rstd[:, :], rstd[:, :], neghalf[:, 0:QT], ALU.pow).then_inc(rstd_ready, 1)
                ch.done()

            pool.sem_inc(mparts_ready, 1)
            shift_parts(0)
            with pool.Fori(0, B - 1) as b:
                shift_parts(b + 1)
                layer_norm(b)
            layer_norm(B - 1)

        @block.scalar
        def _(act):
            k_load(act, 1)
            for hf in range(2):
                act.wait_ge(x1t_ready, hf + 1)
                nc.scalar.activation(x1_T[:, hf, :], ps2[hf][:, 0:HALF], ACT.Copy).then_inc(x1t_copied, 1)
            k_load(act, 3)
            act.sem_inc(probs, 2)
            act.sem_inc(z_copied, 1)

            def copy_shift(b):
                act.wait_ge(shift_turned, b + 1 + 1)
                act.wait_ge(shift_loaded, b * (16 * PARTS) + 1)
                nc.scalar.activation(m_T[:, :], psx[1].ap()[0:PARTS * XH, 0:S // 2].bitcast(BF16),
                                     ACT.Copy).then_inc(shift_copied, 1)

            def body(b, more):
                act.wait_ge(pv_done, b * UNITS + 4)
                nc.scalar.activation(v_cur[:, :, :, :].rearrange("p t h d -> p (t h d)"),
                                     v_aug[:, b, :, :, :].rearrange("p t h d -> p (t h d)"),
                                     ACT.Copy).then_inc(v_ready, 1)

                def copy_z(gr):
                    act.wait_ge(pv_done, b * UNITS + 4 * gr + 4 + 4)
                    act.wait_ge(z_turned, b * 4 + gr + 1)
                    nc.scalar.activation(z_aug[:, gr % 2, :], psx[0][:, 0:S], ACT.Copy).then_inc(z_copied, 1)

                for u in range(UNITS + 2):
                    if u < UNITS:
                        act.wait_ge(col_scores, b * UNITS + u + 1)
                        act.wait_ge(pv_done, b * UNITS + u + 1)
                        nc.scalar.activation(prob[:, u % 4, :], ps2[u % 2][:, :], ACT.Exp).then_inc(probs, 1)
                    if u >= 5 and u % 4 == 1:
                        copy_z((u - 5) // 4)
                act.wait_ge(zn_turned, b + 1)
                nc.scalar.activation(z_T[:, :], psx[1][:, 0:S], ACT.Copy).then_inc(zn_copied, 1)
                if more:
                    copy_shift(b + 1)

            copy_shift(0)
            with act.Fori(0, B - 1) as b:
                body(b, True)
            body(B - 1, False)

        @block.tensor
        def _(pe):
            for hf in range(2):
                for c in range(4):
                    last = nc.tensor.transpose(ps2[hf][:, c * P:(c + 1) * P], x1_n[:, 4 * hf + c, :], ident[:, :])
                last.then_inc(x1t_ready, 1)
            for hf in range(2):
                pe.wait_ge(x1t_copied, hf + 1)
                nc.tensor.matmul(ps2[hf][:, HALF:2 * HALF], xw_T[:, 0, :], x1_T[:, hf, :], start=True,
                                 stop=True).then_inc(q_proj, 1)
                nc.tensor.matmul(psx[hf][:, :], xws_T[:, 0, :], x1_T[:, hf, :], start=True,
                                 stop=True).then_inc(q_proj, 1)

            def row_unit(b, i):
                h, q = i // QT, i % QT
                pe.wait_ge(row_max, b * SC + i + 1)
                nc.tensor.matmul(ps[i % 2][:, :], q_op[0:SROWS, h, bass.ds(b * S + q * P, P)],
                                 k_op[0:SROWS, b, h, :], start=True, stop=True).then_inc(row_scores, 1)

            def turn_shift(b):
                pe.wait_ge(out_taken, b + 1)
                wait_alone(pe, passed, mparts_ready, b + 1 + 1)
                for q in range(QT):
                    last = nc.tensor.transpose(psx[1].ap()[0:PARTS * XH, q * P // 2:(q + 1) * P // 2].bitcast(BF16),
                                               m_parts[:, q, :, :].rearrange("p c h -> p (c h)"), identb[:, :])
                last.then_inc(shift_turned, 1)

            def body(b, more):
                pe.wait_ge(shift_loaded, (b + 1) * (16 * PARTS) + 1)
                pe.wait_ge(v_ready, b + 1)
                pe.wait_ge(psum_zeroed, 1)

                def col_unit(u):
                    gr, kt = u // KT, u % KT
                    pe.wait_ge(probs, b * UNITS + u + 1)
                    for hh in range(4):
                        nc.tensor.matmul(ps2[u % 2][:, hh * S:(hh + 1) * S], identb[:, :], mask_T[:, kt, :],
                                         start=True, stop=False)
                        last = nc.tensor.matmul(ps2[u % 2][:, hh * S:(hh + 1) * S],
                                                k_op[0:TROWS, b, 4 * gr + hh, kt * P:(kt + 1) * P],
                                                q_op[0:TROWS, 4 * gr + hh, bass.ds(b * S, S)],
                                                start=False, stop=True)
                    last.then_inc(col_scores, 1)

                def pv_unit(u):
                    gr, kt = u // KT, u % KT
                    pe.wait_ge(probs, b * UNITS + u + 1 + 2)
                    if kt == 0:
                        pe.wait_ge(z_copied, b * 4 + gr + 1)
                    for hh in range(4):
                        last = nc.tensor.matmul(psx[0][32 * hh:32 * hh + XD + 1, 0:S], v_cur[:, kt, 4 * gr + hh, :],
                                                prob[:, u % 4, hh * S:(hh + 1) * S], start=(kt == 0),
                                                stop=(kt == KT - 1))
                    last.then_inc(pv_done, 1)

                def turn_z(gr):
                    pe.wait_ge(z_copied, b * 4 + gr + 1 + 1)
                    if gr:
                        pe.wait_ge(z_normed, b * 4 + gr)
                    for q in range(QT):
                        last = nc.tensor.transpose(psx[1][:, q * P:(q + 1) * P], z_aug[:, gr % 2, q * P:(q + 1) * P],
                                                   ident[:, :])
                    last.then_inc(z_turned, 1)

                for u in range(UNITS + 3):
                    if u < UNITS:
                        col_unit(u)
                        if more:
                            row_unit(b + 1, 2 * u)
                            row_unit(b + 1, 2 * u + 1)
                    if 2 <= u < UNITS + 2:
                        pv_unit(u - 2)
                    if u >= 6 and u % 4 == 2:
                        turn_z((u - 6) // 4)
                pe.wait_ge(z_normed, b * 4 + 4)
                for q in range(QT):
                    last = nc.tensor.transpose(psx[1][:, q * P:(q + 1) * P],
                                               z_n[:, q, :, :].rearrange("p h d -> p (h d)"), ident[:, :])
                last.then_inc(zn_turned, 1)
                pe.wait_ge(zn_copied, b + 1)
                for q in range(QT):
                    last = nc.tensor.matmul(psx[1][:, q * P:(q + 1) * P], z_T[:, q * P:(q + 1) * P], xw_T[:, 3, :],
                                            start=True, stop=True)
                last.then_inc(out_ready, 1)
                if more:
                    turn_shift(b + 1)

            pe.sem_inc(z_turned, 2)
            pe.sem_inc(shift_turned, 1)
            pe.wait_ge(fill_loaded, 32)
            for hf in range(2):
                pe.wait_ge(q_loaded[hf], Q_LOADS)
            for b in range(B):
                pe.wait_ge(k_loaded[b], K_LOADS)
            for i in range(SC):
                row_unit(0, i)
            pe.sem_inc(pv_done, 4)
            turn_shift(0)
            with pe.Fori(0, B - 1) as b:
                body(b, True)
            body(B - 1, False)

        @block.vector
        def _(dve):
            Q_LINKS = 6
            for hf in range(2):
                ch = Steps(dve, dve_chain, 0, Q_LINKS, base=hf * Q_LINKS)
                table = lambda n: rope[:, n:n + 1, 0:S].broadcast_to((P, 2, S))
                two = lambda v: v.rearrange("p (a c) -> p a c", a=2)
                dve.wait_ge(q_proj, 2 * hf + 1)
                ch.link(nc.vector.scalar_tensor_tensor(two(q_rot[:, 0, :]), two(ps2[hf][:, HALF:2 * HALF]), cols[:, 0:1],
                                                       table(0), ALU.add, ALU.mult))
                dve.wait_ge(q_proj, 2 * hf + 2)
                ch.link(nc.vector.scalar_tensor_tensor(two(q_rot[:, 1, :]), two(psx[hf][:, :]), cols_s[:, 0:1],
                                                       table(1), ALU.add, ALU.mult))
                ch.link(nc.vector.tensor_tensor(q_rot[:, 0, :], q_rot[:, 0, :], q_rot[:, 1, :], ALU.add))
                ch.link(nc.vector.tensor_copy(q_parts[:, hf, 0, :], q_rot[:, 0, :]))
                ch.link(nc.vector.tensor_tensor(q_rot[:, 1, :], q_rot[:, 0, :], q_parts[:, hf, 0, :], ALU.subtract))
                ch.link(nc.vector.tensor_copy(q_parts[:, hf, 1, :], q_rot[:, 1, :]))
                nc.vector.tensor_tensor(q_parts[:, hf, 2, :], q_rot[:, 1, :], q_parts[:, hf, 1, :],
                                        ALU.subtract).then_inc(qparts_ready, 1)
                ch.done()
            nc.vector.memset(psx[0][:, 0:S], 0.0).then_inc(psum_zeroed, 1)

            dve.sem_inc(row_max, 2)
            dve.sem_inc(out_taken, 1)

            def row_unit(b, i):
                h, q = i // QT, i % QT
                if i == 0:
                    dve.wait_ge(mparts_ready, b + 1)
                dve.wait_ge(row_max, b * SC + i + 1)
                wait_alone(dve, passed, row_scores, b * SC + i + 1)
                nc.vector.tensor_tensor_reduce(junk[:, i % 2, :], ps[i % 2][:, :], maskb[:, q, :], -1.0, 3.0e38,
                                               ALU.add, ALU.min, nmax[:, q, h:h + 1]).then_inc(row_max, 1)

            def body(b, more):
                ch = Steps(dve, dve_chain2, b, 4 * 2 + 4)

                def norm_z(gr):
                    dve.wait_ge(z_turned, b * 4 + gr + 1 + 2)
                    z = psx[1][:, 0:S].rearrange("p (q h r) -> p q h r", q=QT, h=4)
                    ch.link(nc.vector.tensor_scalar(rsum[:, :, :], z[:, :, :, XD], TINY, None, ALU.max))
                    ch.link(nc.vector.reciprocal(rsum[:, :, :], rsum[:, :, :]))
                    nc.vector.tensor_tensor(z_n[:, :, 4 * gr:4 * gr + 4, :], z[:, :, :, 0:XD],
                                            rsum[:, :, :].rearrange("p q (h a) -> p q h a", a=1).broadcast_to((P, QT, 4, XD)),
                                            ALU.mult).then_inc(z_normed, 1)

                for u in range(UNITS + 3):
                    if u < UNITS and more:
                        row_unit(b + 1, 2 * u)
                        row_unit(b + 1, 2 * u + 1)
                    if u >= 6 and u % 4 == 2:
                        norm_z((u - 6) // 4)
                dve.wait_ge(out_ready, b + 1)
                dve.wait_ge(x1b_ready, 1)
                two = lambda v: v.rearrange("p (q d) -> p q d", q=QT)
                ins = nc.vector.tensor_tensor(res[:, :, :], two(psx[1][:, 0:S]), x1b[:, bass.ds(2 * b, 2), :], ALU.add)
                ins.then_inc(out_taken, 1)
                dve.wait_ge(out_taken, b + 1 + 1)
                for q in range(QT):
                    ch.link(nc.vector.bn_stats(stats[:, q, :], res[:, q, :]), passed=passed)
                    last = nc.vector.bn_aggr(mv[:, q, :], stats[:, q, :])
                last.then_inc(var_ready, 1)
                dve.wait_ge(rstd_ready, b + 1)
                for q in range(QT):
                    ch.link(nc.vector.tensor_scalar(x2_n[:, 2 * b + q, :], res[:, q, :], mv[:, q, 0:1],
                                                    rstd[:, q:q + 1], ALU.subtract, ALU.mult))
                ch.done()

            for i in range(SC):
                row_unit(0, i)
            with dve.Fori(0, B - 1) as b:
                body(b, True)
            body(B - 1, False)


def moe_block(nc, top, sem, g):
    passed = g["passed"]
    (x2_n, ident, cols, b2_n, w1_T, w2_T, neghalf, iota, ps, ps2, psx, out) = (
        g[k] for k in ("x2_n", "ident", "cols", "b2_n", "w1_T", "w2_T", "neghalf", "iota", "ps", "ps2", "psx", "out"))
    NORM_COL, GATE_COL, B1_COL = 2, 3, 11
    HALF = TOK // 2

    with ExitStack() as st:
        def sb(name, shape, dt=F32):
            return st.enter_context(nc.sbuf_tensor(name, shape, dt))

        sq = sb("sq", [P, 2, D])
        ms = sb("ms", [P, TILES])
        rms = sb("rms", [P, TILES])
        t_n = sb("t_n", [P, TILES, D])
        t_T = sb("t_T", [P, TOK])
        logits = sb("logits", [P, TILES, E])
        top8 = sb("top8", [P, TILES, 8])
        idx8 = sb("idx8", [P, TILES, 8], U32)
        idx = sb("idx", [P, TILES, 2])
        gap = sb("gap", [P, TILES])
        egap = sb("egap", [P, TILES])
        wts = sb("wts", [P, 3, TILES])
        comb = sb("comb", [P, TILES, E])
        comb2 = sb("comb2", [P, TILES, E])
        comb_T = sb("comb_T", [E, TOK])
        w1_cur = sb("w1_cur", [P, 2, 2, P])
        hid = sb("hid", [P, 2, 2, TOK])
        acc = sb("acc", [P, TILES, D])
        stats = sb("statsm", [P, TILES, 6])
        mv = sb("mvm", [P, TILES, 2])
        rstd = sb("rstdm", [P, TILES])
        fin = sb("fin", [P, TILES, D])

        ms_ready = sem("ms_ready"); rms_ready = sem("rms_ready"); t_ready = sem("t_ready")
        t_turned = sem("t_turned"); t_copied = sem("t_copied"); gates = sem("gates"); gap_ready = sem("gap_ready")
        egap_ready = sem("egap_ready"); comb_ready = sem("comb_ready"); comb_turned = sem("comb_turned")
        comb_copied = sem("comb_copied"); bias_ready = sem("bias_ready"); w1c_ready = sem("w1c_ready")
        hid_ready = sem("hid_ready"); gelu_done = sem("gelu_done"); o_ready = sem("o_ready")
        o_added = sem("o_added"); varm_ready = sem("varm_ready"); rstdm_ready = sem("rstdm_ready")
        fin_ready = sem("fin_ready"); stored = sem("stored"); chain = sem("dvem_chain")
        pool_chain = sem("poolm_chain")

        psH = [ps[0], ps[1], psx[0], psx[1]]
        psO = [ps2[0][:, 0:512], ps2[1][:, 0:512]]

        block = st.enter_context(nc.Block())

        @block.sync
        def _(sp):
            ov = out.rearrange("b (t p) m -> p (b t) m", p=P)
            for hf in range(2):
                sp.wait_ge(fin_ready, hf + 1)
                sp.dma_start(ov[:, 4 * hf:4 * hf + 4, :], fin[:, 4 * hf:4 * hf + 4, :]).then_inc(stored, 16)
            sp.wait_ge(stored, 32)

        @block.gpsimd
        def _(pool):
            def copy_w1(e, slot):
                pool.wait_ge(hid_ready, e * 4 + 4)
                nc.gpsimd.tensor_copy(w1_cur[:, slot, :, :], w1_T[:, bass.ds(2 * e, 2), :]).then_inc(w1c_ready, 1)

            pool.wait_ge(ms_ready, 1)
            nc.gpsimd.tensor_scalar(rms[:, :], ms[:, :], RMS_EPS, None, ALU.add).then_inc(pool_chain, 1)
            pool.wait_ge(pool_chain, 1)
            nc.gpsimd.tensor_tensor(rms[:, :], rms[:, :], neghalf[:, :], ALU.pow).then_inc(rms_ready, 1)
            with pool.Fori(0, E // 2) as i:
                copy_w1(2 * i, 0)
                copy_w1(2 * i + 1, 1)
            for hf in range(2):
                half = slice(4 * hf, 4 * hf + 4)
                pool.wait_ge(varm_ready, hf + 1)
                nc.gpsimd.tensor_scalar(rstd[:, half], mv[:, half, 1], LN_EPS, None, ALU.add).then_inc(pool_chain, 1)
                pool.wait_ge(pool_chain, hf + 2)
                nc.gpsimd.tensor_tensor(rstd[:, half], rstd[:, half], neghalf[:, half], ALU.pow).then_inc(rstdm_ready, 1)

        @block.scalar
        def _(act):
            act.wait_ge(gap_ready, 1)
            nc.scalar.activation(egap[:, :], gap[:, :], ACT.Exp).then_inc(egap_ready, 1)
            for hf in range(2):
                act.wait_ge(comb_turned, hf + 1)
                nc.scalar.activation(comb_T[:, hf * HALF:(hf + 1) * HALF], ps2[hf][0:E, 512:1024],
                                     ACT.Copy).then_inc(comb_copied, 1)
            act.sem_inc(gelu_done, 4)

            def gelu(e, slot):
                for u in range(4):
                    t, hf = u // 2, u % 2
                    act.wait_ge(o_ready, e * 2 + 2)
                    wait_alone(act, passed, hid_ready, e * 4 + 8 + u + 1)
                    nc.scalar.activation(hid[:, slot, t, hf * HALF:(hf + 1) * HALF], psH[u][:, :], ACT.Gelu,
                                         bias=cols[:, bass.ds(B1_COL + 2 * e + t, 1)]).then_inc(gelu_done, 1)

            with act.Fori(0, E // 2) as i:
                gelu(2 * i, 0)
                gelu(2 * i + 1, 1)

        @block.tensor
        def _(pe):
            for hf in range(2):
                pe.wait_ge(t_ready, hf + 1)
                for c in range(4):
                    last = nc.tensor.transpose(psH[hf][:, c * P:(c + 1) * P], t_n[:, 4 * hf + c, :], ident[:, :])
                last.then_inc(t_turned, 1)
            pe.wait_ge(t_copied, 2)
            for t in range(TILES):
                last = nc.tensor.matmul(psx[0][:, t * E:(t + 1) * E], t_T[:, t * P:(t + 1) * P],
                                        cols[:, GATE_COL:GATE_COL + E], start=True, stop=True)
            last.then_inc(gates, 1)
            pe.wait_ge(comb_ready, 1)
            for hf in range(2):
                for c in range(4):
                    last = nc.tensor.transpose(ps2[hf][0:E, 512 + c * P:512 + (c + 1) * P], comb[:, 4 * hf + c, :],
                                               ident[:, :])
                last.then_inc(comb_turned, 1)
            for hf in range(2):
                pe.wait_ge(comb_copied, hf + 1)
                for c in range(4):
                    last = nc.tensor.matmul(psO[hf][:, c * D:(c + 1) * D], comb_T[:, (4 * hf + c) * P:(4 * hf + c + 1) * P],
                                            b2_n[:, :], start=True, stop=True)
                last.then_inc(bias_ready, 1)
            pe.sem_inc(o_ready, 4)
            pe.sem_inc(hid_ready, 8)

            def hidden(e, slot):
                pe.wait_ge(w1c_ready, e + 1)
                for u in range(4):
                    t, hf = u // 2, u % 2
                    pe.wait_ge(gelu_done, e * 4 + u + 1)
                    nc.tensor.matmul(psH[u][:, :], w1_cur[:, slot, t, :], t_T[:, hf * HALF:(hf + 1) * HALF],
                                     start=True, stop=True).then_inc(hid_ready, 1)

            def outputs(e, slot):
                pe.wait_ge(gelu_done, e * 4 + 4 + 4)
                for hf in range(2):
                    pe.wait_ge(o_added, e * 2 + hf + 1)
                    for c in range(4):
                        for t in range(2):
                            last = nc.tensor.matmul(psO[hf][:, c * D:(c + 1) * D],
                                                    hid[:, slot, t, (4 * hf + c) * P:(4 * hf + c + 1) * P],
                                                    w2_T[:, bass.ds(2 * e + t, 1), :].rearrange("p a d -> p (a d)"),
                                                    start=(t == 0), stop=(t == 1))
                    last.then_inc(o_ready, 1)

            hidden(0, 0)
            with pe.Fori(0, E // 2 - 1) as i:
                hidden(2 * i + 1, 1)
                outputs(2 * i, 0)
                hidden(2 * i + 2, 0)
                outputs(2 * i + 1, 1)
            hidden(E - 1, 1)
            outputs(E - 2, 0)
            outputs(E - 1, 1)

        @block.vector
        def _(dve):
            LINKS = 10
            ch = Steps(dve, chain, 0, LINKS)
            for t in range(TILES):
                last = nc.vector.tensor_tensor_reduce(t_n[:, t, :], x2_n[:, t, :], x2_n[:, t, :], 1.0 / D, 0.0, ALU.mult,
                                                      ALU.add, ms[:, t:t + 1])
            last.then_inc(ms_ready, 1)
            dve.wait_ge(rms_ready, 1)
            for hf in range(2):
                for c in range(4):
                    t = 4 * hf + c
                    last = nc.vector.tensor_scalar(t_n[:, t, :], x2_n[:, t, :], rms[:, t:t + 1], None, ALU.mult)
                last.then_inc(t_ready, 1)
            for hf in range(2):
                dve.wait_ge(t_turned, hf + 1)
                nc.vector.tensor_scalar(t_T[:, hf * HALF:(hf + 1) * HALF], psH[hf][:, :], cols[:, NORM_COL:NORM_COL + 1],
                                        None, ALU.mult).then_inc(t_copied, 1)
            dve.wait_ge(gates, 1)
            ch.link(nc.vector.tensor_copy(logits[:, :, :], psx[0][:, 0:TILES * E].rearrange("p (t e) -> p t e", t=TILES)))
            for t in range(TILES):
                last = nc.vector.max(top8[:, t, :], logits[:, t, :])
            ch.link(last)
            for t in range(TILES):
                last = nc.vector.max_index(idx8[:, t, :], top8[:, t, :], logits[:, t, :])
            ch.link(last)
            nc.vector.tensor_tensor(gap[:, :], top8[:, :, 1], top8[:, :, 0], ALU.subtract).then_inc(gap_ready, 1)
            ch.link(nc.vector.tensor_copy(idx[:, :, :], idx8[:, :, 0:2]))
            dve.wait_ge(egap_ready, 1)
            ch.link(nc.vector.tensor_scalar(wts[:, 0, :], egap[:, :], 1.0, None, ALU.add))
            ch.link(nc.vector.reciprocal(wts[:, 1, :], wts[:, 0, :]))
            ch.link(nc.vector.tensor_tensor(wts[:, 2, :], egap[:, :], wts[:, 1, :], ALU.mult))
            bc = lambda v: v.rearrange("p (t a) -> p t a", a=1).broadcast_to((P, TILES, E))
            experts = iota[:, :].rearrange("p (a e) -> p a e", a=1).broadcast_to((P, TILES, E))
            nc.vector.tensor_tensor(comb[:, :, :], experts, bc(idx[:, :, 0]), ALU.is_equal)
            ch.link(nc.vector.tensor_tensor(comb2[:, :, :], experts, bc(idx[:, :, 1]), ALU.is_equal))
            nc.vector.tensor_tensor(comb[:, :, :], comb[:, :, :], bc(wts[:, 1, :]), ALU.mult)
            ch.link(nc.vector.tensor_tensor(comb2[:, :, :], comb2[:, :, :], bc(wts[:, 2, :]), ALU.mult))
            nc.vector.tensor_tensor(comb[:, :, :], comb[:, :, :], comb2[:, :, :], ALU.add).then_inc(comb_ready, 1)
            quad = lambda v: v.rearrange("p (t d) -> p t d", t=4)
            for hf in range(2):
                dve.wait_ge(bias_ready, hf + 1)
                last = nc.vector.scalar_tensor_tensor(acc[:, 4 * hf:4 * hf + 4, :], x2_n[:, 4 * hf:4 * hf + 4, :], 2.0,
                                                      quad(psO[hf]), ALU.mult, ALU.add)
                if hf == 0:
                    last.then_inc(chain, 1)
                    ch.n += 1
                    dve.wait_ge(chain, ch.n)
                else:
                    last.then_inc(o_added, 1)
            dve.wait_ge(o_added, 1)
            dve.sem_inc(o_added, 1)
            ch.done()

            def add(e):
                for hf in range(2):
                    dve.wait_ge(o_ready, e * 2 + 4 + hf + 1)
                    dve.wait_ge(o_added, e * 2 + hf + 1)
                    for c in range(4):
                        t = 4 * hf + c
                        last = nc.vector.scalar_tensor_tensor(acc[:, t, :], psO[hf][:, c * D:(c + 1) * D],
                                                              comb[:, t, bass.ds(e, 1)], acc[:, t, :], ALU.mult, ALU.add)
                    last.then_inc(o_added, 1)

            with dve.Fori(0, E) as e:
                add(e)
            dve.wait_ge(o_added, 2 * E + 2)
            for hf in range(2):
                for t in range(4 * hf, 4 * hf + 4):
                    last = nc.vector.bn_stats(stats[:, t, :], acc[:, t, :])
                last.then_inc(chain, 1)
                dve.wait_ge(chain, LINKS + hf + 1)
                for t in range(4 * hf, 4 * hf + 4):
                    last = nc.vector.bn_aggr(mv[:, t, :], stats[:, t, :])
                last.then_inc(varm_ready, 1)
            for hf in range(2):
                dve.wait_ge(rstdm_ready, hf + 1)
                for t in range(4 * hf, 4 * hf + 4):
                    last = nc.vector.tensor_scalar(fin[:, t, :], acc[:, t, :], mv[:, t, 0:1], rstd[:, t:t + 1],
                                                   ALU.subtract, ALU.mult)
                last.then_inc(fin_ready, 1)


_INS = ["x", "ctx_1024", "mask_1x1xSxS2_bk1", "L0_attn_Q", "L0_attn_K", "L0_attn_V", "L0_attn_O", "L0_xattn_Wq",
        "L0_xattn_bq", "L0_xattn_Wk", "L0_xattn_bk", "L0_xattn_Wv", "L0_xattn_bv", "L0_xattn_Wo", "L0_xattn_bo",
        "L0_ffn_norm_weight", "L0_ffn_gate_w", "L0_ffn_w1", "L0_ffn_b1", "L0_ffn_w2", "L0_ffn_b2"]


def _constants():
    import numpy as np

    causal = np.zeros((P, S), np.float32)
    causal[:, P:] = np.where(np.arange(P)[None, :] <= np.arange(P)[:, None], 0.0, NEG_CAUSAL)
    inv = np.exp(np.arange(0, XD, 2, dtype=np.float32) * (-(4.0 * np.log(np.float32(10.0))) / XD)).astype(np.float32)
    angle = np.arange(SK, dtype=np.float32)[None, :] * inv[:, None]
    sin, cos = np.sin(angle), np.cos(angle)
    dim = np.arange(P) % XD
    own = np.where((dim % 2 == 0)[:, None], sin[dim // 2], -sin[dim // 2])
    rope = np.stack([own, -cos[dim // 2]], axis=1).astype(np.float32)
    fill = np.zeros((2, B * XH * SK), np.uint16)
    fill[1] = 0x3F80
    return {"ident": np.eye(P, dtype=np.float32), "causal": causal, "rope": rope, "fill": fill,
            "iota": np.arange(E, dtype=np.float32)[None, :]}


def kernel(**inputs):
    import numpy as np
    import concourse.bacc as bacc
    from concourse.bass_utils import run_bass_kernel_spmd

    nc = bacc.Bacc("TRN2", target_bir_lowering=False, num_devices=1)
    arrays, args = {}, []

    def give(name, a):
        a = np.ascontiguousarray(a)
        arrays[name] = a
        args.append(nc.dram_tensor(name, a.shape, mybir.dt.from_np(a.dtype), kind="ExternalInput").ap())

    for name in _INS:
        give(f"in_{name}", inputs[name])
    for name, a in _constants().items():
        give(f"const_{name}", a)
        if name == "fill":
            args[-1] = args[-1].bitcast(BF16)
    args.append(nc.dram_tensor("out_0", (B, S, D), F32, kind="ExternalOutput").ap())
    build(nc, *args)
    r = run_bass_kernel_spmd(nc, [arrays], core_ids=[0])
    return r.results[0]["out_0"]
```

```python
from contextlib import ExitStack

import concourse.bass as bass
from concourse import mybir

F32 = mybir.dt.float32
BF16 = mybir.dt.bfloat16
U8 = mybir.dt.uint8
U32 = mybir.dt.uint32
ALU = mybir.AluOpType
ACT = mybir.ActivationFunctionType

B, S, D = 4, 256, 128
SK = 512
H, DH = 16, 64
XH, XD = 16, 8
E, F = 8, 256
P = 128
QT = S // P
KT = SK // P
TILES = B * QT
TOK = B * S
NEG_CAUSAL = -1.0e10
NEG_MASK = -1.0e30
SHIFT_MAX = 1.0e15
TINY = 1.0e-30
LN_EPS = 1e-5
RMS_EPS = 1e-6
PARTS = 3
PROWS = XD * PARTS * PARTS
SROWS = 96
TROWS = SROWS + PARTS


def wait_alone(eng, passed, sem, value):
    eng.wait_ge(sem, value)
    eng.sem_inc(passed, 1)


class Steps:

    def __init__(self, eng, sem, i=0, per=0, base=0):
        self.eng, self.sem, self.i, self.per, self.base, self.n = eng, sem, i, per, base, 0

    def link(self, ins, passed=None):
        ins.then_inc(self.sem, 1)
        self.n += 1
        value = self.i * self.per + self.base + self.n
        if passed is None:
            self.eng.wait_ge(self.sem, value)
        else:
            wait_alone(self.eng, passed, self.sem, value)

    def done(self):
        assert self.n == self.per, (self.n, self.per)


def build(nc, x, ctx_in, mask, aQ, aK, aV, aO, Wq, bq, Wk, bk, Wv, bv, Wo, bo, norm_w, gate_w,
          w1, b1, w2, b2, c_ident, c_causal, c_rope, c_fill, c_iota, out):
    with ExitStack() as top:
        def sb(name, shape, dt=F32, scope=top):
            return scope.enter_context(nc.sbuf_tensor(name, shape, dt))

        def sem(name):
            return top.enter_context(nc.semaphore(name))

        x_n = sb("x_n", [P, TILES, D])
        x2_n = x_n
        ident = sb("ident", [P, P])
        cols = sb("cols", [P, 27])
        b2_n = sb("b2_n", [E, D])
        neghalf = sb("neghalf", [P, TILES])
        iota = sb("iota", [P, E])
        big = sb("big", [P, 2 * H * D])
        ps = [top.enter_context(nc.psum_tensor(f"ps{i}", [P, 512], F32)) for i in range(2)]
        ps2 = [top.enter_context(nc.psum_tensor(f"pd{i}", [P, 1024], F32)) for i in range(2)]
        psx = [top.enter_context(nc.psum_tensor(f"px{i}", [P, 512], F32)) for i in range(2)]

        k_parts_d = nc.dram_tensor("k_parts_d", (B, PARTS, XH, XD, SK), BF16, kind="Internal").ap()
        q_parts_d = nc.dram_tensor("q_parts_d", (B, PARTS, XH, XD, S), BF16, kind="Internal").ap()

        passed = sem("passed")
        ops_loaded = sem("ops_loaded")
        w_loaded = [sem(f"w_loaded{n}") for n in range(E // 2)]

        with ExitStack() as att:
            identb = sb("identb", [P, P], BF16, att)
            xw_T = sb("xw_T", [P, 4, D], scope=att)
            xws_T = sb("xws_T", [P, 2, D], scope=att)
            cols_s = sb("cols_s", [P, 2], scope=att)
            bv_bc = sb("bv_bc", [P, D], scope=att)
            bo_bc = sb("bo_bc", [P, D], scope=att)
            rope = sb("rope", [P, 2, SK], scope=att)
            maskb = sb("maskb", [P, QT, SK], BF16, att)
            mask_T = sb("mask_T", [P, KT, S], BF16, att)
            v_aug = sb("v_aug", [P, B, KT, XH, XD + 1], scope=att)
            x1b = sb("x1b", [P, TILES, D], scope=att)
            x1c = sb("x1c", [P, QT, D], scope=att)
            x1_T = sb("x1_T", [P, S], scope=att)
            z_T = sb("z_T", [P, 8, S], scope=att)
            o_T = sb("o_T", [P, 8, D], scope=att)
            rot = sb("rot", [P, 2, SK], scope=att)
            q_parts = sb("q_parts", [P, PARTS, S], BF16, att)
            res = sb("res", [P, QT, D], scope=att)
            stats = sb("stats", [P, QT, 6], scope=att)
            mv = sb("mv", [P, QT, 2], scope=att)
            rstd = sb("rstd", [P, QT], scope=att)
            q_op = sb("q_op", [P, XH, TOK], BF16, att)
            k_op = sb("k_op", [P, B, XH, SK], BF16, att)
            self_block(nc, locals())
            cross_block(nc, locals())
        moe_block(nc, locals())


def out_proj(nc, bank, z_T, o_T):
    for q in range(QT):
        for j in range(8):
            last = nc.tensor.matmul(bank[:, q * D:(q + 1) * D], z_T[:, j, q * P:(q + 1) * P], o_T[:, j, :],
                                    start=(j == 0), stop=(j == 7))
    return last


def moments(nc, ch, res, stats, mv, ready, passed):
    for q in range(QT):
        ch.link(nc.vector.bn_stats(stats[:, q, :], res[:, q, :]), passed=passed)
        last = nc.vector.bn_aggr(mv[:, q, :], stats[:, q, :])
    last.then_inc(ready, 1)


def normalise(nc, res, mv, rstd, dst, ready):
    for q in range(QT):
        last = nc.vector.tensor_scalar(dst[:, q, :], res[:, q, :], mv[:, q, 0:1], rstd[:, q:q + 1],
                                       ALU.subtract, ALU.mult)
    last.then_inc(ready, 1)


def both(row):
    return row.rearrange("p (a d) -> p a d", a=1).broadcast_to((P, QT, D))


def split_queries(nc, ch, rot, q_parts, ready):
    ch.link(nc.vector.tensor_copy(q_parts[:, 0, :], rot[:, 0, 0:S]))
    ch.link(nc.vector.tensor_tensor(rot[:, 1, 0:S], rot[:, 0, 0:S], q_parts[:, 0, :], ALU.subtract))
    ch.link(nc.vector.tensor_copy(q_parts[:, 1, :], rot[:, 1, 0:S]))
    nc.vector.tensor_tensor(q_parts[:, 2, :], rot[:, 1, 0:S], q_parts[:, 1, :], ALU.subtract).then_inc(ready, 1)


def q_round(eng, g, b, value, stored, loaded):
    q_parts, q_parts_d, q_op = g["q_parts"], g["q_parts_d"], g["q_op"]
    for c in range(PARTS):
        eng.dma_start(q_parts_d[b, c].rearrange("h d k -> (h d) k"), q_parts[:, c, :]).then_inc(stored, 16)
    eng.wait_ge(stored, value)
    for a in range(PARTS):
        for c in range(PARTS):
            r = XD * (PARTS * a + c)
            eng.dma_start(q_op[r:r + XD, :, bass.ds(b * S, S)],
                          q_parts_d[b, a].rearrange("h d k -> d h k")).then_inc(loaded, 16)


def self_block(nc, g):
    passed = g["passed"]
    (x, ctx_in, mask, aQ, aK, aV, aO, Wq, bq, Wk, bk, Wv, bv, Wo, bo, norm_w, gate_w, b1, b2, c_ident, c_causal,
     c_rope, c_iota, c_fill) = (
        g[k] for k in ("x", "ctx_in", "mask", "aQ", "aK", "aV", "aO", "Wq", "bq", "Wk", "bk", "Wv", "bv", "Wo",
                       "bo", "norm_w", "gate_w", "b1", "b2", "c_ident", "c_causal", "c_rope", "c_iota", "c_fill"))
    (x_n, x1b, x1c, x1_T, ident, identb, xw_T, xws_T, cols, cols_s, bv_bc, bo_bc, b2_n, rope, maskb, mask_T, v_aug,
     neghalf, iota, ps, ps2, psx, k_parts_d, q_parts_d, k_op, q_op, z_T, o_T, rot, q_parts, big, ops_loaded, res,
     stats, mv, rstd) = (
        g[k] for k in ("x_n", "x1b", "x1c", "x1_T", "ident", "identb", "xw_T", "xws_T", "cols", "cols_s", "bv_bc",
                       "bo_bc", "b2_n", "rope", "maskb", "mask_T", "v_aug", "neghalf", "iota", "ps", "ps2", "psx",
                       "k_parts_d", "q_parts_d", "k_op", "q_op", "z_T", "o_T", "rot", "q_parts", "big",
                       "ops_loaded", "res", "stats", "mv", "rstd"))

    with ExitStack() as st:
        def sb(name, shape, dt=F32):
            return st.enter_context(nc.sbuf_tensor(name, shape, dt))

        def sem(name):
            return g["top"].enter_context(nc.semaphore(name))

        qk_T = big[:, 0:H * D].rearrange("p (h d) -> p h d", h=H)
        v_n = big[:, H * D:2 * H * D].rearrange("p (t f) -> p t f", t=QT)
        y_T = sb("y_T", [P, 8, S])
        causal = sb("causal", [P, S])
        v_T = sb("v_T", [P, H * DH])
        x_T = sb("x_T", [P, TOK])
        xb_T = sb("xb_T", [P, S])
        prob = sb("prob", [P, 4, 3 * P])
        prob_T = sb("prob_T", [P, 4, 3 * P])
        nmax = sb("nmax", [P, 4, 2])
        rsum = sb("rsum", [P, 4, 2])
        rinv = sb("rinv", [P, 4, 2])
        ctx_n = sb("ctx_n", [P, KT, D])
        ctx_T = sb("ctx_T", [P, SK])
        k_parts = sb("k_parts", [P, PARTS, SK], BF16)
        rows = sb("rows", [27, D])
        rows_s = sb("rows_s", [2, D])
        mask_raw = sb("mask_raw", [P, QT, SK], U8)
        q_raw = y_T[0:DH, :, :].rearrange("p a b -> p (a b)").rearrange("p (h d) -> p h d", h=H)
        k_raw = z_T[0:DH, :, :].rearrange("p a b -> p (a b)").rearrange("p (h d) -> p h d", h=H)
        v_raw = v_n[:, 0, :].rearrange("p (j d) -> p j d", j=8)
        o_raw = v_n[:, 1, :]
        xw_raw = prob_T[:, :, 0:D]

        ld_x = sem("ld_x"); ld_qk = sem("ld_qk"); ld_v = sem("ld_v"); ld_o = sem("ld_o")
        ld_id = sem("ld_id"); ld_ca = sem("ld_ca"); ld_xw = sem("ld_xw"); ld_rows = sem("ld_rows")
        ld_mask = sem("ld_mask"); ld_tab = sem("ld_tab"); ld_bc = sem("ld_bc"); ld_ctx = sem("ld_ctx")
        identb_ready = sem("identb_ready"); maskb_ready = sem("maskb_ready"); rows_s_ready = sem("rows_s_ready")
        consts_ready = sem("consts_ready"); setup_ready = sem("setup_ready")
        setup_dve = sem("setup_dve"); setup_act = sem("setup_act")
        xb_ready = sem("xb_ready"); proj_ready = sem("proj_ready"); proj_dve = sem("proj_dve")
        proj_act = sem("proj_act"); score_ready = sem("score_ready"); masked = sem("masked")
        exp_ready = sem("exp_ready"); rinv_ready = sem("rinv_ready"); prob_ready = sem("prob_ready")
        prob_T_ready = sem("prob_T_ready"); prob_T_copied = sem("prob_T_copied"); pv_ready = sem("pv_ready")
        z_copied = sem("z_copied"); var_ready = sem("var_ready"); rstd_ready = sem("rstd_ready")
        x1_ready = sem("x1_ready")
        kparts_ready = sem("kparts_ready"); kparts_stored = sem("kparts_stored")
        qparts_ready = sem("qparts_ready"); qparts_stored = sem("qparts_stored")
        dve_chain = sem("dve_chain"); dve_ln = sem("dve_ln"); dve_q = sem("dve_q"); pool_chain = sem("pool_chain")

        STEP_ITEMS = {0: ["y2"], 1: ["ctx"], 2: ["y3"], 3: ["k0", "k1"], 4: ["y4", "v1"], 5: ["o"], 6: ["y5", "v3"],
                      7: ["cv"], 8: ["y6"], 9: ["xt"], 10: ["y7"], 11: ["q0", "q1"], 12: ["next-v0"],
                      13: ["next-v2"], 14: ["next-y0"], 15: ["next-y1"]}
        ITEMS = [n for t in range(H) for n in STEP_ITEMS[t]]
        BEFORE = ["next-y0", "next-v0", "next-v2", "next-y1"]
        OF_LAST = ["o", "xt", "q0", "q1"]
        FIRST = [n for n in ITEMS if n not in OF_LAST]
        FIRST_ALL = BEFORE + FIRST
        NI = len(ITEMS)
        assert NI == len(FIRST_ALL) and NI % 2 == 0
        by = lambda n: "act" if n.replace("next-", "")[0] == "v" or n in ("ctx", "xt") else "dve"
        COUNT = {e: sum(by(n) == e for n in ITEMS) for e in ("act", "dve")}
        COUNT_FIRST = {e: sum(by(n) == e for n in FIRST_ALL) for e in ("act", "dve")}

        class Place:

            def __init__(self, b, first, last):
                self.b, self.first, self.last = b, first, last

            def has(self, name):
                return not (self.first and name in OF_LAST) and not (self.last and name.startswith("next-"))

            def at(self, name):
                return FIRST_ALL.index(name, len(BEFORE)) if self.first else ITEMS.index(name)

            def bank(self, name):
                return ps[self.at(name) % 2]

            def made(self, name):
                return self.b * NI + self.at(name) + 1

            def base(self, eng):
                return 0 if self.first else self.b * COUNT[eng] + (COUNT_FIRST[eng] - COUNT[eng])

            def emptied_at(self, n):
                names = FIRST_ALL if self.first else ITEMS
                eng = by(names[n])
                return eng, self.base(eng) + sum(by(m) == eng for m in names[:n + 1])

            def emptied(self, name):
                return self.emptied_at(self.at(name))[1]

        def wait_bank(pe, pl, name):
            n = pl.at(name) - 2
            if n >= 0:
                eng, v = pl.emptied_at(n)
            else:
                eng, v = "dve", pl.base("dve") + n + 1
            pe.wait_ge(proj_act if eng == "act" else proj_dve, v)

        psS = [ps2[0][:, 0:512], ps2[0][:, 512:1024]]
        psT = [ps2[1][:, 0:512], ps2[1][:, 512:1024]]
        psZ = psx
        banks = [ps[0][:, :], ps[1][:, :]] + psS + psT + [psx[0][:, :], psx[1][:, :]]

        block = st.enter_context(nc.Block())

        @block.sync
        def _(sp):
            sp.dma_start(ident[:, :], c_ident).then_inc(ld_id, 16)
            xv = x.rearrange("b (t p) m -> p (b t) m", p=P)
            sp.dma_start(x_n[:, 0:4, :], xv[:, 0:4, :]).then_inc(ld_x, 16)
            sp.dma_start(x_n[:, 4:8, :], xv[:, 4:8, :]).then_inc(ld_x, 16)
            sp.dma_start(v_raw, aV.rearrange("(j two) h m -> (two h) j m", two=2)).then_inc(ld_v, 16)
            sp.dma_start(o_raw, aO).then_inc(ld_o, 16)
            for n, w in enumerate((Wq, Wk, Wv, Wo)):
                sp.dma_start(xw_raw[:, n, :], w).then_inc(ld_xw, 16)
            sp.dma_start(mask_raw[:, :, :], mask.rearrange("a b (t p) k -> p (a b t) k", p=P)).then_inc(ld_mask, 16)
            sp.dma_start(causal[:, :], c_causal).then_inc(ld_ca, 16)
            sp.dma_start(rope[:, :, :], c_rope).then_inc(ld_tab, 16)
            sp.dma_start(k_op[SROWS:TROWS, :, :, :].rearrange("p b h k -> p (b h k)"),
                         c_fill[1:2, :].broadcast_to((PARTS, B * XH * SK))).then_inc(ops_loaded, 16)
            sp.dma_start(q_op[PROWS:SROWS, :, :].rearrange("p h k -> p (h k)"),
                         c_fill[0:1, 0:XH * TOK].broadcast_to((SROWS - PROWS, XH * TOK))).then_inc(ops_loaded, 16)

            def load_ctx(b):
                sp.dma_start(ctx_n[:, :, :], ctx_in[b].rearrange("(t p) m -> p t m", p=P)).then_inc(ld_ctx, 16)

            def body(pl):
                b = pl.b
                if not pl.last:
                    sp.wait_ge(proj_ready, pl.made("ctx"))
                    load_ctx(b + 1)
                sp.wait_ge(kparts_ready, b + 1)
                for c in range(PARTS):
                    sp.dma_start(k_parts_d[b, c].rearrange("h d k -> (h d) k"),
                                 k_parts[:, c, :]).then_inc(kparts_stored, 16)
                sp.wait_ge(kparts_stored, (b + 1) * (16 * PARTS) + 1)
                for a in range(PARTS + 1):
                    for c in range(PARTS):
                        r = XD * (PARTS * a + c)
                        sp.dma_start(k_op[r:r + XD, b, :, :],
                                     k_parts_d[b, c].rearrange("h d k -> d h k")).then_inc(ops_loaded, 16)
                if not pl.first:
                    sp.wait_ge(qparts_ready, b)
                    q_round(sp, g, b - 1, b * (16 * PARTS) + 1, qparts_stored, ops_loaded)

            sp.sem_inc(kparts_stored, 1)
            sp.sem_inc(qparts_stored, 1)
            load_ctx(0)
            body(Place(0, True, False))
            with sp.Fori(0, B - 2) as i:
                body(Place(i + 1, False, False))
            body(Place(B - 1, False, True))

        @block.gpsimd
        def _(pool):
            pool.memset(neghalf[:, :], -0.5).then_inc(consts_ready, 1)
            pool.memset(v_aug[:, :, :, :, XD:XD + 1], 1.0).then_inc(consts_ready, 1)

            def body(pl):
                b = pl.b
                for h in range(H):
                    s = h % 4
                    pool.wait_ge(rinv_ready, b * H + h + 1)
                    nc.gpsimd.tensor_tensor(prob[:, s, 0:P], prob[:, s, 0:P],
                                            rinv[:, s, 0:1].broadcast_to((P, P)), ALU.mult)
                    nc.gpsimd.tensor_tensor(prob[:, s, P:3 * P], prob[:, s, P:3 * P],
                                            rinv[:, s, 1:2].broadcast_to((P, S)), ALU.mult).then_inc(prob_ready, 1)
                    if h == 6 and not pl.first:
                        ch = Steps(pool, pool_chain, b - 1, 1)
                        wait_alone(pool, passed, var_ready, b)
                        ch.link(nc.gpsimd.tensor_scalar(rstd[:, :], mv[:, :, 1], LN_EPS, None, ALU.add))
                        nc.gpsimd.tensor_tensor(rstd[:, :], rstd[:, :], neghalf[:, 0:QT],
                                                ALU.pow).then_inc(rstd_ready, 1)
                        ch.done()

            body(Place(0, True, False))
            with pool.Fori(0, B - 2) as i:
                body(Place(i + 1, False, False))
            body(Place(B - 1, False, True))

        @block.scalar
        def _(act):
            act.dma_start(q_raw, aQ.rearrange("n h m -> h n m")).then_inc(ld_qk, 16)
            act.dma_start(k_raw, aK.rearrange("n h m -> h n m")).then_inc(ld_qk, 16)
            one = lambda v: v.rearrange("(a n) -> a n", a=1)
            for r0, n, v in ((0, 1, one(bq)), (1, 1, one(bk)), (2, 1, one(norm_w)), (3, E, gate_w),
                             (11, 2 * E, b1.rearrange("e (t p) -> (e t) p", p=P))):
                act.dma_start(rows[r0:r0 + n, :], v).then_inc(ld_rows, 16)
            act.dma_start(b2_n[:, :], b2).then_inc(ld_bc, 16)
            act.dma_start(bv_bc[:, :], one(bv).broadcast_to((P, D))).then_inc(ld_bc, 16)
            act.dma_start(bo_bc[:, :], one(bo).broadcast_to((P, D))).then_inc(ld_bc, 16)
            act.dma_start(iota[:, :], c_iota.broadcast_to((P, E))).then_inc(ld_bc, 16)

            def take(n, dst, src):
                act.wait_ge(setup_ready, n + 1)
                nc.scalar.activation(dst, src, ACT.Copy).then_inc(setup_act, 1)

            take(1, x_T[:, 512:1024], banks[1])
            take(3, qk_T[:, 4:8, :], banks[3].rearrange("p (a c) -> p a c", a=4))
            take(5, qk_T[:, 12:16, :], banks[5].rearrange("p (a c) -> p a c", a=4))
            take(7, v_T[:, 512:1024], banks[7])
            take(9, o_T[:, 4:8, :], banks[1].rearrange("p (a c) -> p a c", a=4))
            take(11, cols[:, :], banks[3][:, 0:27])
            nc.scalar.activation(cols_s[:, :], banks[3][:, 32:34], ACT.Copy).then_inc(setup_act, 1)

            act.sem_inc(prob_T_copied, 2)
            act.sem_inc(z_copied, 2)

            def v_copy(n, ready, bank):
                act.wait_ge(proj_ready, ready)
                nc.scalar.activation(v_n[:, n // 2, (n % 2) * 512:(n % 2) * 512 + 512], bank[:, :],
                                     ACT.Copy).then_inc(proj_act, 1)

            def exps(b, h):
                s = h % 4
                act.wait_ge(masked, b * H + h + 1 + 2)
                nc.scalar.activation(prob[:, s, 0:P], prob[:, s, 0:P], ACT.Exp, scale=-1.0,
                                     bias=nmax[:, s, 0:1], accum_out=rsum[:, s, 0:1])
                nc.scalar.activation(prob[:, s, P:3 * P], prob[:, s, P:3 * P], ACT.Exp, scale=-1.0,
                                     bias=nmax[:, s, 1:2], accum_out=rsum[:, s, 1:2]).then_inc(exp_ready, 1)

            def take_prob_T(b, h):
                act.wait_ge(prob_T_ready, b * H + h + 1 + 4)
                act.wait_ge(pv_ready, b * H + h + 1)
                nc.scalar.activation(prob_T[:, h % 4, :], psT[h % 2][:, 0:3 * P],
                                     ACT.Copy).then_inc(prob_T_copied, 1)

            def take_z(b, j):
                act.wait_ge(pv_ready, b * H + 2 * j + 2 + 4)
                nc.scalar.activation(z_T[:, j % 8, :], psZ[j % 2][:, 0:S], ACT.Copy).then_inc(z_copied, 1)

            def step(pl, t):
                b = pl.b
                if t < H:
                    exps(b, t)
                if t - 3 < H and (t >= 3 or not pl.first):
                    take_prob_T(b, t - 3)
                if t % 2 == 0 and (t >= 6 or not pl.first):
                    take_z(b, (t - 5) // 2)
                for name in STEP_ITEMS.get(t, ()):
                    if not pl.has(name) or by(name) != "act":
                        continue
                    if name == "ctx":
                        act.wait_ge(proj_ready, pl.made(name))
                        nc.scalar.activation(ctx_T[:, :], pl.bank(name)[:, :], ACT.Copy).then_inc(proj_act, 1)
                    elif name == "xt":
                        act.wait_ge(proj_ready, pl.made(name))
                        nc.scalar.activation(x1_T[:, :], pl.bank(name)[:, 0:S], ACT.Copy).then_inc(proj_act, 1)
                    else:
                        v_copy(int(name[-1]), pl.made(name), pl.bank(name))

            v_copy(0, 2, ps[1])
            v_copy(2, 3, ps[0])
            for t in range(H):
                step(Place(0, True, False), t)
            with act.Fori(0, B - 2) as i:
                for t in range(H):
                    step(Place(i + 1, False, False), t)
            for t in range(H + 5):
                step(Place(B - 1, False, True), t)

        @block.tensor
        def _(pe):
            def transposes(n, src, count=4):
                if n >= 8:
                    pe.wait_ge(setup_dve if n % 2 == 0 else setup_act, (n - 8) // 2 + 1)
                for c in range(count):
                    last = nc.tensor.transpose(banks[n % 8][:, c * P:(c + 1) * P], src(c), ident[:, :])
                last.then_inc(setup_ready, 1)

            pe.wait_ge(ld_id, 16)
            pe.wait_ge(ld_x, 32)
            for n in range(2):
                transposes(n, lambda c: x_n[:, 4 * n + c, :])
            pe.wait_ge(ld_qk, 32)
            for n in range(2, 6):
                for c in range(4):
                    h = 4 * (n - 2) + c
                    last = nc.tensor.matmul(banks[n][:, c * P:(c + 1) * P], q_raw[:, h, :], k_raw[:, h, :],
                                            start=True, stop=True)
                last.then_inc(setup_ready, 1)
            pe.wait_ge(ld_v, 16)
            for n in range(6, 8):
                transposes(n, lambda c: v_raw[:, 4 * (n - 6) + c, :])
            pe.wait_ge(ld_o, 16)
            for n in range(8, 10):
                transposes(n, lambda c: o_raw[:, (4 * (n - 8) + c) * P:(4 * (n - 8) + c + 1) * P])
            pe.wait_ge(ld_xw, 64)
            transposes(10, lambda c: xw_raw[:, c, :])
            pe.wait_ge(ld_rows, 80)
            pe.wait_ge(rows_s_ready, 2)
            pe.wait_ge(setup_act, 2)
            nc.tensor.transpose(banks[3][:, 0:27], rows[:, :], ident[0:27, 0:27])
            nc.tensor.transpose(banks[3][:, 32:34], rows_s[:, :], ident[0:2, 0:2]).then_inc(setup_ready, 1)
            pe.wait_ge(identb_ready, 1)
            pe.wait_ge(maskb_ready, 1)
            pe.wait_ge(setup_dve, 3)
            mbank = banks[4].bitcast(BF16).rearrange("p (k q) -> p k q", k=KT)
            for k in range(KT):
                for q in range(QT):
                    last = nc.tensor.transpose(mbank[:, k, q * P:(q + 1) * P], maskb[:, q, k * P:(k + 1) * P],
                                               identb[:, :])
            last.then_inc(setup_ready, 1)
            pe.wait_ge(setup_act, 7)
            pe.wait_ge(setup_dve, 7)
            pe.sem_inc(pv_ready, 4)
            pe.sem_inc(prob_T_ready, 4)

            def y_proj(b, j, bank):
                for i in range(2):
                    last = nc.tensor.matmul(bank[:, i * S:(i + 1) * S], qk_T[:, 2 * j + i, :], x_T[:, bass.ds(b * S, S)],
                                            start=True, stop=True)
                last.then_inc(proj_ready, 1)

            def v_proj(n, bank):
                nc.tensor.matmul(bank[:, :], xb_T[:, (n // 2) * P:(n // 2 + 1) * P],
                                 v_T[:, (n % 2) * 512:(n % 2) * 512 + 512], start=True, stop=True).then_inc(proj_ready, 1)

            def item(pl, name):
                b, bank = pl.b, pl.bank(name)
                wait_bank(pe, pl, name)
                if name[0] == "y":
                    y_proj(b, int(name[1]), bank)
                elif name[0] == "v":
                    v_proj(int(name[1]), bank)
                elif name == "next-v0":
                    pe.wait_ge(xb_ready, b + 2)
                    v_proj(0, bank)
                elif name == "next-v2":
                    v_proj(2, bank)
                elif name.startswith("next-y"):
                    y_proj(b + 1, int(name[-1]), bank)
                elif name == "ctx":
                    pe.wait_ge(ld_ctx, (b + 1) * 16)
                    for c in range(KT):
                        last = nc.tensor.transpose(bank[:, c * P:(c + 1) * P], ctx_n[:, c, :], ident[:, :])
                    last.then_inc(proj_ready, 1)
                elif name in ("k0", "k1"):
                    pe.wait_ge(proj_act, pl.emptied("ctx"))
                    w = xw_T[:, 1, :] if name == "k0" else xws_T[:, 1, :]
                    nc.tensor.matmul(bank[:, :], w, ctx_T[:, :], start=True, stop=True).then_inc(proj_ready, 1)
                elif name == "cv":
                    for c in range(KT):
                        last = nc.tensor.matmul(bank[:, c * P:(c + 1) * P], ctx_T[:, c * P:(c + 1) * P],
                                                xw_T[:, 2, :], start=True, stop=True)
                    last.then_inc(proj_ready, 1)
                elif name == "o":
                    pe.wait_ge(z_copied, b * (H // 2) + 2)
                    out_proj(nc, bank, z_T, o_T).then_inc(proj_ready, 1)
                elif name == "xt":
                    pe.wait_ge(x1_ready, b)
                    for q in range(QT):
                        last = nc.tensor.transpose(bank[:, q * P:(q + 1) * P], x1c[:, q, :], ident[:, :])
                    last.then_inc(proj_ready, 1)
                else:
                    pe.wait_ge(proj_act, pl.emptied("xt"))
                    w = xw_T[:, 0, :] if name == "q0" else xws_T[:, 0, :]
                    nc.tensor.matmul(bank[:, 0:S], w, x1_T[:, :], start=True, stop=True).then_inc(proj_ready, 1)

            def scores(pl, h):
                b = pl.b
                if h >= 4:
                    pe.wait_ge(proj_dve, pl.emptied(f"y{h // 2}"))
                elif pl.first:
                    pe.wait_ge(proj_dve, h // 2 + 1)
                else:
                    pe.wait_ge(proj_dve, pl.base("dve") - 1 + h // 2)
                pe.wait_ge(masked, b * H + h + 1)
                nc.tensor.matmul(psS[h % 2][:, 0:P], y_T[:, h % 8, 0:P], x_T[:, bass.ds(b * S, P)], start=True, stop=True)
                nc.tensor.matmul(psS[h % 2][:, P:3 * P], y_T[:, h % 8, P:2 * P], x_T[:, bass.ds(b * S, S)], start=True,
                                 stop=True).then_inc(score_ready, 1)

            def turn(b, h):
                pe.wait_ge(prob_ready, b * H + h + 1)
                pe.wait_ge(prob_T_copied, b * H + h + 1)
                for c in range(3):
                    last = nc.tensor.transpose(psT[h % 2][:, c * P:(c + 1) * P],
                                               prob[:, h % 4, c * P:(c + 1) * P], ident[:, :])
                last.then_inc(prob_T_ready, 1)

            def pv(pl, h):
                b = pl.b
                pe.wait_ge(prob_T_copied, b * H + h + 1 + 2)
                if h == 0:
                    pe.wait_ge(proj_act, 2 if pl.first else pl.base("act"))
                if h == 8:
                    pe.wait_ge(proj_act, pl.emptied("v3"))
                if h % 2 == 0:
                    pe.wait_ge(z_copied, b * (H // 2) + h // 2 + 1)
                r = DH * (h % 2)
                z = psZ[(h // 2) % 2]
                v = lambda t: v_n[:, t, (h % H) * DH:(h % H + 1) * DH]
                nc.tensor.matmul(z[r:r + DH, 0:P], v(0), prob_T[:, h % 4, 0:P], start=True, stop=True)
                nc.tensor.matmul(z[r:r + DH, P:S], v(0), prob_T[:, h % 4, P:S], start=True, stop=False)
                nc.tensor.matmul(z[r:r + DH, P:S], v(1), prob_T[:, h % 4, S:3 * P], start=False,
                                 stop=True).then_inc(pv_ready, 1)

            def step(pl, t):
                if t < H:
                    scores(pl, t)
                if t - 3 < H and (t >= 3 or not pl.first):
                    turn(pl.b, t - 3)
                for name in STEP_ITEMS.get(t, ()):
                    if pl.has(name):
                        item(pl, name)
                if t >= 4 or not pl.first:
                    pv(pl, t - 4)

            y_proj(0, 0, ps[0])
            pe.wait_ge(xb_ready, 1)
            v_proj(0, ps[1])
            pe.wait_ge(proj_dve, 1)
            v_proj(2, ps[0])
            pe.wait_ge(proj_act, 1)
            y_proj(0, 1, ps[1])
            for t in range(H):
                step(Place(0, True, False), t)
            with pe.Fori(0, B - 2) as i:
                for t in range(H):
                    step(Place(i + 1, False, False), t)
            for t in range(H + 4):
                step(Place(B - 1, False, True), t)

        @block.vector
        def _(dve):
            dve.wait_ge(ld_id, 16)
            nc.vector.tensor_copy(identb[:, :], ident[:, :]).then_inc(identb_ready, 1)

            def take(n, dst, src, swapped=None):
                dve.wait_ge(setup_ready, n + 1)
                nc.vector.tensor_copy(dst, src).then_inc(setup_dve, 1)

            take(0, x_T[:, 0:512], banks[0])
            take(2, qk_T[:, 0:4, :], banks[2].rearrange("p (a c) -> p a c", a=4))
            take(4, qk_T[:, 8:12, :], banks[4].rearrange("p (a c) -> p a c", a=4))
            take(6, v_T[:, 0:512], banks[6])
            take(8, o_T[:, 0:4, :], banks[0].rearrange("p (a c) -> p a c", a=4))
            dve.wait_ge(ld_rows, 80)
            pair = lambda v: v.rearrange("p (i two) -> p i two", two=2)
            for i in range(2):
                nc.vector.tensor_copy(pair(rows_s[:, :])[:, :, i], pair(rows[0:2, :])[:, :, 1 - i]).then_inc(rows_s_ready, 1)
            dve.wait_ge(ld_mask, 16)
            nc.vector.tensor_scalar(maskb[:, :, :], mask_raw[:, :, :], NEG_MASK, None, ALU.mult).then_inc(maskb_ready, 1)
            dve.wait_ge(setup_ready, 11)
            nc.vector.tensor_copy(xw_T[:, :, :], banks[2].rearrange("p (a c) -> p a c", a=4))
            four = lambda v: v.rearrange("p a (i two) -> p a i two", two=2)
            for i in range(2):
                last = nc.vector.tensor_copy(four(xws_T[:, :, :])[:, :, :, i],
                                             four(banks[2].rearrange("p (a c) -> p a c", a=4)[:, 0:2, :])[:, :, :, 1 - i])
            last.then_inc(setup_dve, 1)
            dve.wait_ge(setup_ready, 13)
            nc.vector.tensor_copy(mask_T[:, :, :], banks[4].bitcast(BF16).rearrange("p (k q) -> p k q", k=KT)
                                  ).then_inc(setup_dve, 1)
            dve.wait_ge(ld_ca, 16)
            dve.wait_ge(ld_tab, 16)
            dve.wait_ge(ld_bc, 64)
            dve.wait_ge(setup_act, 7)
            dve.wait_ge(consts_ready, 2)
            dve.sem_inc(masked, 2)

            def copy_xb(b):
                nc.vector.tensor_copy(xb_T[:, :], x_T[:, bass.ds(b * S, S)]).then_inc(xb_ready, 1)

            def take_y(j, ready, bank):
                dve.wait_ge(proj_ready, ready)
                nc.vector.tensor_copy(y_T[:, 2 * (j % 4):2 * (j % 4) + 2, :],
                                      bank[:, :].rearrange("p (a c) -> p a c", a=2)).then_inc(proj_dve, 1)

            def mask_scores(b, h):
                s = h % 4
                dve.wait_ge(prob_T_ready, b * H + h + 1)
                wait_alone(dve, passed, score_ready, b * H + h + 1)
                nc.vector.tensor_tensor_reduce(prob[:, s, 0:P], psS[h % 2][:, 0:P], causal[:, P:2 * P], -1.0,
                                               3.0e38, ALU.add, ALU.min, nmax[:, s, 0:1])
                nc.vector.tensor_tensor_reduce(prob[:, s, P:3 * P], psS[h % 2][:, P:3 * P], causal[:, :], -1.0,
                                               3.0e38, ALU.add, ALU.min, nmax[:, s, 1:2]).then_inc(masked, 1)

            def invert(b, h):
                dve.wait_ge(exp_ready, b * H + h + 1)
                nc.vector.reciprocal(rinv[:, h % 4, :], rsum[:, h % 4, :]).then_inc(rinv_ready, 1)

            def item(pl, name, ch, chl, chq):
                b, bank = pl.b, pl.bank(name)
                if name[0] == "y":
                    take_y(int(name[1]), pl.made(name), bank)
                    return
                if name.startswith("next-"):
                    take_y(int(name[-1]), pl.made(name), bank)
                    return
                dve.wait_ge(proj_ready, pl.made(name))
                if name in ("k0", "k1"):
                    n = int(name[1])
                    bias = (cols, cols_s)[n][:, 1:2]
                    nc.vector.scalar_tensor_tensor(rot[:, n, :], bank[:, :], bias, rope[:, n, :], ALU.add,
                                                   ALU.mult).then_inc(proj_dve, 1)
                    if n == 1:
                        dve.wait_ge(proj_dve, pl.emptied("k1"))
                        ch.link(nc.vector.tensor_tensor(rot[:, 0, :], rot[:, 0, :], rot[:, 1, :], ALU.add))
                        dve.wait_ge(kparts_stored, b * (16 * PARTS) + 1)
                        ch.link(nc.vector.tensor_copy(k_parts[:, 0, :], rot[:, 0, :]))
                        ch.link(nc.vector.tensor_tensor(rot[:, 1, :], rot[:, 0, :], k_parts[:, 0, :], ALU.subtract))
                        ch.link(nc.vector.tensor_copy(k_parts[:, 1, :], rot[:, 1, :]))
                        nc.vector.tensor_tensor(k_parts[:, 2, :], rot[:, 1, :], k_parts[:, 1, :],
                                                ALU.subtract).then_inc(kparts_ready, 1)
                elif name == "cv":
                    nc.vector.tensor_tensor(v_aug[:, b, :, :, 0:XD].rearrange("p t h d -> p t h d"),
                                            bank[:, :].rearrange("p (t h d) -> p t h d", t=KT, h=XH),
                                            bv_bc[:, :].rearrange("p (a h d) -> p a h d", a=1, h=XH).broadcast_to((P, KT, XH, XD)),
                                            ALU.add).then_inc(proj_dve, 1)
                elif name == "o":
                    last = nc.vector.tensor_tensor(res[:, :, :], bank[:, 0:S].rearrange("p (q d) -> p q d", q=QT),
                                                   x_n[:, bass.ds(2 * b - 2, 2), :], ALU.add)
                    last.then_inc(proj_dve, 1)
                    dve.wait_ge(proj_dve, pl.emptied("o"))
                    moments(nc, chl, res, stats, mv, var_ready, passed)
                elif name in ("q0", "q1"):
                    n = int(name[1])
                    bias = (cols, cols_s)[n][:, 0:1]
                    nc.vector.scalar_tensor_tensor(rot[:, n, 0:S], bank[:, 0:S], bias, rope[:, n, 0:S], ALU.add,
                                                   ALU.mult).then_inc(proj_dve, 1)
                    if n == 1:
                        dve.wait_ge(proj_dve, pl.emptied("q1"))
                        chq.link(nc.vector.tensor_tensor(rot[:, 0, 0:S], rot[:, 0, 0:S], rot[:, 1, 0:S], ALU.add))
                        dve.wait_ge(qparts_stored, (b - 1) * (16 * PARTS) + 1)
                        split_queries(nc, chq, rot, q_parts, qparts_ready)

            def body(pl):
                b = pl.b
                ch = Steps(dve, dve_chain, b, 4)
                chl = Steps(dve, dve_ln, b - 1, 2)
                chq = Steps(dve, dve_q, b - 1, 4)
                for t in range(H + pl.last):
                    if t < H:
                        mask_scores(b, t)
                    if t >= 1 or not pl.first:
                        invert(b, t - 1)
                    if t == 8 and not pl.first:
                        dve.wait_ge(rstd_ready, b)
                        normalise(nc, res, mv, rstd, x1c, x1_ready)
                        dve.wait_ge(x1_ready, b)
                        nc.vector.tensor_tensor(x1b[:, bass.ds(2 * b - 2, 2), :], x1c[:, :, :], both(bo_bc[:, :]),
                                                ALU.add)
                    if t == 9 and not pl.last:
                        dve.wait_ge(proj_ready, pl.made("v3"))
                        copy_xb(b + 1)
                    for name in STEP_ITEMS.get(t, ()):
                        if pl.has(name) and by(name) == "dve":
                            item(pl, name, ch, chl, chq)
                ch.done()
                if not pl.first:
                    chl.done()
                    chq.done()

            copy_xb(0)
            take_y(0, 1, ps[0])
            take_y(1, 4, ps[1])
            body(Place(0, True, False))
            with dve.Fori(0, B - 2) as i:
                body(Place(i + 1, False, False))
            body(Place(B - 1, False, True))


def cross_block(nc, g):
    passed = g["passed"]
    (x_n, x1b, x1c, x1_T, x2_n, ident, identb, xw_T, xws_T, cols, cols_s, bo_bc, rope, maskb, mask_T, v_aug, neghalf,
     ps, ps2, psx, k_op, q_op, z_Ts, o_T, rot, q_parts, big, res, stats, mv, rstd, ops_loaded, w_loaded) = (
        g[k] for k in ("x_n", "x1b", "x1c", "x1_T", "x2_n", "ident", "identb", "xw_T", "xws_T", "cols", "cols_s",
                       "bo_bc", "rope", "maskb", "mask_T", "v_aug", "neghalf", "ps", "ps2", "psx", "k_op", "q_op",
                       "z_T", "o_T", "rot", "q_parts", "big", "res", "stats", "mv", "rstd", "ops_loaded",
                       "w_loaded"))
    UNITS = 4 * KT
    SC = XH * QT

    with ExitStack() as st:
        def sb(name, shape, dt=F32):
            return st.enter_context(nc.sbuf_tensor(name, shape, dt))

        junk = sb("junk", [P, 2, SK], BF16)
        nmax = sb("nmaxx", [P, QT, XH])
        nrest = sb("nrest", [P, QT, XH])
        m_parts = sb("m_parts", [P, QT, PARTS, XH], BF16)
        m_T = sb("m_T", [PARTS * XH, S], BF16)
        v_cur = sb("v_cur", [P, KT, XH, XD + 1])
        prob = sb("probx", [P, 4, 4 * S])
        z_aug = sb("z_aug", [P, 2, S])
        rsum = sb("rsumx", [P, QT, 4])
        z_n = sb("z_n", [P, QT, XH, XD])
        z_T = sb("z_Tx", [P, S])

        def sem(name):
            return g["top"].enter_context(nc.semaphore(name))

        o_made = sem("o_made"); o_out = sem("o_out"); var3_ready = sem("var3_ready"); rstd3_ready = sem("rstd3_ready")
        x13_ready = sem("x13_ready"); x1t_ready = sem("x1t_ready"); x1t_copied = sem("x1t_copied")
        q_proj = sem("q_proj"); qparts3_ready = sem("qparts3_ready"); q3_stored = sem("q3_stored")
        q3_loaded = sem("q3_loaded"); x1b_ready = sem("x1b_ready"); tail_chain = sem("tail_chain")
        pool_tail = sem("pool_tail"); psum_zeroed = sem("psum_zeroed")
        row_scores = sem("row_scores"); row_max = sem("row_max"); mparts_ready = sem("mparts_ready")
        shift_turned = sem("shift_turned"); shift_copied = sem("shift_copied"); shift_loaded = sem("shift_loaded")
        v_ready = sem("v_ready"); col_scores = sem("col_scores"); probs = sem("probs"); pv_done = sem("pv_done")
        z_copied = sem("zx_copied"); z_turned = sem("z_turned"); z_normed = sem("z_normed")
        zn_turned = sem("zn_turned"); zn_copied = sem("zn_copied"); out_ready = sem("out_ready")
        out_taken = sem("out_taken"); var_ready = sem("varx_ready")
        rstd_ready = sem("rstdx_ready"); dve_chain = sem("dvex_chain"); dve_chain2 = sem("dvex_chain2")
        pool_chain = sem("poolx_chain"); pool_ln = sem("pool_ln")

        block = st.enter_context(nc.Block())

        ALL_OPS = 16 * (2 + B * PARTS * (PARTS + 1) + (B - 1) * PARTS * PARTS)
        e_raw = big[:, :].rearrange("p (e c d) -> p e c d", e=E, c=4)

        @block.sync
        def _(sp):
            sp.wait_ge(qparts3_ready, 1)
            q_round(sp, g, B - 1, 16 * PARTS, q3_stored, q3_loaded)
            for e in range(E):
                sp.dma_start(e_raw[:, e, 0:2, :], g["w1"][e].rearrange("(t p) d -> p t d", p=P)).then_inc(w_loaded[e // 2], 16)
                sp.dma_start(e_raw[:, e, 2:4, :], g["w2"][e].rearrange("d (t p) -> d t p", p=P)).then_inc(w_loaded[e // 2], 16)
            sp.sem_inc(shift_loaded, 1)
            with sp.Fori(0, B) as b:
                sp.wait_ge(shift_copied, b + 1)
                for c in range(PARTS):
                    sp.dma_start(q_op[SROWS + c:SROWS + c + 1, :, bass.ds(b * S, S)],
                                 m_T[XH * c:XH * (c + 1), :]).then_inc(shift_loaded, 16)
            sp.wait_ge(shift_loaded, 16 * PARTS * B + 1)

        @block.gpsimd
        def _(pool):
            pool.wait_ge(var3_ready, 1)
            nc.gpsimd.tensor_scalar(rstd[:, :], mv[:, :, 1], LN_EPS, None, ALU.add).then_inc(pool_tail, 1)
            pool.wait_ge(pool_tail, 1)
            nc.gpsimd.tensor_tensor(rstd[:, :], rstd[:, :], neghalf[:, 0:QT], ALU.pow).then_inc(rstd3_ready, 1)

            def shift_parts(b):
                ch = Steps(pool, pool_chain, b, 4)
                pool.wait_ge(shift_turned, b + 1)
                wait_alone(pool, passed, row_max, (b + 1) * SC + 2)
                ch.link(nc.gpsimd.tensor_scalar(nrest[:, :, :], nmax[:, :, :], SHIFT_MAX, None, ALU.min), passed=passed)
                ch.link(nc.gpsimd.tensor_copy(m_parts[:, :, 0, :], nrest[:, :, :]))
                ch.link(nc.gpsimd.tensor_tensor(nrest[:, :, :], nrest[:, :, :], m_parts[:, :, 0, :], ALU.subtract),
                        passed=passed)
                ch.link(nc.gpsimd.tensor_copy(m_parts[:, :, 1, :], nrest[:, :, :]))
                nc.gpsimd.tensor_tensor(m_parts[:, :, 2, :], nrest[:, :, :], m_parts[:, :, 1, :],
                                        ALU.subtract).then_inc(mparts_ready, 1)
                ch.done()

            def layer_norm(b):
                ch = Steps(pool, pool_ln, b, 1)
                wait_alone(pool, passed, var_ready, b + 1)
                ch.link(nc.gpsimd.tensor_scalar(rstd[:, :], mv[:, :, 1], LN_EPS, None, ALU.add))
                nc.gpsimd.tensor_tensor(rstd[:, :], rstd[:, :], neghalf[:, 0:QT], ALU.pow).then_inc(rstd_ready, 1)
                ch.done()

            pool.sem_inc(mparts_ready, 1)
            shift_parts(0)
            with pool.Fori(0, B - 1) as b:
                shift_parts(b + 1)
                layer_norm(b)
            layer_norm(B - 1)

        @block.scalar
        def _(act):
            act.wait_ge(x1t_ready, 1)
            nc.scalar.activation(x1_T[:, :], psx[1][:, 0:S], ACT.Copy).then_inc(x1t_copied, 1)
            act.sem_inc(probs, 2)
            act.sem_inc(z_copied, 1)

            def copy_shift(b):
                act.wait_ge(shift_turned, b + 1 + 1)
                act.wait_ge(shift_loaded, b * (16 * PARTS) + 1)
                nc.scalar.activation(m_T[:, :], psx[1].ap()[0:PARTS * XH, 0:S // 2].bitcast(BF16),
                                     ACT.Copy).then_inc(shift_copied, 1)

            def body(b, more):
                act.wait_ge(pv_done, b * UNITS + 4)
                nc.scalar.activation(v_cur[:, :, :, :].rearrange("p t h d -> p (t h d)"),
                                     v_aug[:, b, :, :, :].rearrange("p t h d -> p (t h d)"),
                                     ACT.Copy).then_inc(v_ready, 1)

                def copy_z(gr):
                    act.wait_ge(pv_done, b * UNITS + 4 * gr + 4 + 4)
                    act.wait_ge(z_turned, b * 4 + gr + 1)
                    nc.scalar.activation(z_aug[:, gr % 2, :], psx[0][:, 0:S], ACT.Copy).then_inc(z_copied, 1)

                for u in range(UNITS + 2):
                    if u < UNITS:
                        act.wait_ge(col_scores, b * UNITS + u + 1)
                        act.wait_ge(pv_done, b * UNITS + u + 1)
                        nc.scalar.activation(prob[:, u % 4, :], ps2[u % 2][:, :], ACT.Exp).then_inc(probs, 1)
                    if u >= 5 and u % 4 == 1:
                        copy_z((u - 5) // 4)
                act.wait_ge(zn_turned, b + 1)
                nc.scalar.activation(z_T[:, :], psx[1][:, 0:S], ACT.Copy).then_inc(zn_copied, 1)
                if more:
                    copy_shift(b + 1)

            copy_shift(0)
            with act.Fori(0, B - 1) as b:
                body(b, True)
            body(B - 1, False)

        @block.tensor
        def _(pe):
            def row_unit(b, i):
                h, q = i // QT, i % QT
                pe.wait_ge(row_max, b * SC + i + 1)
                nc.tensor.matmul(ps[i % 2][:, :], q_op[0:SROWS, h, bass.ds(b * S + q * P, P)],
                                 k_op[0:SROWS, b, h, :], start=True, stop=True).then_inc(row_scores, 1)

            def turn_shift(b):
                pe.wait_ge(out_taken, b + 1)
                wait_alone(pe, passed, mparts_ready, b + 1 + 1)
                for q in range(QT):
                    last = nc.tensor.transpose(psx[1].ap()[0:PARTS * XH, q * P // 2:(q + 1) * P // 2].bitcast(BF16),
                                               m_parts[:, q, :, :].rearrange("p c h -> p (c h)"), identb[:, :])
                last.then_inc(shift_turned, 1)

            def body(b, more):
                pe.wait_ge(shift_loaded, (b + 1) * (16 * PARTS) + 1)
                pe.wait_ge(v_ready, b + 1)
                pe.wait_ge(psum_zeroed, 1)

                def col_unit(u):
                    gr, kt = u // KT, u % KT
                    pe.wait_ge(probs, b * UNITS + u + 1)
                    for hh in range(4):
                        nc.tensor.matmul(ps2[u % 2][:, hh * S:(hh + 1) * S], identb[:, :], mask_T[:, kt, :],
                                         start=True, stop=False)
                        last = nc.tensor.matmul(ps2[u % 2][:, hh * S:(hh + 1) * S],
                                                k_op[0:TROWS, b, 4 * gr + hh, kt * P:(kt + 1) * P],
                                                q_op[0:TROWS, 4 * gr + hh, bass.ds(b * S, S)],
                                                start=False, stop=True)
                    last.then_inc(col_scores, 1)

                def pv_unit(u):
                    gr, kt = u // KT, u % KT
                    pe.wait_ge(probs, b * UNITS + u + 1 + 2)
                    if kt == 0:
                        pe.wait_ge(z_copied, b * 4 + gr + 1)
                    for hh in range(4):
                        last = nc.tensor.matmul(psx[0][32 * hh:32 * hh + XD + 1, 0:S], v_cur[:, kt, 4 * gr + hh, :],
                                                prob[:, u % 4, hh * S:(hh + 1) * S], start=(kt == 0),
                                                stop=(kt == KT - 1))
                    last.then_inc(pv_done, 1)

                def turn_z(gr):
                    pe.wait_ge(z_copied, b * 4 + gr + 1 + 1)
                    if gr:
                        pe.wait_ge(z_normed, b * 4 + gr)
                    for q in range(QT):
                        last = nc.tensor.transpose(psx[1][:, q * P:(q + 1) * P], z_aug[:, gr % 2, q * P:(q + 1) * P],
                                                   ident[:, :])
                    last.then_inc(z_turned, 1)

                for u in range(UNITS + 3):
                    if u < UNITS:
                        col_unit(u)
                        if more:
                            row_unit(b + 1, 2 * u)
                            row_unit(b + 1, 2 * u + 1)
                    if 2 <= u < UNITS + 2:
                        pv_unit(u - 2)
                    if u >= 6 and u % 4 == 2:
                        turn_z((u - 6) // 4)
                pe.wait_ge(z_normed, b * 4 + 4)
                for q in range(QT):
                    last = nc.tensor.transpose(psx[1][:, q * P:(q + 1) * P],
                                               z_n[:, q, :, :].rearrange("p h d -> p (h d)"), ident[:, :])
                last.then_inc(zn_turned, 1)
                pe.wait_ge(zn_copied, b + 1)
                for q in range(QT):
                    last = nc.tensor.matmul(psx[1][:, q * P:(q + 1) * P], z_T[:, q * P:(q + 1) * P], xw_T[:, 3, :],
                                            start=True, stop=True)
                last.then_inc(out_ready, 1)
                if more:
                    turn_shift(b + 1)

            pe.sem_inc(z_turned, 2)
            pe.sem_inc(shift_turned, 1)
            out_proj(nc, psx[0], z_Ts, o_T).then_inc(o_made, 1)
            pe.wait_ge(ops_loaded, ALL_OPS)
            for i in range(4):
                row_unit(0, i)
            pe.wait_ge(x13_ready, 1)
            for q in range(QT):
                last = nc.tensor.transpose(psx[1][:, q * P:(q + 1) * P], x1c[:, q, :], ident[:, :])
            last.then_inc(x1t_ready, 1)
            for i in range(4, 8):
                row_unit(0, i)
            pe.wait_ge(x1t_copied, 1)
            for n, w in enumerate((xw_T[:, 0, :], xws_T[:, 0, :])):
                nc.tensor.matmul(ps2[n][:, 0:S], w, x1_T[:, :], start=True, stop=True).then_inc(q_proj, 1)
            for i in range(8, SC):
                row_unit(0, i)
            pe.wait_ge(q3_loaded, 16 * PARTS * PARTS)
            pe.wait_ge(qparts3_ready, 1)
            pe.sem_inc(pv_done, 4)
            turn_shift(0)
            with pe.Fori(0, B - 1) as b:
                body(b, True)
            body(B - 1, False)

        @block.vector
        def _(dve):
            ch_tail = Steps(dve, tail_chain, 0, 7)
            dve.wait_ge(o_made, 1)
            nc.vector.tensor_tensor(res[:, :, :], psx[0][:, 0:S].rearrange("p (q d) -> p q d", q=QT),
                                    x_n[:, 2 * B - 2:2 * B, :], ALU.add).then_inc(o_out, 1)
            dve.wait_ge(o_out, 1)
            moments(nc, ch_tail, res, stats, mv, var3_ready, passed)
            nc.vector.memset(psx[0][:, 0:S], 0.0).then_inc(psum_zeroed, 1)

            def tail_norm():
                dve.wait_ge(rstd3_ready, 1)
                normalise(nc, res, mv, rstd, x1c, x13_ready)
                dve.wait_ge(x13_ready, 1)
                nc.vector.tensor_tensor(x1b[:, 2 * B - 2:2 * B, :], x1c[:, :, :], both(bo_bc[:, :]),
                                        ALU.add).then_inc(x1b_ready, 1)

            def tail_queries():
                for n, bias in enumerate((cols, cols_s)):
                    dve.wait_ge(q_proj, n + 1)
                    last = nc.vector.scalar_tensor_tensor(rot[:, n, 0:S], ps2[n][:, 0:S], bias[:, 0:1], rope[:, n, 0:S],
                                                          ALU.add, ALU.mult)
                ch_tail.link(last)
                dve.wait_ge(ops_loaded, ALL_OPS)
                nc.vector.tensor_tensor(rot[:, 0, 0:S], rot[:, 0, 0:S], rot[:, 1, 0:S], ALU.add).then_inc(tail_chain, 1)
                ch_tail.n += 1
                dve.wait_ge(tail_chain, ch_tail.n)
                split_queries(nc, ch_tail, rot, q_parts, qparts3_ready)
                ch_tail.done()

            dve.sem_inc(row_max, 2)
            dve.sem_inc(out_taken, 1)

            def row_unit(b, i):
                h, q = i // QT, i % QT
                if i == 0:
                    dve.wait_ge(mparts_ready, b + 1)
                dve.wait_ge(row_max, b * SC + i + 1)
                wait_alone(dve, passed, row_scores, b * SC + i + 1)
                nc.vector.tensor_tensor_reduce(junk[:, i % 2, :], ps[i % 2][:, :], maskb[:, q, :], -1.0, 3.0e38,
                                               ALU.add, ALU.min, nmax[:, q, h:h + 1]).then_inc(row_max, 1)

            def body(b, more):
                ch = Steps(dve, dve_chain2, b, 4 * 2 + 4)

                def norm_z(gr):
                    dve.wait_ge(z_turned, b * 4 + gr + 1 + 2)
                    z = psx[1][:, 0:S].rearrange("p (q h r) -> p q h r", q=QT, h=4)
                    ch.link(nc.vector.tensor_scalar(rsum[:, :, :], z[:, :, :, XD], TINY, None, ALU.max))
                    ch.link(nc.vector.reciprocal(rsum[:, :, :], rsum[:, :, :]))
                    nc.vector.tensor_tensor(z_n[:, :, 4 * gr:4 * gr + 4, :], z[:, :, :, 0:XD],
                                            rsum[:, :, :].rearrange("p q (h a) -> p q h a", a=1).broadcast_to((P, QT, 4, XD)),
                                            ALU.mult).then_inc(z_normed, 1)

                for u in range(UNITS + 3):
                    if u < UNITS and more:
                        row_unit(b + 1, 2 * u)
                        row_unit(b + 1, 2 * u + 1)
                    if u >= 6 and u % 4 == 2:
                        norm_z((u - 6) // 4)
                dve.wait_ge(out_ready, b + 1)
                two = lambda v: v.rearrange("p (q d) -> p q d", q=QT)
                ins = nc.vector.tensor_tensor(res[:, :, :], two(psx[1][:, 0:S]), x1b[:, bass.ds(2 * b, 2), :], ALU.add)
                ins.then_inc(out_taken, 1)
                dve.wait_ge(out_taken, b + 1 + 1)
                moments(nc, ch, res, stats, mv, var_ready, passed)
                dve.wait_ge(rstd_ready, b + 1)
                for q in range(QT):
                    ch.link(nc.vector.tensor_scalar(x2_n[:, 2 * b + q, :], res[:, q, :], mv[:, q, 0:1],
                                                    rstd[:, q:q + 1], ALU.subtract, ALU.mult))
                ch.done()

            for i in range(SC):
                row_unit(0, i)
                if i == 3:
                    tail_norm()
                if i == 7:
                    tail_queries()
            dve.wait_ge(x1b_ready, 1)
            with dve.Fori(0, B - 1) as b:
                body(b, True)
            body(B - 1, False)


def moe_block(nc, g):
    passed = g["passed"]
    (x2_n, ident, cols, b2_n, neghalf, iota, ps, ps2, psx, big, w_loaded, out) = (
        g[k] for k in ("x2_n", "ident", "cols", "b2_n", "neghalf", "iota", "ps", "ps2", "psx", "big", "w_loaded",
                       "out"))
    NORM_COL, GATE_COL, B1_COL = 2, 3, 11
    HALF = TOK // 2

    with ExitStack() as st:
        def sb(name, shape, dt=F32):
            return st.enter_context(nc.sbuf_tensor(name, shape, dt))

        def sem(name):
            return g["top"].enter_context(nc.semaphore(name))

        w1_T = sb("w1_T", [P, 2 * E, P])
        w2_T = sb("w2_T", [P, 2 * E, D])
        ms = sb("ms", [P, TILES])
        rms = sb("rms", [P, TILES])
        t_n = sb("t_n", [P, TILES, D])
        t_T = sb("t_T", [P, TOK])
        logits = sb("logits", [P, TILES, E])
        top8 = sb("top8", [P, TILES, 8])
        idx8 = sb("idx8", [P, TILES, 8], U32)
        idx = sb("idx", [P, TILES, 2])
        gap = sb("gap", [P, TILES])
        egap = sb("egap", [P, TILES])
        wts = sb("wts", [P, 3, TILES])
        comb = sb("comb", [P, TILES, E])
        comb2 = sb("comb2", [P, TILES, E])
        comb_T = sb("comb_T", [E, TOK])
        w1_cur = sb("w1_cur", [P, 2, 2, P])
        hid = sb("hid", [P, 2, 2, TOK])
        acc = sb("acc", [P, TILES, D])
        stats = sb("statsm", [P, TILES, 6])
        mv = sb("mvm", [P, TILES, 2])
        rstd = sb("rstdm", [P, TILES])
        fin = sb("fin", [P, TILES, D])

        ms_ready = sem("ms_ready"); rms_ready = sem("rms_ready"); t_ready = sem("t_ready")
        t_turned = sem("t_turned"); t_copied = sem("t_copied"); gates = sem("gates"); gap_ready = sem("gap_ready")
        egap_ready = sem("egap_ready"); comb_ready = sem("comb_ready"); comb_turned = sem("comb_turned")
        comb_copied = sem("comb_copied"); bias_ready = sem("bias_ready"); w1c_ready = sem("w1c_ready")
        hid_ready = sem("hid_ready"); gelu_done = sem("gelu_done"); o_ready = sem("o_ready")
        o_added = sem("o_added"); varm_ready = sem("varm_ready"); rstdm_ready = sem("rstdm_ready")
        fin_ready = sem("fin_ready"); stored = sem("stored"); chain = sem("dvem_chain")
        pool_chain = sem("poolm_chain")

        psH = [ps[0], ps[1], psx[0], psx[1]]
        psO = [ps2[0][:, 0:512], ps2[1][:, 0:512]]

        e_raw = big[:, :].rearrange("p (e c d) -> p e c d", e=E, c=4)
        psW = [psx[0][:, :], psx[1][:, :], ps2[1][:, 0:512], ps2[1][:, 512:1024]]
        w_turned = sem("w_turned"); w_copied = sem("w_copied")

        block = st.enter_context(nc.Block())

        @block.sync
        def _(sp):
            ov = out.rearrange("b (t p) m -> p (b t) m", p=P)
            for hf in range(2):
                sp.wait_ge(fin_ready, hf + 1)
                sp.dma_start(ov[:, 4 * hf:4 * hf + 4, :], fin[:, 4 * hf:4 * hf + 4, :]).then_inc(stored, 16)
            sp.wait_ge(stored, 32)

        @block.gpsimd
        def _(pool):
            def copy_w1(e, slot):
                pool.wait_ge(hid_ready, e * 4 + 4)
                nc.gpsimd.tensor_copy(w1_cur[:, slot, :, :], w1_T[:, bass.ds(2 * e, 2), :]).then_inc(w1c_ready, 1)

            pool.wait_ge(ms_ready, 1)
            nc.gpsimd.tensor_scalar(rms[:, :], ms[:, :], RMS_EPS, None, ALU.add).then_inc(pool_chain, 1)
            pool.wait_ge(pool_chain, 1)
            nc.gpsimd.tensor_tensor(rms[:, :], rms[:, :], neghalf[:, :], ALU.pow).then_inc(rms_ready, 1)
            pool.wait_ge(w_copied, E)
            with pool.Fori(0, E // 2) as i:
                copy_w1(2 * i, 0)
                copy_w1(2 * i + 1, 1)
            for hf in range(2):
                half = slice(4 * hf, 4 * hf + 4)
                pool.wait_ge(varm_ready, hf + 1)
                nc.gpsimd.tensor_scalar(rstd[:, half], mv[:, half, 1], LN_EPS, None, ALU.add).then_inc(pool_chain, 1)
                pool.wait_ge(pool_chain, hf + 2)
                nc.gpsimd.tensor_tensor(rstd[:, half], rstd[:, half], neghalf[:, half], ALU.pow).then_inc(rstdm_ready, 1)

        @block.scalar
        def _(act):
            for n in range(E):
                act.wait_ge(w_turned, n + 1)
                dst = (w1_T, w2_T)[n % 2]
                nc.scalar.activation(dst[:, 4 * (n // 2):4 * (n // 2) + 4, :], psW[n % 4].rearrange("p (a c) -> p a c", a=4),
                                     ACT.Copy).then_inc(w_copied, 1)
            act.wait_ge(gap_ready, 1)
            nc.scalar.activation(egap[:, :], gap[:, :], ACT.Exp).then_inc(egap_ready, 1)
            for hf in range(2):
                act.wait_ge(comb_turned, hf + 1)
                nc.scalar.activation(comb_T[:, hf * HALF:(hf + 1) * HALF], ps2[hf][0:E, 512:1024],
                                     ACT.Copy).then_inc(comb_copied, 1)
            act.sem_inc(gelu_done, 4)

            def gelu(e, slot):
                for u in range(4):
                    t, hf = u // 2, u % 2
                    act.wait_ge(o_ready, e * 2 + 2)
                    wait_alone(act, passed, hid_ready, e * 4 + 8 + u + 1)
                    nc.scalar.activation(hid[:, slot, t, hf * HALF:(hf + 1) * HALF], psH[u][:, :], ACT.Gelu,
                                         bias=cols[:, bass.ds(B1_COL + 2 * e + t, 1)]).then_inc(gelu_done, 1)

            with act.Fori(0, E // 2) as i:
                gelu(2 * i, 0)
                gelu(2 * i + 1, 1)

        @block.tensor
        def _(pe):
            for n in range(E):
                pe.wait_ge(w_loaded[n // 2], 64)
                if n >= 4:
                    pe.wait_ge(w_copied, n - 3)
                for c in range(4):
                    e, t = 2 * (n // 2) + c // 2, c % 2
                    last = nc.tensor.transpose(psW[n % 4][:, c * P:(c + 1) * P], e_raw[:, e, 2 * (n % 2) + t, :], ident[:, :])
                last.then_inc(w_turned, 1)
            for hf in range(2):
                pe.wait_ge(t_ready, hf + 1)
                for c in range(4):
                    last = nc.tensor.transpose(psH[hf][:, c * P:(c + 1) * P], t_n[:, 4 * hf + c, :], ident[:, :])
                last.then_inc(t_turned, 1)
            pe.wait_ge(t_copied, 2)
            for t in range(TILES):
                last = nc.tensor.matmul(ps2[0][:, t * E:(t + 1) * E], t_T[:, t * P:(t + 1) * P],
                                        cols[:, GATE_COL:GATE_COL + E], start=True, stop=True)
            last.then_inc(gates, 1)
            pe.wait_ge(w_copied, E)
            pe.wait_ge(comb_ready, 1)
            for hf in range(2):
                for c in range(4):
                    last = nc.tensor.transpose(ps2[hf][0:E, 512 + c * P:512 + (c + 1) * P], comb[:, 4 * hf + c, :],
                                               ident[:, :])
                last.then_inc(comb_turned, 1)
            for hf in range(2):
                pe.wait_ge(comb_copied, hf + 1)
                for c in range(4):
                    last = nc.tensor.matmul(psO[hf][:, c * D:(c + 1) * D], comb_T[:, (4 * hf + c) * P:(4 * hf + c + 1) * P],
                                            b2_n[:, :], start=True, stop=True)
                last.then_inc(bias_ready, 1)
            pe.sem_inc(o_ready, 4)
            pe.sem_inc(hid_ready, 8)

            def hidden(e, slot):
                pe.wait_ge(w1c_ready, e + 1)
                for u in range(4):
                    t, hf = u // 2, u % 2
                    pe.wait_ge(gelu_done, e * 4 + u + 1)
                    nc.tensor.matmul(psH[u][:, :], w1_cur[:, slot, t, :], t_T[:, hf * HALF:(hf + 1) * HALF],
                                     start=True, stop=True).then_inc(hid_ready, 1)

            def outputs(e, slot):
                pe.wait_ge(gelu_done, e * 4 + 4 + 4)
                for hf in range(2):
                    pe.wait_ge(o_added, e * 2 + hf + 1)
                    for c in range(4):
                        for t in range(2):
                            last = nc.tensor.matmul(psO[hf][:, c * D:(c + 1) * D],
                                                    hid[:, slot, t, (4 * hf + c) * P:(4 * hf + c + 1) * P],
                                                    w2_T[:, bass.ds(2 * e + t, 1), :].rearrange("p a d -> p (a d)"),
                                                    start=(t == 0), stop=(t == 1))
                    last.then_inc(o_ready, 1)

            hidden(0, 0)
            with pe.Fori(0, E // 2 - 1) as i:
                hidden(2 * i + 1, 1)
                outputs(2 * i, 0)
                hidden(2 * i + 2, 0)
                outputs(2 * i + 1, 1)
            hidden(E - 1, 1)
            outputs(E - 2, 0)
            outputs(E - 1, 1)

        @block.vector
        def _(dve):
            LINKS = 10
            ch = Steps(dve, chain, 0, LINKS)
            for t in range(TILES):
                last = nc.vector.tensor_tensor_reduce(t_n[:, t, :], x2_n[:, t, :], x2_n[:, t, :], 1.0 / D, 0.0, ALU.mult,
                                                      ALU.add, ms[:, t:t + 1])
            last.then_inc(ms_ready, 1)
            dve.wait_ge(rms_ready, 1)
            for hf in range(2):
                for c in range(4):
                    t = 4 * hf + c
                    last = nc.vector.tensor_scalar(t_n[:, t, :], x2_n[:, t, :], rms[:, t:t + 1], None, ALU.mult)
                last.then_inc(t_ready, 1)
            for hf in range(2):
                dve.wait_ge(t_turned, hf + 1)
                nc.vector.tensor_scalar(t_T[:, hf * HALF:(hf + 1) * HALF], psH[hf][:, :], cols[:, NORM_COL:NORM_COL + 1],
                                        None, ALU.mult).then_inc(t_copied, 1)
            dve.wait_ge(gates, 1)
            ch.link(nc.vector.tensor_copy(logits[:, :, :], ps2[0][:, 0:TILES * E].rearrange("p (t e) -> p t e", t=TILES)))
            for t in range(TILES):
                last = nc.vector.max(top8[:, t, :], logits[:, t, :])
            ch.link(last)
            for t in range(TILES):
                last = nc.vector.max_index(idx8[:, t, :], top8[:, t, :], logits[:, t, :])
            ch.link(last)
            nc.vector.tensor_tensor(gap[:, :], top8[:, :, 1], top8[:, :, 0], ALU.subtract).then_inc(gap_ready, 1)
            ch.link(nc.vector.tensor_copy(idx[:, :, :], idx8[:, :, 0:2]))
            dve.wait_ge(egap_ready, 1)
            ch.link(nc.vector.tensor_scalar(wts[:, 0, :], egap[:, :], 1.0, None, ALU.add))
            ch.link(nc.vector.reciprocal(wts[:, 1, :], wts[:, 0, :]))
            ch.link(nc.vector.tensor_tensor(wts[:, 2, :], egap[:, :], wts[:, 1, :], ALU.mult))
            bc = lambda v: v.rearrange("p (t a) -> p t a", a=1).broadcast_to((P, TILES, E))
            experts = iota[:, :].rearrange("p (a e) -> p a e", a=1).broadcast_to((P, TILES, E))
            nc.vector.tensor_tensor(comb[:, :, :], experts, bc(idx[:, :, 0]), ALU.is_equal)
            ch.link(nc.vector.tensor_tensor(comb2[:, :, :], experts, bc(idx[:, :, 1]), ALU.is_equal))
            nc.vector.tensor_tensor(comb[:, :, :], comb[:, :, :], bc(wts[:, 1, :]), ALU.mult)
            ch.link(nc.vector.tensor_tensor(comb2[:, :, :], comb2[:, :, :], bc(wts[:, 2, :]), ALU.mult))
            nc.vector.tensor_tensor(comb[:, :, :], comb[:, :, :], comb2[:, :, :], ALU.add).then_inc(comb_ready, 1)
            quad = lambda v: v.rearrange("p (t d) -> p t d", t=4)
            for hf in range(2):
                dve.wait_ge(bias_ready, hf + 1)
                last = nc.vector.scalar_tensor_tensor(acc[:, 4 * hf:4 * hf + 4, :], x2_n[:, 4 * hf:4 * hf + 4, :], 2.0,
                                                      quad(psO[hf]), ALU.mult, ALU.add)
                if hf == 0:
                    last.then_inc(chain, 1)
                    ch.n += 1
                    dve.wait_ge(chain, ch.n)
                else:
                    last.then_inc(o_added, 1)
            dve.wait_ge(o_added, 1)
            dve.sem_inc(o_added, 1)
            ch.done()

            def add(e):
                for hf in range(2):
                    dve.wait_ge(o_ready, e * 2 + 4 + hf + 1)
                    dve.wait_ge(o_added, e * 2 + hf + 1)
                    for c in range(4):
                        t = 4 * hf + c
                        last = nc.vector.scalar_tensor_tensor(acc[:, t, :], psO[hf][:, c * D:(c + 1) * D],
                                                              comb[:, t, bass.ds(e, 1)], acc[:, t, :], ALU.mult, ALU.add)
                    last.then_inc(o_added, 1)

            with dve.Fori(0, E) as e:
                add(e)
            dve.wait_ge(o_added, 2 * E + 2)
            for hf in range(2):
                for t in range(4 * hf, 4 * hf + 4):
                    last = nc.vector.bn_stats(stats[:, t, :], acc[:, t, :])
                last.then_inc(chain, 1)
                dve.wait_ge(chain, LINKS + hf + 1)
                for t in range(4 * hf, 4 * hf + 4):
                    last = nc.vector.bn_aggr(mv[:, t, :], stats[:, t, :])
                last.then_inc(varm_ready, 1)
            for hf in range(2):
                dve.wait_ge(rstdm_ready, hf + 1)
                for t in range(4 * hf, 4 * hf + 4):
                    last = nc.vector.tensor_scalar(fin[:, t, :], acc[:, t, :], mv[:, t, 0:1], rstd[:, t:t + 1],
                                                   ALU.subtract, ALU.mult)
                last.then_inc(fin_ready, 1)


_INS = ["x", "ctx_1024", "mask_1x1xSxS2_bk1", "L0_attn_Q", "L0_attn_K", "L0_attn_V", "L0_attn_O", "L0_xattn_Wq",
        "L0_xattn_bq", "L0_xattn_Wk", "L0_xattn_bk", "L0_xattn_Wv", "L0_xattn_bv", "L0_xattn_Wo", "L0_xattn_bo",
        "L0_ffn_norm_weight", "L0_ffn_gate_w", "L0_ffn_w1", "L0_ffn_b1", "L0_ffn_w2", "L0_ffn_b2"]


def _constants():
    import numpy as np

    causal = np.zeros((P, S), np.float32)
    causal[:, P:] = np.where(np.arange(P)[None, :] <= np.arange(P)[:, None], 0.0, NEG_CAUSAL)
    inv = np.exp(np.arange(0, XD, 2, dtype=np.float32) * (-(4.0 * np.log(np.float32(10.0))) / XD)).astype(np.float32)
    angle = np.arange(SK, dtype=np.float32)[None, :] * inv[:, None]
    sin, cos = np.sin(angle), np.cos(angle)
    dim = np.arange(P) % XD
    own = np.where((dim % 2 == 0)[:, None], sin[dim // 2], -sin[dim // 2])
    rope = np.stack([own, -cos[dim // 2]], axis=1).astype(np.float32)
    fill = np.zeros((2, B * XH * SK), np.uint16)
    fill[1] = 0x3F80
    return {"ident": np.eye(P, dtype=np.float32), "causal": causal, "rope": rope, "fill": fill,
            "iota": np.arange(E, dtype=np.float32)[None, :]}


def kernel(**inputs):
    import numpy as np
    import concourse.bacc as bacc
    from concourse.bass_utils import run_bass_kernel_spmd

    nc = bacc.Bacc("TRN2", target_bir_lowering=False, num_devices=1)
    arrays, args = {}, []

    def give(name, a):
        a = np.ascontiguousarray(a)
        arrays[name] = a
        args.append(nc.dram_tensor(name, a.shape, mybir.dt.from_np(a.dtype), kind="ExternalInput").ap())

    for name in _INS:
        give(f"in_{name}", inputs[name])
    for name, a in _constants().items():
        give(f"const_{name}", a)
        if name == "fill":
            args[-1] = args[-1].bitcast(BF16)
    args.append(nc.dram_tensor("out_0", (B, S, D), F32, kind="ExternalOutput").ap())
    build(nc, *args)
    r = run_bass_kernel_spmd(nc, [arrays], core_ids=[0])
    return r.results[0]["out_0"]
```

```python
from contextlib import ExitStack

import concourse.bass as bass
from concourse import mybir

F32 = mybir.dt.float32
BF16 = mybir.dt.bfloat16
U8 = mybir.dt.uint8
U32 = mybir.dt.uint32
I32 = mybir.dt.int32
ALU = mybir.AluOpType
ACT = mybir.ActivationFunctionType
AX = mybir.AxisListType

B, S, D = 4, 256, 128
SK = 512
H, DH = 16, 64
XH, XD = 16, 8
E, F = 8, 256
P = 128
QT = S // P
KT = SK // P
TILES = B * QT
TOK = B * S
NEG_CAUSAL = -1.0e10
NEG_MASK = -1.0e30
SHIFT_MAX = 1.0e15
TINY = 1.0e-30
LN_EPS = 1e-5
RMS_EPS = 1e-6
PARTS = 3
PROWS = XD * PARTS * PARTS
SROWS = 96
TROWS = SROWS + PARTS


def wait_alone(eng, passed, sem, value):
    eng.wait_ge(sem, value)
    eng.sem_inc(passed, 1)


class Steps:

    def __init__(self, eng, sem, i=0, per=0, base=0):
        self.eng, self.sem, self.i, self.per, self.base, self.n = eng, sem, i, per, base, 0

    def link(self, ins, passed=None):
        ins.then_inc(self.sem, 1)
        self.n += 1
        value = self.i * self.per + self.base + self.n
        if passed is None:
            self.eng.wait_ge(self.sem, value)
        else:
            wait_alone(self.eng, passed, self.sem, value)

    def done(self):
        assert self.n == self.per, (self.n, self.per)


ROW_LEAD, ROWS_A_STEP, OUT_STEP = 2, 3, 3
OPS_FIXED = 2
OPS_K = PARTS * (PARTS + 1)
OPS_Q = PARTS


class Plan:

    def __init__(self, tiles):
        self.tiles, self.n, self.t0 = tiles, len(tiles), tiles[0]
        self.units = 4 * self.n
        self.heads = 4 // self.n
        self.rows = XH // self.heads * QT
        self.k0, self.width = tiles[0] * P, self.n * P


def for_either(eng, early_open, program):
    flag = eng.value_load(early_open[0:1, 0:1])
    with eng.If(flag == 0):
        program(Plan([KT - 1]))
    with eng.If(flag != 0):
        program(Plan(list(range(KT))))


def build(nc, x, ctx_in, mask, aQ, aK, aV, aO, Wq, bq, Wk, bk, Wv, bv, Wo, bo, norm_w, gate_w,
          w1, b1, w2, b2, c_ident, c_causal, c_rope, c_fill, c_iota, out):
    with ExitStack() as top:
        def sb(name, shape, dt=F32, scope=top):
            return scope.enter_context(nc.sbuf_tensor(name, shape, dt))

        def sem(name):
            return top.enter_context(nc.semaphore(name))

        x_n = sb("x_n", [P, TILES, D])
        x2_n = x_n
        ident = sb("ident", [P, P])
        cols = sb("cols", [P, 27])
        b2_n = sb("b2_n", [E, D])
        neghalf = sb("neghalf", [P, TILES])
        iota = sb("iota", [P, E])
        big = sb("big", [P, 2 * H * D])
        ps = [top.enter_context(nc.psum_tensor(f"ps{i}", [P, 512], F32)) for i in range(2)]
        ps2 = [top.enter_context(nc.psum_tensor(f"pd{i}", [P, 1024], F32)) for i in range(2)]
        psx = [top.enter_context(nc.psum_tensor(f"px{i}", [P, 512], F32)) for i in range(2)]

        k_parts_d = nc.dram_tensor("k_parts_d", (B, XH, XD, PARTS, SK), BF16, kind="Internal").ap()
        q_parts_d = nc.dram_tensor("q_parts_d", (B, XH, XD, PARTS, S), BF16, kind="Internal").ap()

        passed = sem("passed")
        ops_loaded = sem("ops_loaded")
        w_loaded = [sem(f"w_loaded{n}") for n in range(2)]
        flag_ready = sem("flag_ready")
        row_scores = sem("row_scores"); row_max = sem("row_max")

        with ExitStack() as att:
            identb = sb("identb", [P, P], BF16, att)
            early_open = sb("early_open", [1, 1], I32, att)
            xw_T = sb("xw_T", [P, 4, D], scope=att)
            xws_T = sb("xws_T", [P, 2, D], scope=att)
            cols_s = sb("cols_s", [P, 2], scope=att)
            bv_bc = sb("bv_bc", [P, D], scope=att)
            bo_bc = sb("bo_bc", [P, D], scope=att)
            rope = sb("rope", [P, 2, SK], scope=att)
            maskb = sb("maskb", [P, QT, SK], BF16, att)
            mask_T = sb("mask_T", [P, KT, S], BF16, att)
            v_aug = sb("v_aug", [P, B, KT, XH, XD + 1], scope=att)
            x1b = sb("x1b", [P, TILES, D], scope=att)
            x1c = sb("x1c", [P, QT, D], scope=att)
            x1_T = sb("x1_T", [P, S], scope=att)
            z_T = sb("z_T", [P, 8, S], scope=att)
            o_T = sb("o_T", [P, 8, D], scope=att)
            rot = sb("rot", [P, 2, SK], scope=att)
            q_parts = sb("q_parts", [P, PARTS, S], BF16, att)
            res = sb("res", [P, QT, D], scope=att)
            stats = sb("stats", [P, QT, 6], scope=att)
            mv = sb("mv", [P, QT, 2], scope=att)
            rstd = sb("rstd", [P, QT], scope=att)
            nmax = sb("nmaxx", [P, B, QT, XH], scope=att)
            q_op = sb("q_op", [P, XH, TOK], BF16, att)
            k_op = sb("k_op", [P, B, XH, SK], BF16, att)
            self_block(nc, locals())
            cross_and_moe_block(nc, locals())


def out_proj(nc, bank, z_T, o_T, q):
    for j in range(8):
        last = nc.tensor.matmul(bank[:, q * D:(q + 1) * D], z_T[:, j, q * P:(q + 1) * P], o_T[:, j, :],
                                start=(j == 0), stop=(j == 7))
    return last


def moments(nc, ch, res, stats, mv, ready, passed):
    for q in range(QT):
        ch.link(nc.vector.bn_stats(stats[:, q, :], res[:, q, :]), passed=passed)
        last = nc.vector.bn_aggr(mv[:, q, :], stats[:, q, :])
    last.then_inc(ready, 1)


def normalise(nc, res, mv, rstd, dst, ready):
    for q in range(QT):
        last = nc.vector.tensor_scalar(dst[:, q, :], res[:, q, :], mv[:, q, 0:1], rstd[:, q:q + 1],
                                       ALU.subtract, ALU.mult)
    last.then_inc(ready, 1)


def both(row):
    return row.rearrange("p (a d) -> p a d", a=1).broadcast_to((P, QT, D))


def split_queries(nc, ch, rot, q_parts, ready):
    ch.link(nc.vector.tensor_copy(q_parts[:, 0, :], rot[:, 0, 0:S]))
    ch.link(nc.vector.tensor_tensor(rot[:, 1, 0:S], rot[:, 0, 0:S], q_parts[:, 0, :], ALU.subtract))
    ch.link(nc.vector.tensor_copy(q_parts[:, 1, :], rot[:, 1, 0:S]))
    nc.vector.tensor_tensor(q_parts[:, 2, :], rot[:, 1, 0:S], q_parts[:, 1, :], ALU.subtract).then_inc(ready, 1)


def q_round(eng, g, b, value, stored, loaded):
    q_parts, q_parts_d, q_op = g["q_parts"], g["q_parts_d"], g["q_op"]
    eng.dma_start(q_parts_d[b].rearrange("h d a k -> (h d) (a k)"),
                  q_parts[:, :, :].rearrange("p a k -> p (a k)")).then_inc(stored, 16)
    eng.wait_ge(stored, value)
    rows = XD * PARTS
    for c in range(PARTS):
        eng.dma_start(q_op[rows * c:rows * (c + 1), :, bass.ds(b * S, S)],
                      q_parts_d[b].rearrange("h d a k -> (d a) h k")).then_inc(loaded, 16)


def row_scores_unit(nc, pe, g, plan, b, i, done):
    ps, q_op, k_op, identb, maskb = (g[k] for k in ("ps", "q_op", "k_op", "identb", "maskb"))
    h0, q = i // QT * plan.heads, i % QT
    for hh in range(plan.heads):
        dst = ps[i % 2][:, hh * plan.width:(hh + 1) * plan.width]
        ks = slice(plan.k0, plan.k0 + plan.width)
        nc.tensor.matmul(dst, identb[:, :], maskb[:, q, ks], start=True, stop=False)
        last = nc.tensor.matmul(dst, q_op[0:SROWS, h0 + hh, b * S + q * P:b * S + (q + 1) * P],
                                k_op[0:SROWS, b, h0 + hh, ks], start=False, stop=True)
    last.then_inc(done, 1)


def row_max_unit(nc, g, plan, b, i, done):
    h0, q = i // QT * plan.heads, i % QT
    nc.vector.tensor_reduce(g["nmax"][:, b, q, h0:h0 + plan.heads],
                            g["ps"][i % 2][:, :].rearrange("p (h k) -> p h k", k=plan.width), AX.X, ALU.max,
                            negate=True).then_inc(done, 1)


def self_block(nc, g):
    passed = g["passed"]
    (x, ctx_in, mask, aQ, aK, aV, aO, Wq, bq, Wk, bk, Wv, bv, Wo, bo, norm_w, gate_w, b1, b2, c_ident, c_causal,
     c_rope, c_iota, c_fill) = (
        g[k] for k in ("x", "ctx_in", "mask", "aQ", "aK", "aV", "aO", "Wq", "bq", "Wk", "bk", "Wv", "bv", "Wo",
                       "bo", "norm_w", "gate_w", "b1", "b2", "c_ident", "c_causal", "c_rope", "c_iota", "c_fill"))
    (x_n, x1b, x1c, x1_T, ident, identb, xw_T, xws_T, cols, cols_s, bv_bc, bo_bc, b2_n, rope, maskb, mask_T, v_aug,
     neghalf, iota, ps, ps2, psx, k_parts_d, q_parts_d, k_op, q_op, z_T, o_T, rot, q_parts, big, ops_loaded, res,
     stats, mv, rstd) = (
        g[k] for k in ("x_n", "x1b", "x1c", "x1_T", "ident", "identb", "xw_T", "xws_T", "cols", "cols_s", "bv_bc",
                       "bo_bc", "b2_n", "rope", "maskb", "mask_T", "v_aug", "neghalf", "iota", "ps", "ps2", "psx",
                       "k_parts_d", "q_parts_d", "k_op", "q_op", "z_T", "o_T", "rot", "q_parts", "big",
                       "ops_loaded", "res", "stats", "mv", "rstd"))
    early_open, row_scores, row_max = g["early_open"], g["row_scores"], g["row_max"]

    with ExitStack() as st:
        def sb(name, shape, dt=F32):
            return st.enter_context(nc.sbuf_tensor(name, shape, dt))

        def sem(name):
            return g["top"].enter_context(nc.semaphore(name))

        qk_T = big[:, 0:H * D].rearrange("p (h d) -> p h d", h=H)
        v_n = big[:, H * D:2 * H * D].rearrange("p (t f) -> p t f", t=QT)
        y_T = sb("y_T", [P, 8, S])
        causal = sb("causal", [P, S])
        v_T = sb("v_T", [P, H * DH])
        x_T = sb("x_T", [P, TOK])
        xb_T = sb("xb_T", [P, S])
        prob = sb("prob", [P, 4, 3 * P])
        prob_T = sb("prob_T", [P, 4, 3 * P])
        nmax = sb("nmax", [P, 4, 2])
        rsum = sb("rsum", [P, 4, 2])
        rinv = sb("rinv", [P, 4, 2])
        ctx_n = sb("ctx_n", [P, KT, D])
        ctx_T = sb("ctx_T", [P, SK])
        k_parts = sb("k_parts", [P, PARTS, SK], BF16)
        rows = sb("rows", [27, D])
        rows_s = sb("rows_s", [2, D])
        mask_raw = sb("mask_raw", [P, QT, SK], U8)
        open_row = sb("open_row", [P, 2])
        q_raw = y_T[0:DH, :, :].rearrange("p a b -> p (a b)").rearrange("p (h d) -> p h d", h=H)
        k_raw = z_T[0:DH, :, :].rearrange("p a b -> p (a b)").rearrange("p (h d) -> p h d", h=H)
        v_raw = v_n[:, 0, :].rearrange("p (j d) -> p j d", j=8)
        o_raw = x1b[:, :, :].rearrange("p t d -> p (t d)")
        xw_raw = prob_T[:, :, 0:D]

        ld_x = sem("ld_x"); ld_qk = [sem(f"ld_qk{n}") for n in range(2)]; ld_v = sem("ld_v"); ld_o = sem("ld_o")
        ld_id = sem("ld_id"); ld_ca = sem("ld_ca"); ld_xw = sem("ld_xw"); ld_rows = sem("ld_rows")
        ld_mask = sem("ld_mask"); ld_tab = sem("ld_tab"); ld_bc = sem("ld_bc"); ld_ctx = sem("ld_ctx")
        identb_ready = sem("identb_ready"); maskb_ready = sem("maskb_ready"); rows_s_ready = sem("rows_s_ready")
        open_max = sem("open_max"); open_ready = sem("open_ready"); open_summed = sem("open_summed")
        flag_ready = g["flag_ready"]
        consts_ready = sem("consts_ready"); setup_ready = sem("setup_ready")
        setup_dve = sem("setup_dve"); setup_act = sem("setup_act")
        xb_ready = sem("xb_ready"); proj_ready = sem("proj_ready"); proj_dve = sem("proj_dve")
        proj_act = sem("proj_act"); score_ready = sem("score_ready"); masked = sem("masked")
        exp_ready = sem("exp_ready"); rinv_ready = sem("rinv_ready"); prob_ready = sem("prob_ready")
        prob_T_ready = sem("prob_T_ready"); prob_T_copied = sem("prob_T_copied"); pv_ready = sem("pv_ready")
        z_copied = sem("z_copied"); var_ready = sem("var_ready"); rstd_ready = sem("rstd_ready")
        x1_ready = sem("x1_ready")
        kparts_ready = sem("kparts_ready"); kparts_stored = sem("kparts_stored")
        qparts_ready = sem("qparts_ready"); qparts_stored = sem("qparts_stored")
        dve_chain = sem("dve_chain"); dve_ln = sem("dve_ln"); dve_q = sem("dve_q"); pool_chain = sem("pool_chain")

        STEP_ITEMS = {0: ["y2"], 1: ["ctx"], 2: ["y3"], 3: ["k0", "k1"], 4: ["y4", "v1"], 5: ["o"], 6: ["y5", "v3"],
                      7: ["cv"], 8: ["y6"], 9: ["xt"], 10: ["y7"], 11: ["q0", "q1"], 12: ["next-v0"],
                      13: ["next-v2"], 14: ["next-y0"], 15: ["next-y1"]}
        ITEMS = [n for t in range(H) for n in STEP_ITEMS[t]]
        BEFORE = ["next-y0", "next-v0", "next-v2", "next-y1"]
        OF_LAST = ["o", "xt", "q0", "q1"]
        STEP_FIRST = {t: [n for n in names if n not in OF_LAST] for t, names in STEP_ITEMS.items()}
        for t, name in ((0, "s-xw"), (1, "s-rows"), (5, "s-o0"), (9, "s-o1"), (11, "s-mask0"), (12, "s-mask1")):
            STEP_FIRST[t].append(name)
        FIRST_ALL = BEFORE + [n for t in range(H) for n in STEP_FIRST[t]]
        NI, NI_FIRST = len(ITEMS), len(FIRST_ALL)
        assert NI_FIRST % 2 == 0 and NI % 2 == 0
        by = lambda n: "act" if n.replace("next-", "")[0] == "v" or n in ("ctx", "xt", "s-rows", "s-o0") else "dve"
        COUNT = {e: sum(by(n) == e for n in ITEMS) for e in ("act", "dve")}
        COUNT_FIRST = {e: sum(by(n) == e for n in FIRST_ALL) for e in ("act", "dve")}

        class Place:

            def __init__(self, b, first, last):
                self.b, self.first, self.last = b, first, last

            def items(self, t):
                names = (STEP_FIRST if self.first else STEP_ITEMS).get(t, ())
                return [n for n in names if not (self.last and n.startswith("next-"))]

            def at(self, name):
                return FIRST_ALL.index(name, len(BEFORE)) if self.first else ITEMS.index(name)

            def bank(self, name):
                return ps[self.at(name) % 2]

            def made(self, name):
                return self.at(name) + 1 if self.first else self.b * NI + (NI_FIRST - NI) + self.at(name) + 1

            def base(self, eng):
                return 0 if self.first else self.b * COUNT[eng] + (COUNT_FIRST[eng] - COUNT[eng])

            def emptied_at(self, n):
                names = FIRST_ALL if self.first else ITEMS
                eng = by(names[n])
                return eng, self.base(eng) + sum(by(m) == eng for m in names[:n + 1])

            def emptied(self, name):
                return self.emptied_at(self.at(name))[1]

        def wait_bank(pe, pl, name):
            n = pl.at(name) - 2
            if n >= 0:
                eng, v = pl.emptied_at(n)
            else:
                eng, v = "dve", pl.base("dve") + n + 1
            pe.wait_ge(proj_act if eng == "act" else proj_dve, v)

        ROW_STEP = 12

        def row_units(plan, t):
            n = ROW_LEAD * plan.rows
            each = -(-n // (H + 4 - ROW_STEP))
            return [(j // plan.rows, j % plan.rows) for j in range(each * (t - ROW_STEP), min(each * (t - ROW_STEP + 1), n))
                    ] if t >= ROW_STEP else []

        psS = [ps2[0][:, 0:512], ps2[0][:, 512:1024]]
        psT = [ps2[1][:, 0:512], ps2[1][:, 512:1024]]
        psZ = psx
        banks = [ps[0][:, :], ps[1][:, :]] + psS + psT + [psx[0][:, :], psx[1][:, :]]

        block = st.enter_context(nc.Block())

        @block.sync
        def _(sp):
            half = lambda w, n: w[n * H // 2:(n + 1) * H // 2].rearrange("n h m -> h n m")
            xv = x.rearrange("b (t p) m -> p (b t) m", p=P)
            for n in range(2):
                sp.dma_start(q_raw[:, n * H // 2:(n + 1) * H // 2, :], half(aQ, n)).then_inc(ld_qk[n], 16)
            sp.dma_start(x_n[:, 0:4, :], xv[:, 0:4, :]).then_inc(ld_x, 16)
            sp.dma_start(x_n[:, 4:8, :], xv[:, 4:8, :]).then_inc(ld_x, 16)
            sp.dma_start(mask_raw[:, :, :], mask.rearrange("a b (t p) k -> p (a b t) k", p=P)).then_inc(ld_mask, 16)
            sp.dma_start(v_raw, aV.rearrange("(j two) h m -> (two h) j m", two=2)).then_inc(ld_v, 16)
            sp.dma_start(causal[:, :], c_causal).then_inc(ld_ca, 16)
            for n, w in enumerate((Wq, Wk, Wv, Wo)):
                sp.dma_start(xw_raw[:, n, :], w).then_inc(ld_xw, 16)
            sp.dma_start(ctx_n[:, :, :], ctx_in[0].rearrange("(t p) m -> p t m", p=P)).then_inc(ld_ctx, 16)
            sp.dma_start(rope[:, :, :], c_rope).then_inc(ld_tab, 16)
            sp.dma_start(o_raw, aO).then_inc(ld_o, 16)
            sp.dma_start(k_op[SROWS:TROWS, :, :, :].rearrange("p b h k -> p (b h k)"),
                         c_fill[1:2, :].broadcast_to((PARTS, B * XH * SK))).then_inc(ops_loaded, 16)
            sp.dma_start(q_op[PROWS:SROWS, :, :].rearrange("p h k -> p (h k)"),
                         c_fill[0:1, 0:XH * TOK].broadcast_to((SROWS - PROWS, XH * TOK))).then_inc(ops_loaded, 16)

            sp.sem_inc(kparts_stored, 1)
            sp.sem_inc(qparts_stored, 1)
            sp.wait_ge(flag_ready, 1)

            def body(pl, plan):
                b = pl.b
                issued = OPS_FIXED if pl.first else OPS_FIXED + b * OPS_K + (b - 1) * OPS_Q
                sp.wait_ge(ops_loaded, issued * 16)
                ks = slice(plan.k0, plan.k0 + plan.width)
                if not pl.last:
                    sp.wait_ge(proj_ready, pl.made("ctx"))
                    sp.dma_start(ctx_n[:, plan.t0:, :], ctx_in[b + 1, ks].rearrange("(t p) m -> p t m", p=P)
                                 ).then_inc(ld_ctx, 16)
                sp.wait_ge(kparts_ready, b + 1)
                sp.dma_start(k_parts_d[b, :, :, :, ks].rearrange("h d c k -> (h d) c k"),
                             k_parts[:, :, 0:plan.width]).then_inc(kparts_stored, 16)
                sp.wait_ge(kparts_stored, (b + 1) * 16 + 1)
                for c in range(PARTS + 1):
                    for a in range(PARTS):
                        r0, r1 = PARTS * XD * c + a, PARTS * XD * (c + 1)
                        sp.dma_start(k_op[r0:r1:PARTS, b, :, ks],
                                     k_parts_d[b, :, :, c % PARTS, ks].rearrange("h d k -> d h k")).then_inc(ops_loaded, 16)
                if not pl.first:
                    sp.wait_ge(qparts_ready, b)
                    q_round(sp, g, b - 1, b * 16 + 1, qparts_stored, ops_loaded)

            def program(plan):
                body(Place(0, True, False), plan)
                with sp.Fori(0, B - 2) as i:
                    body(Place(i + 1, False, False), plan)
                body(Place(B - 1, False, True), plan)

            for_either(sp, early_open, program)

        @block.gpsimd
        def _(pool):
            pool.memset(neghalf[:, :], -0.5).then_inc(consts_ready, 1)
            pool.memset(v_aug[:, :, :, :, XD:XD + 1], 1.0).then_inc(consts_ready, 1)

            def body(pl):
                b = pl.b
                for h in range(H):
                    s = h % 4
                    pool.wait_ge(rinv_ready, b * H + h + 1)
                    nc.gpsimd.tensor_tensor(prob[:, s, 0:P], prob[:, s, 0:P],
                                            rinv[:, s, 0:1].broadcast_to((P, P)), ALU.mult)
                    nc.gpsimd.tensor_tensor(prob[:, s, P:3 * P], prob[:, s, P:3 * P],
                                            rinv[:, s, 1:2].broadcast_to((P, S)), ALU.mult).then_inc(prob_ready, 1)
                    if h == 6 and not pl.first:
                        ch = Steps(pool, pool_chain, b - 1, 1)
                        wait_alone(pool, passed, var_ready, b)
                        ch.link(nc.gpsimd.tensor_scalar(rstd[:, :], mv[:, :, 1], LN_EPS, None, ALU.add))
                        nc.gpsimd.tensor_tensor(rstd[:, :], rstd[:, :], neghalf[:, 0:QT],
                                                ALU.pow).then_inc(rstd_ready, 1)
                        ch.done()

            body(Place(0, True, False))
            with pool.Fori(0, B - 2) as i:
                body(Place(i + 1, False, False))
            body(Place(B - 1, False, True))

        @block.scalar
        def _(act):
            half = lambda w, n: w[n * H // 2:(n + 1) * H // 2].rearrange("n h m -> h n m")
            for n in range(2):
                act.dma_start(k_raw[:, n * H // 2:(n + 1) * H // 2, :], half(aK, n)).then_inc(ld_qk[n], 16)
            act.dma_start(ident[:, :], c_ident).then_inc(ld_id, 16)
            one = lambda v: v.rearrange("(a n) -> a n", a=1)
            for r0, n, v in ((0, 1, one(bq)), (1, 1, one(bk)), (2, 1, one(norm_w)), (3, E, gate_w),
                             (11, 2 * E, b1.rearrange("e (t p) -> (e t) p", p=P))):
                act.dma_start(rows[r0:r0 + n, :], v).then_inc(ld_rows, 16)

            def take(n, dst, src):
                act.wait_ge(setup_ready, n + 1)
                nc.scalar.activation(dst, src, ACT.Copy).then_inc(setup_act, 1)

            take(1, qk_T[:, 4:8, :], banks[1].rearrange("p (a c) -> p a c", a=4))
            take(3, qk_T[:, 12:16, :], banks[3].rearrange("p (a c) -> p a c", a=4))
            take(5, x_T[:, 512:1024], banks[5])
            take(7, v_T[:, 512:1024], banks[7])
            act.dma_start(b2_n[:, :], b2).then_inc(ld_bc, 16)
            act.dma_start(bv_bc[:, :], one(bv).broadcast_to((P, D))).then_inc(ld_bc, 16)
            act.dma_start(bo_bc[:, :], one(bo).broadcast_to((P, D))).then_inc(ld_bc, 16)
            act.dma_start(iota[:, :], c_iota.broadcast_to((P, E))).then_inc(ld_bc, 16)
            act.wait_ge(flag_ready, 1)

            act.sem_inc(prob_T_copied, 2)
            act.sem_inc(z_copied, 2)

            def v_copy(n, ready, bank):
                act.wait_ge(proj_ready, ready)
                nc.scalar.activation(v_n[:, n // 2, (n % 2) * 512:(n % 2) * 512 + 512], bank[:, :],
                                     ACT.Copy).then_inc(proj_act, 1)

            def exps(b, h):
                s = h % 4
                act.wait_ge(masked, b * H + h + 1 + 2)
                nc.scalar.activation(prob[:, s, 0:P], prob[:, s, 0:P], ACT.Exp, scale=-1.0,
                                     bias=nmax[:, s, 0:1], accum_out=rsum[:, s, 0:1])
                nc.scalar.activation(prob[:, s, P:3 * P], prob[:, s, P:3 * P], ACT.Exp, scale=-1.0,
                                     bias=nmax[:, s, 1:2], accum_out=rsum[:, s, 1:2]).then_inc(exp_ready, 1)

            def take_prob_T(b, h):
                act.wait_ge(prob_T_ready, b * H + h + 1 + 4)
                act.wait_ge(pv_ready, b * H + h + 1)
                nc.scalar.activation(prob_T[:, h % 4, :], psT[h % 2][:, 0:3 * P],
                                     ACT.Copy).then_inc(prob_T_copied, 1)

            def take_z(b, j):
                act.wait_ge(pv_ready, b * H + 2 * j + 2 + 4)
                nc.scalar.activation(z_T[:, j % 8, :], psZ[j % 2][:, 0:S], ACT.Copy).then_inc(z_copied, 1)

            def step(pl, plan, t):
                b = pl.b
                if t < H:
                    exps(b, t)
                if t - 3 < H and (t >= 3 or not pl.first):
                    take_prob_T(b, t - 3)
                if t % 2 == 0 and (t >= 6 or not pl.first):
                    take_z(b, (t - 5) // 2)
                for name in pl.items(t):
                    if by(name) != "act":
                        continue
                    if name == "ctx":
                        act.wait_ge(proj_ready, pl.made(name))
                        nc.scalar.activation(ctx_T[:, 0:plan.width], pl.bank(name)[:, 0:plan.width],
                                             ACT.Copy).then_inc(proj_act, 1)
                    elif name == "s-rows":
                        act.wait_ge(proj_ready, pl.made(name))
                        nc.scalar.activation(cols[:, :], pl.bank(name)[:, 0:27], ACT.Copy)
                        nc.scalar.activation(cols_s[:, :], pl.bank(name)[:, 32:34], ACT.Copy).then_inc(proj_act, 1)
                    elif name == "s-o0":
                        act.wait_ge(proj_ready, pl.made(name))
                        nc.scalar.activation(o_T[:, 0:4, :], pl.bank(name)[:, :].rearrange("p (a c) -> p a c", a=4),
                                             ACT.Copy).then_inc(proj_act, 1)
                    elif name == "xt":
                        act.wait_ge(proj_ready, pl.made(name))
                        nc.scalar.activation(x1_T[:, :], pl.bank(name)[:, 0:S], ACT.Copy).then_inc(proj_act, 1)
                    else:
                        v_copy(int(name[-1]), pl.made(name), pl.bank(name))

            v_copy(0, 2, ps[1])
            v_copy(2, 3, ps[0])

            def program(plan):
                for t in range(H):
                    step(Place(0, True, False), plan, t)
                with act.Fori(0, B - 2) as i:
                    for t in range(H):
                        step(Place(i + 1, False, False), plan, t)
                for t in range(H + 5):
                    step(Place(B - 1, False, True), plan, t)

            for_either(act, early_open, program)

        @block.tensor
        def _(pe):
            def transposes(n, src):
                for c in range(4):
                    last = nc.tensor.transpose(banks[n][:, c * P:(c + 1) * P], src(c), ident[:, :])
                last.then_inc(setup_ready, 1)

            for n in range(4):
                pe.wait_ge(ld_qk[n // 2], 32)
                for c in range(4):
                    h = 4 * n + c
                    last = nc.tensor.matmul(banks[n][:, c * P:(c + 1) * P], q_raw[:, h, :], k_raw[:, h, :],
                                            start=True, stop=True)
                last.then_inc(setup_ready, 1)
            pe.wait_ge(ld_id, 16)
            pe.wait_ge(ld_x, 32)
            for n in range(4, 6):
                transposes(n, lambda c: x_n[:, 4 * (n - 4) + c, :])
            pe.wait_ge(ld_v, 16)
            for n in range(6, 8):
                transposes(n, lambda c: v_raw[:, 4 * (n - 6) + c, :])
            pe.wait_ge(open_ready, 1)
            pe.wait_ge(setup_dve, 2)
            nc.tensor.matmul(banks[2][0:1, 0:1], open_row[:, 1:2], open_row[:, 1:2], start=True,
                             stop=True).then_inc(open_summed, 1)
            pe.wait_ge(setup_act, 4)
            pe.wait_ge(setup_dve, 4)
            pe.wait_ge(flag_ready, 1)
            pe.sem_inc(pv_ready, 4)
            pe.sem_inc(prob_T_ready, 4)

            def y_proj(b, j, bank):
                for i in range(2):
                    last = nc.tensor.matmul(bank[:, i * S:(i + 1) * S], qk_T[:, 2 * j + i, :], x_T[:, bass.ds(b * S, S)],
                                            start=True, stop=True)
                last.then_inc(proj_ready, 1)

            def v_proj(n, bank):
                nc.tensor.matmul(bank[:, :], xb_T[:, (n // 2) * P:(n // 2 + 1) * P],
                                 v_T[:, (n % 2) * 512:(n % 2) * 512 + 512], start=True, stop=True).then_inc(proj_ready, 1)

            def turn_four(bank, src):
                for c in range(4):
                    last = nc.tensor.transpose(bank[:, c * P:(c + 1) * P], src(c), ident[:, :])
                last.then_inc(proj_ready, 1)

            def item(pl, plan, name):
                b, bank = pl.b, pl.bank(name)
                wait_bank(pe, pl, name)
                if name[0] == "y":
                    y_proj(b, int(name[1]), bank)
                elif name[0] == "v":
                    v_proj(int(name[1]), bank)
                elif name == "next-v0":
                    pe.wait_ge(xb_ready, b + 2)
                    v_proj(0, bank)
                elif name == "next-v2":
                    v_proj(2, bank)
                elif name.startswith("next-y"):
                    y_proj(b + 1, int(name[-1]), bank)
                elif name == "ctx":
                    pe.wait_ge(ld_ctx, (b + 1) * 16)
                    for c, kt in enumerate(plan.tiles):
                        last = nc.tensor.transpose(bank[:, c * P:(c + 1) * P], ctx_n[:, kt, :], ident[:, :])
                    last.then_inc(proj_ready, 1)
                elif name == "s-xw":
                    pe.wait_ge(ld_xw, 64)
                    turn_four(bank, lambda c: xw_raw[:, c, :])
                elif name == "s-rows":
                    pe.wait_ge(rows_s_ready, 2)
                    nc.tensor.transpose(bank[:, 0:27], rows[:, :], ident[0:27, 0:27])
                    nc.tensor.transpose(bank[:, 32:34], rows_s[:, :], ident[0:2, 0:2]).then_inc(proj_ready, 1)
                elif name in ("s-o0", "s-o1"):
                    pe.wait_ge(ld_o, 16)
                    turn_four(bank, lambda c: o_raw[:, (4 * int(name[-1]) + c) * P:(4 * int(name[-1]) + c + 1) * P])
                elif name in ("s-mask0", "s-mask1"):
                    pe.wait_ge(identb_ready, 1)
                    mbank = bank.ap().bitcast(BF16)[:, 0:2 * S].rearrange("p (k q) -> p k q", k=2)
                    for k in range(2):
                        kt = 2 * int(name[-1]) + k
                        for q in range(QT):
                            last = nc.tensor.transpose(mbank[:, k, q * P:(q + 1) * P],
                                                       maskb[:, q, kt * P:(kt + 1) * P], identb[:, :])
                    last.then_inc(proj_ready, 1)
                elif name in ("k0", "k1"):
                    pe.wait_ge(proj_act, pl.emptied("ctx"))
                    if pl.first:
                        pe.wait_ge(proj_dve, pl.emptied("s-xw"))
                    w = xw_T[:, 1, :] if name == "k0" else xws_T[:, 1, :]
                    nc.tensor.matmul(bank[:, 0:plan.width], w, ctx_T[:, 0:plan.width], start=True, stop=True).then_inc(proj_ready, 1)
                elif name == "cv":
                    for c in range(plan.n):
                        last = nc.tensor.matmul(bank[:, c * P:(c + 1) * P], ctx_T[:, c * P:(c + 1) * P],
                                                xw_T[:, 2, :], start=True, stop=True)
                    last.then_inc(proj_ready, 1)
                elif name == "o":
                    pe.wait_ge(z_copied, b * (H // 2) + 2)
                    out_proj(nc, bank, z_T, o_T, 0)
                    out_proj(nc, bank, z_T, o_T, 1).then_inc(proj_ready, 1)
                elif name == "xt":
                    pe.wait_ge(x1_ready, b)
                    for q in range(QT):
                        last = nc.tensor.transpose(bank[:, q * P:(q + 1) * P], x1c[:, q, :], ident[:, :])
                    last.then_inc(proj_ready, 1)
                else:
                    pe.wait_ge(proj_act, pl.emptied("xt"))
                    w = xw_T[:, 0, :] if name == "q0" else xws_T[:, 0, :]
                    nc.tensor.matmul(bank[:, 0:S], w, x1_T[:, :], start=True, stop=True).then_inc(proj_ready, 1)

            def scores(pl, h):
                b = pl.b
                if h >= 4:
                    pe.wait_ge(proj_dve, pl.emptied(f"y{h // 2}"))
                elif pl.first:
                    pe.wait_ge(proj_dve, h // 2 + 1)
                else:
                    pe.wait_ge(proj_dve, pl.base("dve") - 1 + h // 2)
                pe.wait_ge(masked, b * H + h + 1)
                nc.tensor.matmul(psS[h % 2][:, 0:P], y_T[:, h % 8, 0:P], x_T[:, bass.ds(b * S, P)], start=True, stop=True)
                nc.tensor.matmul(psS[h % 2][:, P:3 * P], y_T[:, h % 8, P:2 * P], x_T[:, bass.ds(b * S, S)], start=True,
                                 stop=True).then_inc(score_ready, 1)

            def turn(b, h):
                pe.wait_ge(prob_ready, b * H + h + 1)
                pe.wait_ge(prob_T_copied, b * H + h + 1)
                for c in range(3):
                    last = nc.tensor.transpose(psT[h % 2][:, c * P:(c + 1) * P],
                                               prob[:, h % 4, c * P:(c + 1) * P], ident[:, :])
                last.then_inc(prob_T_ready, 1)

            def pv(pl, h):
                b = pl.b
                pe.wait_ge(prob_T_copied, b * H + h + 1 + 2)
                if h == 0:
                    pe.wait_ge(proj_act, 2 if pl.first else pl.base("act"))
                if h == 8:
                    pe.wait_ge(proj_act, pl.emptied("v3"))
                if h % 2 == 0:
                    pe.wait_ge(z_copied, b * (H // 2) + h // 2 + 1)
                r = DH * (h % 2)
                z = psZ[(h // 2) % 2]
                v = lambda t: v_n[:, t, (h % H) * DH:(h % H + 1) * DH]
                nc.tensor.matmul(z[r:r + DH, 0:P], v(0), prob_T[:, h % 4, 0:P], start=True, stop=True)
                nc.tensor.matmul(z[r:r + DH, P:S], v(0), prob_T[:, h % 4, P:S], start=True, stop=False)
                nc.tensor.matmul(z[r:r + DH, P:S], v(1), prob_T[:, h % 4, S:3 * P], start=False,
                                 stop=True).then_inc(pv_ready, 1)

            def step(pl, plan, t):
                if t < H:
                    scores(pl, t)
                if t - 3 < H and (t >= 3 or not pl.first):
                    turn(pl.b, t - 3)
                for name in pl.items(t):
                    item(pl, plan, name)
                if pl.last:
                    for rb, i in row_units(plan, t):
                        if rb == 0 and i == 0:
                            pe.wait_ge(proj_dve, pl.emptied("q1"))
                            pe.wait_ge(ops_loaded, 16 * (OPS_FIXED + (B - 1) * OPS_K + (B - 2) * OPS_Q))
                        pe.wait_ge(row_max, rb * plan.rows + i + 1)
                        row_scores_unit(nc, pe, g, plan, rb, i, row_scores)
                if t >= 4 or not pl.first:
                    pv(pl, t - 4)

            y_proj(0, 0, ps[0])
            pe.wait_ge(xb_ready, 1)
            v_proj(0, ps[1])
            pe.wait_ge(proj_dve, 1)
            v_proj(2, ps[0])
            pe.wait_ge(proj_act, 1)
            y_proj(0, 1, ps[1])

            def program(plan):
                for t in range(H):
                    step(Place(0, True, False), plan, t)
                with pe.Fori(0, B - 2) as i:
                    for t in range(H):
                        step(Place(i + 1, False, False), plan, t)
                for t in range(H + 4):
                    step(Place(B - 1, False, True), plan, t)

            for_either(pe, early_open, program)

        @block.vector
        def _(dve):
            def take(n, dst, src):
                dve.wait_ge(setup_ready, n + 1)
                nc.vector.tensor_copy(dst, src).then_inc(setup_dve, 1)

            dve.wait_ge(ld_id, 16)
            nc.vector.tensor_copy(identb[:, :], ident[:, :]).then_inc(identb_ready, 1)
            take(0, qk_T[:, 0:4, :], banks[0].rearrange("p (a c) -> p a c", a=4))
            take(2, qk_T[:, 8:12, :], banks[2].rearrange("p (a c) -> p a c", a=4))
            dve.wait_ge(ld_mask, 16)
            nc.vector.tensor_scalar(maskb[:, :, :], mask_raw[:, :, :], NEG_MASK, None, ALU.mult).then_inc(maskb_ready, 1)
            dve.wait_ge(maskb_ready, 1)
            nc.vector.tensor_reduce(open_row[:, 0:1], maskb[:, :, 0:(KT - 1) * P], AX.XY, ALU.max).then_inc(open_max, 1)
            dve.wait_ge(open_max, 1)
            nc.vector.tensor_scalar(open_row[:, 1:2], open_row[:, 0:1], -1.0, None, ALU.is_ge).then_inc(open_ready, 1)
            take(4, x_T[:, 0:512], banks[4])
            take(6, v_T[:, 0:512], banks[6])
            dve.wait_ge(open_summed, 1)
            nc.vector.tensor_copy(early_open[:, :], banks[2][0:1, 0:1]).then_inc(flag_ready, 1)
            dve.wait_ge(ld_rows, 80)
            pair = lambda v: v.rearrange("p (i two) -> p i two", two=2)
            for i in range(2):
                nc.vector.tensor_copy(pair(rows_s[:, :])[:, :, i], pair(rows[0:2, :])[:, :, 1 - i]).then_inc(rows_s_ready, 1)
            dve.wait_ge(ld_ca, 16)
            dve.wait_ge(setup_act, 4)
            dve.wait_ge(flag_ready, 1)
            dve.sem_inc(masked, 2)
            dve.sem_inc(row_max, 2)

            def copy_xb(b):
                nc.vector.tensor_copy(xb_T[:, :], x_T[:, bass.ds(b * S, S)]).then_inc(xb_ready, 1)

            def take_y(j, ready, bank):
                dve.wait_ge(proj_ready, ready)
                nc.vector.tensor_copy(y_T[:, 2 * (j % 4):2 * (j % 4) + 2, :],
                                      bank[:, :].rearrange("p (a c) -> p a c", a=2)).then_inc(proj_dve, 1)

            def mask_scores(b, h):
                s = h % 4
                dve.wait_ge(prob_T_ready, b * H + h + 1)
                wait_alone(dve, passed, score_ready, b * H + h + 1)
                nc.vector.tensor_tensor_reduce(prob[:, s, 0:P], psS[h % 2][:, 0:P], causal[:, P:2 * P], -1.0,
                                               3.0e38, ALU.add, ALU.min, nmax[:, s, 0:1])
                nc.vector.tensor_tensor_reduce(prob[:, s, P:3 * P], psS[h % 2][:, P:3 * P], causal[:, :], -1.0,
                                               3.0e38, ALU.add, ALU.min, nmax[:, s, 1:2]).then_inc(masked, 1)

            def invert(b, h):
                dve.wait_ge(exp_ready, b * H + h + 1)
                nc.vector.reciprocal(rinv[:, h % 4, :], rsum[:, h % 4, :]).then_inc(rinv_ready, 1)

            four = lambda v: v.rearrange("p (a c) -> p a c", a=4)

            def item(pl, plan, name, ch, chl, chq):
                b, bank, width = pl.b, pl.bank(name), plan.width
                if name[0] == "y":
                    take_y(int(name[1]), pl.made(name), bank)
                    return
                if name.startswith("next-"):
                    take_y(int(name[-1]), pl.made(name), bank)
                    return
                dve.wait_ge(proj_ready, pl.made(name))
                if name == "s-xw":
                    nc.vector.tensor_copy(xw_T[:, :, :], four(bank[:, :]))
                    pairs = lambda v: v.rearrange("p a (i two) -> p a i two", two=2)
                    for i in range(2):
                        last = nc.vector.tensor_copy(pairs(xws_T[:, :, :])[:, :, :, i],
                                                     pairs(four(bank[:, :])[:, 0:2, :])[:, :, :, 1 - i])
                    last.then_inc(proj_dve, 1)
                elif name == "s-o1":
                    nc.vector.tensor_copy(o_T[:, 4:8, :], four(bank[:, :])).then_inc(proj_dve, 1)
                elif name in ("s-mask0", "s-mask1"):
                    kt = 2 * int(name[-1])
                    nc.vector.tensor_copy(mask_T[:, kt:kt + 2, :], bank.ap().bitcast(BF16)[:, 0:2 * S].rearrange(
                        "p (k q) -> p k q", k=2)).then_inc(proj_dve, 1)
                elif name in ("k0", "k1"):
                    if pl.first and name == "k0":
                        dve.wait_ge(proj_act, pl.emptied("s-rows"))
                        dve.wait_ge(ld_tab, 16)
                        dve.wait_ge(ld_bc, 64)
                        dve.wait_ge(consts_ready, 2)
                    n = int(name[1])
                    bias = (cols, cols_s)[n][:, 1:2]
                    nc.vector.scalar_tensor_tensor(rot[:, n, 0:width], bank[:, 0:width], bias,
                                                   rope[:, n, plan.k0:plan.k0 + width], ALU.add,
                                                   ALU.mult).then_inc(proj_dve, 1)
                    if n == 1:
                        dve.wait_ge(proj_dve, pl.emptied("k1"))
                        r0, r1 = rot[:, 0, 0:width], rot[:, 1, 0:width]
                        ch.link(nc.vector.tensor_tensor(r0, r0, r1, ALU.add))
                        dve.wait_ge(kparts_stored, b * 16 + 1)
                        ch.link(nc.vector.tensor_copy(k_parts[:, 0, 0:width], r0))
                        ch.link(nc.vector.tensor_tensor(r1, r0, k_parts[:, 0, 0:width], ALU.subtract))
                        ch.link(nc.vector.tensor_copy(k_parts[:, 1, 0:width], r1))
                        nc.vector.tensor_tensor(k_parts[:, 2, 0:width], r1, k_parts[:, 1, 0:width],
                                                ALU.subtract).then_inc(kparts_ready, 1)
                elif name == "cv":
                    heads = lambda v, t: v.rearrange("p (t h d) -> p t h d", t=t, h=XH)
                    nc.vector.tensor_tensor(v_aug[:, b, plan.t0:, :, 0:XD].rearrange("p t h d -> p t h d"),
                                            heads(bank[:, 0:width], plan.n),
                                            heads(bv_bc[:, :], 1).broadcast_to((P, plan.n, XH, XD)),
                                            ALU.add).then_inc(proj_dve, 1)
                elif name == "o":
                    last = nc.vector.tensor_tensor(res[:, :, :], bank[:, 0:S].rearrange("p (q d) -> p q d", q=QT),
                                                   x_n[:, bass.ds(2 * b - 2, 2), :], ALU.add)
                    last.then_inc(proj_dve, 1)
                    dve.wait_ge(proj_dve, pl.emptied("o"))
                    moments(nc, chl, res, stats, mv, var_ready, passed)
                elif name in ("q0", "q1"):
                    n = int(name[1])
                    bias = (cols, cols_s)[n][:, 0:1]
                    nc.vector.scalar_tensor_tensor(rot[:, n, 0:S], bank[:, 0:S], bias, rope[:, n, 0:S], ALU.add,
                                                   ALU.mult).then_inc(proj_dve, 1)
                    if n == 1:
                        dve.wait_ge(proj_dve, pl.emptied("q1"))
                        chq.link(nc.vector.tensor_tensor(rot[:, 0, 0:S], rot[:, 0, 0:S], rot[:, 1, 0:S], ALU.add))
                        dve.wait_ge(qparts_stored, (b - 1) * 16 + 1)
                        split_queries(nc, chq, rot, q_parts, qparts_ready)

            def body(pl, plan):
                b = pl.b
                ch = Steps(dve, dve_chain, b, 4)
                chl = Steps(dve, dve_ln, b - 1, 2)
                chq = Steps(dve, dve_q, b - 1, 4)
                for t in range(H + 4 if pl.last else H):
                    if t < H:
                        mask_scores(b, t)
                    if t <= H and (t >= 1 or not pl.first):
                        invert(b, t - 1)
                    if pl.last:
                        for rb, i in row_units(plan, t):
                            dve.wait_ge(row_scores, rb * plan.rows + i + 1)
                            row_max_unit(nc, g, plan, rb, i, row_max)
                    if t == 8 and not pl.first:
                        dve.wait_ge(rstd_ready, b)
                        normalise(nc, res, mv, rstd, x1c, x1_ready)
                        dve.wait_ge(x1_ready, b)
                        nc.vector.tensor_tensor(x1b[:, bass.ds(2 * b - 2, 2), :], x1c[:, :, :], both(bo_bc[:, :]),
                                                ALU.add)
                    if t == 9 and not pl.last:
                        dve.wait_ge(proj_ready, pl.made("v3"))
                        copy_xb(b + 1)
                    for name in pl.items(t):
                        if by(name) == "dve":
                            item(pl, plan, name, ch, chl, chq)
                ch.done()
                if not pl.first:
                    chl.done()
                    chq.done()

            copy_xb(0)
            take_y(0, 1, ps[0])
            take_y(1, 4, ps[1])

            def program(plan):
                body(Place(0, True, False), plan)
                with dve.Fori(0, B - 2) as i:
                    body(Place(i + 1, False, False), plan)
                body(Place(B - 1, False, True), plan)

            for_either(dve, early_open, program)


def mixture(nc, g, st, sem, c):
    passed = g["passed"]
    (x2_n, ident, cols, b2_n, neghalf, iota, ps, ps2, psx, out) = (
        g[k] for k in ("x2_n", "ident", "cols", "b2_n", "neghalf", "iota", "ps", "ps2", "psx", "out"))
    (t_n, t_T, w1_T, w2_T, w1_cur, old, t_copied, w_copied, w1c_ready, out_taken, z_copied, z_normed,
     x2c_copied) = (
        c[k] for k in ("t_n", "t_T", "w1_T", "w2_T", "w1_cur", "old", "t_copied", "w_copied", "w1c_ready",
                       "out_taken", "z_copied", "z_normed", "x2c_copied"))
    GATE_COL, B1_COL = 3, 11
    HALF = TOK // 2

    def sb(name, shape, dt=F32):
        return st.enter_context(nc.sbuf_tensor(name, shape, dt))

    logits = sb("logits", [P, TILES, E])
    top8 = sb("top8", [P, TILES, 8])
    idx8 = sb("idx8", [P, TILES, 8], U32)
    idx = sb("idx", [P, TILES, 2])
    gap = sb("gap", [P, TILES])
    tgap = sb("tgap", [P, TILES])
    wts = sb("wts", [P, 2, TILES])
    comb = sb("comb", [P, TILES, E])
    comb2 = sb("comb2", [P, TILES, E])
    hid = old[1].rearrange("p (s t n) -> p s t n", s=2, t=2)
    acc = old[2][:, 0:TILES * D].rearrange("p (t d) -> p t d", d=D)
    fin = old[2][:, TILES * D:2 * TILES * D].rearrange("p (t d) -> p t d", d=D)
    comb_T = old[3][0:E, 0:TOK]
    gate_T = old[3][0:E, TOK:2 * TOK]
    stats = sb("statsm", [P, TILES, 6])
    mv = sb("mvm", [P, TILES, 2])
    rstd = sb("rstdm", [P, TILES])

    gates = sem("gates"); gates_T = sem("gates_T"); gates_copied = sem("gates_copied"); gap_ready = sem("gap_ready")
    tgap_ready = sem("tgap_ready"); comb_ready = sem("comb_ready"); comb_turned = sem("comb_turned")
    comb_copied = sem("comb_copied"); bias_ready = sem("bias_ready")
    hid_ready = sem("hid_ready"); gelu_done = sem("gelu_done"); o_ready = sem("o_ready")
    o_added = sem("o_added"); varm_ready = sem("varm_ready"); rstdm_ready = sem("rstdm_ready")
    fin_ready = sem("fin_ready"); stored = sem("stored"); chain = sem("dvem_chain")
    pool_chain = sem("poolm_chain")

    psH = [ps[0], ps[1], psx[0], psx[1]]
    psO = [ps2[0][:, 0:512], ps2[1][:, 0:512]]

    class Programs:
        pass

    moe = Programs()

    def sync(sp):
        ov = out.rearrange("b (t p) m -> p (b t) m", p=P)
        for hf in range(2):
            sp.wait_ge(fin_ready, hf + 1)
            sp.dma_start(ov[:, 4 * hf:4 * hf + 4, :], fin[:, 4 * hf:4 * hf + 4, :]).then_inc(stored, 16)
        sp.wait_ge(stored, 32)

    def gpsimd(pool):
        def copy_w1(e, slot):
            pool.wait_ge(hid_ready, e * 4 + 4)
            nc.gpsimd.tensor_copy(w1_cur[:, slot, :, :], w1_T[:, bass.ds(2 * e, 2), :]).then_inc(w1c_ready, 1)

        with pool.Fori(1, E // 2) as i:
            copy_w1(2 * i, 0)
            copy_w1(2 * i + 1, 1)
        for hf in range(2):
            half = slice(4 * hf, 4 * hf + 4)
            pool.wait_ge(varm_ready, hf + 1)
            nc.gpsimd.tensor_scalar(rstd[:, half], mv[:, half, 1], LN_EPS, None, ALU.add).then_inc(pool_chain, 1)
            pool.wait_ge(pool_chain, hf + 1)
            nc.gpsimd.tensor_tensor(rstd[:, half], rstd[:, half], neghalf[:, half], ALU.pow).then_inc(rstdm_ready, 1)

    def scalar(act):
        for e in range(2):
            act.wait_ge(w_copied, 1)
            nc.scalar.activation(w1_cur[:, e, :, :], w1_T[:, 2 * e:2 * e + 2, :], ACT.Copy).then_inc(w1c_ready, 1)
        act.sem_inc(gelu_done, 4)

        def take_gates(hf):
            act.wait_ge(gates_T, hf + 1)
            nc.scalar.activation(gate_T[:, hf * HALF:(hf + 1) * HALF], ps2[0][0:E, hf * HALF:(hf + 1) * HALF],
                                 ACT.Copy).then_inc(gates_copied, 1)

        def gelu(e, slot, units=range(4)):
            for u in units:
                hf, t = u // 2, u % 2
                act.wait_ge(o_ready, e * 2 + 2)
                wait_alone(act, passed, hid_ready, e * 4 + 8 + u + 1)
                nc.scalar.activation(hid[:, slot, t, hf * HALF:(hf + 1) * HALF], psH[u][:, :], ACT.Gelu,
                                     bias=cols[:, bass.ds(B1_COL + 2 * e + t, 1)]).then_inc(gelu_done, 1)

        for hf in range(2):
            take_gates(hf)
            gelu(0, 0, range(2 * hf, 2 * hf + 2))
        gelu(1, 1, range(2))
        act.wait_ge(gap_ready, 1)
        nc.scalar.activation(tgap[:, :], gap[:, :], ACT.Tanh, scale=0.5).then_inc(tgap_ready, 1)
        gelu(1, 1, range(2, 4))
        for hf in range(2):
            act.wait_ge(comb_turned, hf + 1)
            nc.scalar.activation(comb_T[:, hf * HALF:(hf + 1) * HALF], ps2[hf][0:E, 512:1024],
                                 ACT.Copy).then_inc(comb_copied, 1)
        with act.Fori(1, E // 2) as i:
            gelu(2 * i, 0)
            gelu(2 * i + 1, 1)

    def tensor(pe, turn_tokens):
        pe.sem_inc(hid_ready, 8)
        pe.sem_inc(o_ready, 4)

        def gates_of(hf):
            nc.tensor.matmul(ps2[0][0:E, hf * HALF:(hf + 1) * HALF], cols[:, GATE_COL:GATE_COL + E],
                             t_T[:, hf * HALF:(hf + 1) * HALF], start=True, stop=True).then_inc(gates_T, 1)

        def hidden(e, slot, units=range(4)):
            pe.wait_ge(w1c_ready, e + 1)
            for u in units:
                hf, t = u // 2, u % 2
                pe.wait_ge(gelu_done, e * 4 + u + 1)
                nc.tensor.matmul(psH[u][:, :], w1_cur[:, slot, t, :], t_T[:, hf * HALF:(hf + 1) * HALF],
                                 start=True, stop=True).then_inc(hid_ready, 1)

        def outputs(e, slot, rnd, halves=range(2)):
            pe.wait_ge(gelu_done, e * 4 + 4 + 4)
            for hf in halves:
                pe.wait_ge(o_added, rnd * 2 + hf + 1)
                for c in range(4):
                    for t in range(2):
                        last = nc.tensor.matmul(psO[hf][:, c * D:(c + 1) * D],
                                                hid[:, slot, t, (4 * hf + c) * P:(4 * hf + c + 1) * P],
                                                w2_T[:, bass.ds(2 * e + t, 1), :].rearrange("p a d -> p (a d)"),
                                                start=(t == 0), stop=(t == 1))
                last.then_inc(o_ready, 1)

        pe.wait_ge(w_copied, E)
        pe.wait_ge(t_copied, B - 1 + 1)
        pe.wait_ge(out_taken, B + 2)
        pe.wait_ge(z_copied, 4 * B + 1)
        pe.wait_ge(z_normed, 4 * B + 1)
        gates_of(0)
        hidden(0, 0, range(2))
        turn_tokens(B - 1, ps2[1][:, 512:1024])
        pe.wait_ge(t_copied, B + 1)
        gates_of(1)
        hidden(0, 0, range(2, 4))
        pe.wait_ge(gates_copied, 2)
        for t in range(TILES):
            last = nc.tensor.transpose(ps2[0][:, t * E:(t + 1) * E], gate_T[:, t * P:(t + 1) * P], ident[0:E, 0:E])
        last.then_inc(gates, 1)
        hidden(1, 1)
        outputs(0, 0, 0, range(1))
        pe.wait_ge(comb_ready, 1)
        for hf in range(2):
            for c in range(4):
                last = nc.tensor.transpose(ps2[hf][0:E, 512 + c * P:512 + (c + 1) * P], comb[:, 4 * hf + c, :],
                                           ident[:, :])
            last.then_inc(comb_turned, 1)
        outputs(0, 0, 0, range(1, 2))
        for hf in range(2):
            pe.wait_ge(comb_copied, hf + 1)
            pe.wait_ge(o_added, 2 + hf + 1)
            for c in range(4):
                last = nc.tensor.matmul(psO[hf][:, c * D:(c + 1) * D], comb_T[:, (4 * hf + c) * P:(4 * hf + c + 1) * P],
                                        b2_n[:, :], start=True, stop=True)
            last.then_inc(bias_ready, 1)
        with pe.Fori(0, E // 2 - 1) as i:
            hidden(2 * i + 2, 0)
            outputs(2 * i + 1, 1, 2 * i + 2)
            hidden(2 * i + 3, 1)
            outputs(2 * i + 2, 0, 2 * i + 3)
        outputs(E - 1, 1, E)

    def vector(dve, mean_squares, scale_tokens, take_tokens):
        LINKS = 7
        ch = Steps(dve, chain, 0, LINKS)
        mean_squares(B - 1)
        scale_tokens(B - 1)
        take_tokens(B - 1, ps2[1][:, 512:1024])
        dve.wait_ge(gates, 1)
        ch.link(nc.vector.tensor_copy(logits[:, :, :], ps2[0][:, 0:TILES * E].rearrange("p (t e) -> p t e", t=TILES)))
        for t in range(TILES):
            last = nc.vector.max(top8[:, t, :], logits[:, t, :])
        ch.link(last)
        for t in range(TILES):
            last = nc.vector.max_index(idx8[:, t, :], top8[:, t, :], logits[:, t, :])
        ch.link(last)
        nc.vector.tensor_tensor(gap[:, :], top8[:, :, 1], top8[:, :, 0], ALU.subtract).then_inc(gap_ready, 1)
        ch.link(nc.vector.tensor_copy(idx[:, :, :], idx8[:, :, 0:2]))
        dve.wait_ge(x2c_copied, B + 1)
        for hf in range(2):
            nc.vector.tensor_scalar(acc[:, 4 * hf:4 * hf + 4, :], x2_n[:, 4 * hf:4 * hf + 4, :], 2.0, None,
                                    ALU.mult).then_inc(o_added, 1)
        dve.wait_ge(tgap_ready, 1)
        nc.vector.tensor_scalar(wts[:, 0, :], tgap[:, :], -0.5, 0.5, ALU.mult, ALU.add)
        ch.link(nc.vector.tensor_scalar(wts[:, 1, :], tgap[:, :], 0.5, 0.5, ALU.mult, ALU.add))
        bc = lambda v: v.rearrange("p (t a) -> p t a", a=1).broadcast_to((P, TILES, E))
        experts = iota[:, :].rearrange("p (a e) -> p a e", a=1).broadcast_to((P, TILES, E))
        nc.vector.tensor_tensor(comb[:, :, :], experts, bc(idx[:, :, 0]), ALU.is_equal)
        ch.link(nc.vector.tensor_tensor(comb2[:, :, :], experts, bc(idx[:, :, 1]), ALU.is_equal))
        nc.vector.tensor_tensor(comb[:, :, :], comb[:, :, :], bc(wts[:, 0, :]), ALU.mult)
        ch.link(nc.vector.tensor_tensor(comb2[:, :, :], comb2[:, :, :], bc(wts[:, 1, :]), ALU.mult))
        nc.vector.tensor_tensor(comb[:, :, :], comb[:, :, :], comb2[:, :, :], ALU.add).then_inc(comb_ready, 1)
        ch.done()

        def add(e, hf, rnd):
            dve.wait_ge(o_ready, e * 2 + 4 + hf + 1)
            dve.wait_ge(o_added, rnd * 2 + hf + 1)
            for c in range(4):
                t = 4 * hf + c
                last = nc.vector.scalar_tensor_tensor(acc[:, t, :], psO[hf][:, c * D:(c + 1) * D],
                                                      comb[:, t, bass.ds(e, 1)], acc[:, t, :], ALU.mult, ALU.add)
            last.then_inc(o_added, 1)

        dve.wait_ge(comb_ready, 1)
        for hf in range(2):
            add(0, hf, 0)
        for hf in range(2):
            dve.wait_ge(bias_ready, hf + 1)
            dve.wait_ge(o_added, 2 + hf + 1)
            nc.vector.tensor_tensor(acc[:, 4 * hf:4 * hf + 4, :], psO[hf].rearrange("p (t d) -> p t d", t=4),
                                    acc[:, 4 * hf:4 * hf + 4, :], ALU.add).then_inc(o_added, 1)
        with dve.Fori(1, E - 1) as e:
            for hf in range(2):
                add(e, hf, e + 1)
        for hf in range(2):
            add(E - 1, hf, E)
            dve.wait_ge(o_added, 2 * (E + 1) + hf + 1)
            for t in range(4 * hf, 4 * hf + 4):
                last = nc.vector.bn_stats(stats[:, t, :], acc[:, t, :])
            last.then_inc(chain, 1)
            dve.wait_ge(chain, LINKS + hf + 1)
            for t in range(4 * hf, 4 * hf + 4):
                last = nc.vector.bn_aggr(mv[:, t, :], stats[:, t, :])
            last.then_inc(varm_ready, 1)
        for hf in range(2):
            dve.wait_ge(rstdm_ready, hf + 1)
            for t in range(4 * hf, 4 * hf + 4):
                last = nc.vector.tensor_scalar(fin[:, t, :], acc[:, t, :], mv[:, t, 0:1], rstd[:, t:t + 1],
                                               ALU.subtract, ALU.mult)
            last.then_inc(fin_ready, 1)

    moe.sync, moe.gpsimd, moe.scalar, moe.tensor, moe.vector = sync, gpsimd, scalar, tensor, vector
    return moe


def cross_and_moe_block(nc, g):
    passed = g["passed"]
    (x_n, x1b, x1c, x1_T, x2_n, ident, identb, xw_T, xws_T, cols, cols_s, bo_bc, rope, maskb, mask_T, v_aug, neghalf,
     ps, ps2, psx, k_op, q_op, z_Ts, o_T, rot, q_parts, big, res, stats, mv, rstd, ops_loaded, w_loaded,
     early_open, nmax, row_scores, row_max) = (
        g[k] for k in ("x_n", "x1b", "x1c", "x1_T", "x2_n", "ident", "identb", "xw_T", "xws_T", "cols", "cols_s",
                       "bo_bc", "rope", "maskb", "mask_T", "v_aug", "neghalf", "ps", "ps2", "psx", "k_op", "q_op",
                       "z_T", "o_T", "rot", "q_parts", "big", "res", "stats", "mv", "rstd", "ops_loaded",
                       "w_loaded", "early_open", "nmax", "row_scores", "row_max"))

    with ExitStack() as st:
        def sb(name, shape, dt=F32):
            return st.enter_context(nc.sbuf_tensor(name, shape, dt))

        def sem(name):
            return g["top"].enter_context(nc.semaphore(name))

        nrest = sb("nrest", [P, QT, XH])
        m_parts = sb("m_parts", [P, QT, PARTS, XH], BF16)
        m_T = sb("m_T", [PARTS * XH, S], BF16)
        v_cur = sb("v_cur", [P, KT, XH, XD + 1])
        prob = sb("probx", [P, 4, 4 * S])
        z_aug = sb("z_aug", [P, 2, S])
        rsum = sb("rsumx", [P, QT, 4])
        z_n = sb("z_n", [P, QT, XH, XD])
        z_T = sb("z_Tx", [P, S])
        mid = sb("mid", [P, QT, D])
        x2c = sb("x2c", [P, QT, D])
        ms = sb("ms", [P, QT])
        rms = sb("rms", [P, QT])
        t_n = sb("t_n", [P, QT, D])
        t_T = sb("t_T", [P, TOK])
        old = [k_op[:, b, :, :].rearrange("p h k -> p (h k)").bitcast(F32) for b in range(B)]
        w1_T = old[0][:, 0:E * F].rearrange("p (n f) -> p n f", f=P)
        w2_T = old[0][:, E * F:2 * E * F].rearrange("p (n d) -> p n d", d=D)
        w1_cur = sb("w1_cur", [P, 2, 2, P])

        o_made = sem("o_made"); o_out = sem("o_out"); var3_ready = sem("var3_ready"); rstd3_ready = sem("rstd3_ready")
        x13_ready = sem("x13_ready"); x1t_ready = sem("x1t_ready"); x1t_copied = sem("x1t_copied")
        q_proj = sem("q_proj"); qparts3_ready = sem("qparts3_ready"); q3_stored = sem("q3_stored")
        q3_loaded = sem("q3_loaded"); x1b_ready = sem("x1b_ready"); tail_chain = sem("tail_chain")
        pool_tail = sem("pool_tail"); psum_zeroed = sem("psum_zeroed")
        q3_out = sem("q3_out")
        x2c_copied = sem("x2c_copied"); ms_ready = sem("ms_ready"); rms_ready = sem("rms_ready")
        t_ready = sem("t_ready"); t_turned = sem("t_turned"); t_copied = sem("t_copied"); pool_rms = sem("pool_rms")
        w_turned = sem("w_turned"); w_copied = sem("w_copied"); w1c_ready = sem("w1c_ready")
        mparts_ready = sem("mparts_ready")
        shift_turned = sem("shift_turned"); shift_copied = sem("shift_copied"); shift_loaded = sem("shift_loaded")
        v_ready = sem("v_ready"); col_scores = sem("col_scores"); probs = sem("probs"); pv_done = sem("pv_done")
        z_copied = sem("zx_copied"); z_turned = sem("z_turned"); z_normed = sem("z_normed")
        norm_chain = sem("norm_chain"); zn_turned = sem("zn_turned"); zn_copied = sem("zn_copied")
        out_ready = sem("out_ready"); out_taken = sem("out_taken"); var_ready = sem("varx_ready")
        x2_done = sem("x2_done"); ln_chain = sem("ln_chain"); pool_chain = sem("poolx_chain"); pool_ln = sem("pool_ln")

        ALL_OPS = 16 * (OPS_FIXED + B * OPS_K + (B - 1) * OPS_Q)
        w1_raw = big[:, 0:E * F].rearrange("p (n d) -> p n d", d=D)
        w2_raw = big[:, E * F:2 * E * F].rearrange("p (e f) -> p e f", e=E)
        NORM_COL = 2
        ROWS_BEFORE_NORM = 1
        psW = [ps2[0][:, 0:512], ps2[0][:, 512:1024], ps2[1][:, 0:512], ps2[1][:, 512:1024]]
        psz = psx[1][:, 0:S]
        psm = ps[1][:, 0:S]

        def bodies(eng, body):
            body(0, True, True, False)
            body(1, False, True, False)
            with eng.Fori(2, B) as b:
                body(b, False, False, False)
            body(B, False, False, True)

        def due(step, n, first, last):
            gr = step // n - 1
            return gr if step % n == 0 and (gr >= 0 or not first) and (gr < 0 or not last) else None

        moe = mixture(nc, g, st, sem, locals())

        block = st.enter_context(nc.Block())

        @block.sync
        def _(sp):
            sp.sem_inc(shift_loaded, 1)

            def shift(b):
                sp.wait_ge(shift_copied, b + 1)
                sp.dma_start(q_op[SROWS:TROWS, :, bass.ds(b * S, S)], m_T[:, :]).then_inc(shift_loaded, 16)

            for b in range(ROW_LEAD):
                shift(b)
            sp.wait_ge(qparts3_ready, 1)
            q_round(sp, g, B - 1, 16, q3_stored, q3_loaded)
            for n in range(2):
                es = slice(n * E // 2, (n + 1) * E // 2)
                sp.dma_start(w1_raw[:, n * E:(n + 1) * E, :],
                             g["w1"][es].rearrange("e (t p) d -> p (e t) d", p=P)).then_inc(w_loaded[n], 16)
                sp.dma_start(w2_raw[:, es, :], g["w2"][es].rearrange("e d f -> d e f")).then_inc(w_loaded[n], 16)
            with sp.Fori(ROW_LEAD, B) as b:
                shift(b)
            sp.wait_ge(shift_loaded, 16 * B + 1)
            moe.sync(sp)

        @block.gpsimd
        def _(pool):
            pool.sem_inc(x2_done, 1)

            def program(plan):
                def shift_parts(b):
                    ch = Steps(pool, pool_chain, b, 4)
                    pool.wait_ge(shift_turned, b + 1)
                    pool.wait_ge(row_max, (b + 1) * plan.rows + 2)
                    ch.link(nc.gpsimd.tensor_scalar(nrest[:, :, :], nmax[:, b, :, :], SHIFT_MAX, None, ALU.min))
                    ch.link(nc.gpsimd.tensor_copy(m_parts[:, :, 0, :], nrest[:, :, :]))
                    ch.link(nc.gpsimd.tensor_tensor(nrest[:, :, :], nrest[:, :, :], m_parts[:, :, 0, :], ALU.subtract))
                    ch.link(nc.gpsimd.tensor_copy(m_parts[:, :, 1, :], nrest[:, :, :]))
                    nc.gpsimd.tensor_tensor(m_parts[:, :, 2, :], nrest[:, :, :], m_parts[:, :, 1, :],
                                            ALU.subtract).then_inc(mparts_ready, 1)
                    ch.done()

                def layer_norm(b):
                    ch = Steps(pool, pool_ln, b, 3)
                    wait_alone(pool, passed, var_ready, b + 1)
                    ch.link(nc.gpsimd.tensor_scalar(rstd[:, :], mv[:, :, 1], LN_EPS, None, ALU.add))
                    ch.link(nc.gpsimd.tensor_tensor(rstd[:, :], rstd[:, :], neghalf[:, 0:QT], ALU.pow))
                    wide = lambda v: v.rearrange("p (q a) -> p q a", a=1).broadcast_to((P, QT, D))
                    ch.link(nc.gpsimd.tensor_tensor(mid[:, :, :], res[:, :, :], wide(mv[:, :, 0]), ALU.subtract))
                    pool.wait_ge(t_ready, b + 1)
                    pool.wait_ge(x2c_copied, b + 1)
                    nc.gpsimd.tensor_tensor(x2c[:, :, :], mid[:, :, :], wide(rstd[:, :]), ALU.mult).then_inc(x2_done, 1)
                    ch.done()
                    ch = Steps(pool, pool_rms, b, 1)
                    wait_alone(pool, passed, ms_ready, b + 1)
                    ch.link(nc.gpsimd.tensor_scalar(rms[:, :], ms[:, :], RMS_EPS, None, ALU.add))
                    nc.gpsimd.tensor_tensor(rms[:, :], rms[:, :], neghalf[:, 0:QT], ALU.pow).then_inc(rms_ready, 1)
                    ch.done()

                for b in range(ROW_LEAD):
                    shift_parts(b)
                pool.wait_ge(var3_ready, 1)
                nc.gpsimd.tensor_scalar(rstd[:, :], mv[:, :, 1], LN_EPS, None, ALU.add).then_inc(pool_tail, 1)
                pool.wait_ge(pool_tail, 1)
                nc.gpsimd.tensor_tensor(rstd[:, :], rstd[:, :], neghalf[:, 0:QT], ALU.pow).then_inc(rstd3_ready, 1)
                for b in range(ROW_LEAD, B):
                    shift_parts(b)
                with pool.Fori(0, B) as b:
                    layer_norm(b)

            for_either(pool, early_open, program)
            moe.gpsimd(pool)

        @block.scalar
        def _(act):
            act.sem_inc(probs, 2)
            act.sem_inc(z_copied, 1)

            def take_w(n):
                act.wait_ge(w_turned, n + 1)
                dst = (w1_T, w2_T)[n % 2]
                nc.scalar.activation(dst[:, 4 * (n // 2):4 * (n // 2) + 4, :], psW[n % 4].rearrange("p (a c) -> p a c", a=4),
                                     ACT.Copy).then_inc(w_copied, 1)

            def copy_shift(b, bank, c0=0):
                act.wait_ge(shift_turned, b + 1 + 1)
                if b:
                    act.wait_ge(shift_loaded, b * 16 + 1)
                nc.scalar.activation(m_T[:, :], bank.ap()[0:PARTS * XH, c0:c0 + S // 2].bitcast(BF16),
                                     ACT.Copy).then_inc(shift_copied, 1)

            def program(plan):
                n, units = plan.n, plan.units

                def exps(b, u):
                    act.wait_ge(col_scores, b * units + u + 1)
                    act.wait_ge(pv_done, b * units + u + 1)
                    nc.scalar.activation(prob[:, u % 4, :], ps2[u % 2][:, :], ACT.Exp).then_inc(probs, 1)

                def copy_z(b, gr):
                    act.wait_ge(pv_done, b * units + (gr + 1) * n + 4)
                    act.wait_ge(z_turned, b * 4 + gr + 1)
                    nc.scalar.activation(z_aug[:, gr % 2, :], psx[0][:, 0:S],
                                         ACT.Copy).then_inc(z_copied, 1)

                def body(b, first, rows, last):
                    for u in range(OUT_STEP + 1 if last else units):
                        if not last:
                            exps(b, u)
                        gr = due(u - 1, n, first, last)
                        if gr is not None:
                            copy_z(b, gr)
                        if u == 1 and not last:
                            act.wait_ge(pv_done, b * units + 4)
                            nc.scalar.activation(v_cur[:, plan.tiles[0]:, :, :].rearrange("p t h d -> p (t h d)"),
                                                 v_aug[:, b, plan.tiles[0]:, :, :].rearrange("p t h d -> p (t h d)"),
                                                 ACT.Copy).then_inc(v_ready, 1)
                        if u == 0 and first:
                            act.wait_ge(x1t_ready, 1)
                            nc.scalar.activation(x1_T[:, :], psz, ACT.Copy).then_inc(x1t_copied, 1)
                        if last:
                            for n_w in (2 * u, 2 * u + 1):
                                take_w(n_w)
                        if u == units - 1 and rows:
                            copy_shift(b + ROW_LEAD, ps[0])

                copy_shift(0, psx[1])
                copy_shift(1, psx[1], S // 2)
                bodies(act, body)

            for_either(act, early_open, program)
            moe.scalar(act)

        @block.tensor
        def _(pe):
            pe.sem_inc(z_turned, 2)
            pe.sem_inc(shift_turned, 1)
            pe.sem_inc(pv_done, 4)

            def tail_norm():
                pe.wait_ge(shift_copied, 2)
                pe.wait_ge(x13_ready, 1)
                for q in range(QT):
                    last = nc.tensor.transpose(psz[:, q * P:(q + 1) * P], x1c[:, q, :], ident[:, :])
                last.then_inc(x1t_ready, 1)

            def tail_queries():
                pe.wait_ge(x1t_copied, 1)
                for n, w in enumerate((xw_T[:, 0, :], xws_T[:, 0, :])):
                    nc.tensor.matmul(psx[1][:, n * S:(n + 1) * S], w, x1_T[:, :], start=True, stop=True).then_inc(q_proj, 1)

            def turn_w(n, scores_through):
                pe.wait_ge(w_loaded[n // 4], 32)
                if n < 4:
                    pe.wait_ge(probs, scores_through)
                else:
                    pe.wait_ge(w_copied, n - 3)
                src = (w1_raw, w2_raw.rearrange("p e (t f) -> p (e t) f", t=2))[n % 2]
                for c in range(4):
                    last = nc.tensor.transpose(psW[n % 4][:, c * P:(c + 1) * P], src[:, 4 * (n // 2) + c, :], ident[:, :])
                last.then_inc(w_turned, 1)

            def turn_tokens(bb, bank):
                pe.wait_ge(t_ready, bb + 1 + 1)
                for q in range(QT):
                    last = nc.tensor.transpose(bank[:, q * P:(q + 1) * P], t_n[:, q, :], ident[:, :])
                last.then_inc(t_turned, 1)

            def turn_shift(b, bank, c0=0):
                pe.wait_ge(mparts_ready, b + 1)
                for q in range(QT):
                    c = c0 + q * P // 2
                    last = nc.tensor.transpose(bank.ap()[0:PARTS * XH, c:c + P // 2].bitcast(BF16),
                                               m_parts[:, q, :, :].rearrange("p c h -> p (c h)"), identb[:, :])
                last.then_inc(shift_turned, 1)

            def program(plan):
                n, units, width, k0 = plan.n, plan.units, plan.width, plan.k0

                def row_unit(b, i):
                    pe.wait_ge(row_max, b * plan.rows + i + 1)
                    row_scores_unit(nc, pe, g, plan, b, i, row_scores)

                def col_unit(b, u):
                    gr, kt = u // n, plan.tiles[u % n]
                    pe.wait_ge(probs, b * units + u + 1)
                    for hh in range(4):
                        dst = ps2[u % 2][:, hh * S:(hh + 1) * S]
                        nc.tensor.matmul(dst, identb[:, :], mask_T[:, kt, :], start=True, stop=False)
                        last = nc.tensor.matmul(dst, k_op[0:TROWS, b, 4 * gr + hh, kt * P:(kt + 1) * P],
                                                q_op[0:TROWS, 4 * gr + hh, bass.ds(b * S, S)], start=False, stop=True)
                    last.then_inc(col_scores, 1)

                def pv_unit(b, u):
                    gr, kt = u // n, plan.tiles[u % n]
                    pe.wait_ge(probs, b * units + u + 1 + 2)
                    if u % n == 0:
                        pe.wait_ge(z_copied, b * 4 + gr + 1)
                    for hh in range(4):
                        last = nc.tensor.matmul(psx[0][32 * hh:32 * hh + XD + 1, 0:S],
                                                v_cur[:, kt, 4 * (gr % 4) + hh, :], prob[:, u % 4, hh * S:(hh + 1) * S],
                                                start=(u % n == 0), stop=(u % n == n - 1))
                    last.then_inc(pv_done, 1)

                def turn_z(b, gr):
                    pe.wait_ge(z_copied, b * 4 + gr + 1 + 1)
                    pe.wait_ge(z_normed, b * 4 + gr + 1)
                    for q in range(QT):
                        last = nc.tensor.transpose(psz[:, q * P:(q + 1) * P], z_aug[:, gr % 2, q * P:(q + 1) * P],
                                                   ident[:, :])
                    last.then_inc(z_turned, 1)

                def body(b, first, rows, last_body):
                    for u in range(OUT_STEP + 1 if last_body else units):
                        if not last_body:
                            if u == 0:
                                pe.wait_ge(shift_loaded, (b + 1) * 16 + 1)
                            col_unit(b, u)
                        if (u >= 2 or not first) and (u < 2 or not last_body):
                            if u == 2:
                                pe.wait_ge(v_ready, b + 1)
                            if u == 2 and first:
                                pe.wait_ge(psum_zeroed, 1)
                            pv_unit(b, u - 2)
                        if rows and u == 0 and not first:
                            pe.wait_ge(q3_loaded, 16 * OPS_Q)
                        if rows:
                            for i in range(ROWS_A_STEP * u, min(ROWS_A_STEP * (u + 1), plan.rows)):
                                if i == 0 and not first:
                                    pe.wait_ge(shift_copied, b + ROW_LEAD)
                                if i == ROWS_A_STEP * (OUT_STEP + 1) and not first:
                                    pe.wait_ge(out_taken, b + 2)
                                row_unit(b + ROW_LEAD, i)
                                if i == ROWS_BEFORE_NORM - 1 and first:
                                    tail_norm()
                        if u == 0 and first:
                            tail_queries()
                        if u == OUT_STEP and not first:
                            pe.wait_ge(z_normed, b * 4 + 1)
                            pe.wait_ge(out_taken, b + 1)
                            if rows:
                                made = min(ROWS_A_STEP * (u + 1), plan.rows)
                                pe.wait_ge(row_max, (b + ROW_LEAD) * plan.rows + made + 2)
                            for q in range(QT):
                                last = nc.tensor.transpose(psm[:, q * P:(q + 1) * P],
                                                           z_n[:, q, :, :].rearrange("p h d -> p (h d)"), ident[:, :])
                            last.then_inc(zn_turned, 1)
                        gr = due(u - 2, n, first, last_body)
                        if gr is not None:
                            if first and gr == 0:
                                pe.wait_ge(q3_out, 1)
                            turn_z(b, gr)
                        if u == OUT_STEP and not first:
                            pe.wait_ge(zn_copied, b)
                            for q in range(QT):
                                last = nc.tensor.matmul(psm[:, q * P:(q + 1) * P], z_T[:, q * P:(q + 1) * P],
                                                        xw_T[:, 3, :], start=True, stop=True)
                            last.then_inc(out_ready, 1)
                        if last_body:
                            for n_w in (2 * u, 2 * u + 1):
                                turn_w(n_w, B * units + 2)
                        if u == OUT_STEP and not rows:
                            pe.wait_ge(shift_copied, B)
                            pe.wait_ge(t_copied, b - ROW_LEAD + 1)
                            turn_tokens(b - ROW_LEAD, ps[0])
                        if u == units - 1 and rows:
                            turn_shift(b + ROW_LEAD, ps[0])

                out_proj(nc, psx[0], z_Ts, o_T, 0).then_inc(o_made, 1)
                turn_shift(0, psx[1])
                out_proj(nc, psx[0], z_Ts, o_T, 1).then_inc(o_made, 1)
                pe.wait_ge(shift_copied, 1)
                turn_shift(1, psx[1], S // 2)
                pe.wait_ge(ops_loaded, ALL_OPS)
                bodies(pe, body)

            for_either(pe, early_open, program)
            moe.tensor(pe, turn_tokens)

        @block.vector
        def _(dve):
            dve.wait_ge(o_made, 2)
            nc.vector.tensor_tensor(res[:, :, :], psx[0][:, 0:S].rearrange("p (q d) -> p q d", q=QT),
                                    x_n[:, 2 * B - 2:2 * B, :], ALU.add).then_inc(o_out, 1)
            dve.wait_ge(o_out, 1)
            moments(nc, Steps(dve, tail_chain, 0, 2), res, stats, mv, var3_ready, passed)
            nc.vector.memset(psx[0][:, 0:S], 0.0).then_inc(psum_zeroed, 1)
            dve.sem_inc(out_taken, 2)
            dve.sem_inc(z_normed, 1)
            dve.sem_inc(t_ready, 1)
            dve.sem_inc(t_copied, 1)
            dve.sem_inc(x2c_copied, 1)

            def mean_squares(bb):
                dve.wait_ge(x2_done, bb + 1 + 1)
                nc.vector.tensor_copy(x2_n[:, bass.ds(2 * bb, 2), :], x2c[:, :, :]).then_inc(x2c_copied, 1)
                for q in range(QT):
                    last = nc.vector.tensor_tensor_reduce(t_n[:, q, :], x2c[:, q, :], x2c[:, q, :], 1.0 / D, 0.0, ALU.mult,
                                                          ALU.add, ms[:, q:q + 1])
                last.then_inc(ms_ready, 1)

            def scale_tokens(bb):
                dve.wait_ge(rms_ready, bb + 1)
                for q in range(QT):
                    last = nc.vector.tensor_scalar(t_n[:, q, :], x2c[:, q, :], rms[:, q:q + 1], None, ALU.mult)
                last.then_inc(t_ready, 1)

            def take_tokens(bb, bank):
                dve.wait_ge(t_turned, bb + 1)
                nc.vector.tensor_scalar(t_T[:, bass.ds(bb * S, S)], bank[:, 0:S], cols[:, NORM_COL:NORM_COL + 1], None,
                                        ALU.mult).then_inc(t_copied, 1)

            def tail_norm():
                dve.wait_ge(rstd3_ready, 1)
                normalise(nc, res, mv, rstd, x1c, x13_ready)
                dve.wait_ge(x13_ready, 1)
                nc.vector.tensor_tensor(x1b[:, 2 * B - 2:2 * B, :], x1c[:, :, :], both(bo_bc[:, :]),
                                        ALU.add).then_inc(x1b_ready, 1)

            def tail_queries():
                ch = Steps(dve, tail_chain, 0, 4, base=2)
                dve.wait_ge(q_proj, 2)
                for n, bias in enumerate((cols, cols_s)):
                    last = nc.vector.scalar_tensor_tensor(rot[:, n, 0:S], psx[1][:, n * S:(n + 1) * S], bias[:, 0:1],
                                                          rope[:, n, 0:S], ALU.add, ALU.mult)
                last.then_inc(q3_out, 1)
                dve.wait_ge(q3_out, 1)
                dve.wait_ge(ops_loaded, ALL_OPS)
                ch.link(nc.vector.tensor_tensor(rot[:, 0, 0:S], rot[:, 0, 0:S], rot[:, 1, 0:S], ALU.add))
                split_queries(nc, ch, rot, q_parts, qparts3_ready)
                ch.done()

            def program(plan):
                n, units, width = plan.n, plan.units, plan.width

                def row_unit(b, i):
                    dve.wait_ge(row_scores, b * plan.rows + i + 1)
                    row_max_unit(nc, g, plan, b, i, row_max)

                def norm_z(b, gr):
                    dve.wait_ge(z_turned, b * 4 + gr + 1 + 2)
                    z = psz.rearrange("p (q h r) -> p q h r", q=QT, h=4)
                    nc.vector.tensor_scalar(rsum[:, :, :], z[:, :, :, XD], TINY, None, ALU.max).then_inc(norm_chain, 1)
                    dve.wait_ge(norm_chain, (b * 4 + gr) * 2 + 1)
                    nc.vector.reciprocal(rsum[:, :, :], rsum[:, :, :]).then_inc(norm_chain, 1)
                    dve.wait_ge(norm_chain, (b * 4 + gr) * 2 + 2)
                    h0 = 4 * (gr % 4)
                    nc.vector.tensor_tensor(z_n[:, :, h0:h0 + 4, :], z[:, :, :, 0:XD],
                                            rsum[:, :, :].rearrange("p q (h a) -> p q h a", a=1).broadcast_to((P, QT, 4, XD)),
                                            ALU.mult).then_inc(z_normed, 1)

                def body(b, first, rows, last_body):
                    for u in range(OUT_STEP + 1 if last_body else units):
                        if rows:
                            for i in range(ROWS_A_STEP * u, min(ROWS_A_STEP * (u + 1), plan.rows)):
                                row_unit(b + ROW_LEAD, i)
                                if i == ROWS_BEFORE_NORM - 1 and first:
                                    tail_norm()
                        if u == 0 and first:
                            tail_queries()
                        if u == 2 and not rows:
                            mean_squares(b - ROW_LEAD)
                        if u == OUT_STEP and not first:
                            dve.wait_ge(zn_turned, b)
                            nc.vector.tensor_copy(z_T[:, :], psm).then_inc(zn_copied, 1)
                        gr = due(u - 2, n, first, last_body)
                        if gr is not None:
                            norm_z(b, gr)
                        if u == OUT_STEP and not rows:
                            scale_tokens(b - ROW_LEAD)
                        if u == OUT_STEP and not first:
                            if rows:
                                dve.wait_ge(x1b_ready, 1)
                            dve.wait_ge(out_ready, b)
                            dve.wait_ge(x2_done, b)
                            nc.vector.tensor_tensor(res[:, :, :], psm.rearrange("p (q d) -> p q d", q=QT),
                                                    x1b[:, bass.ds(2 * b - 2, 2), :], ALU.add).then_inc(out_taken, 1)
                            dve.wait_ge(out_taken, b + 2)
                            ch = Steps(dve, ln_chain, b - 1, 2)
                            moments(nc, ch, res, stats, mv, var_ready, passed)
                            ch.done()
                        if u == OUT_STEP and not rows:
                            take_tokens(b - ROW_LEAD, ps[0])

                bodies(dve, body)

            for_either(dve, early_open, program)
            moe.vector(dve, mean_squares, scale_tokens, take_tokens)


_INS = ["x", "ctx_1024", "mask_1x1xSxS2_bk1", "L0_attn_Q", "L0_attn_K", "L0_attn_V", "L0_attn_O", "L0_xattn_Wq",
        "L0_xattn_bq", "L0_xattn_Wk", "L0_xattn_bk", "L0_xattn_Wv", "L0_xattn_bv", "L0_xattn_Wo", "L0_xattn_bo",
        "L0_ffn_norm_weight", "L0_ffn_gate_w", "L0_ffn_w1", "L0_ffn_b1", "L0_ffn_w2", "L0_ffn_b2"]


def _constants():
    import numpy as np

    causal = np.zeros((P, S), np.float32)
    causal[:, P:] = np.where(np.arange(P)[None, :] <= np.arange(P)[:, None], 0.0, NEG_CAUSAL)
    inv = np.exp(np.arange(0, XD, 2, dtype=np.float32) * (-(4.0 * np.log(np.float32(10.0))) / XD)).astype(np.float32)
    angle = np.arange(SK, dtype=np.float32)[None, :] * inv[:, None]
    sin, cos = np.sin(angle), np.cos(angle)
    dim = np.arange(P) % XD
    own = np.where((dim % 2 == 0)[:, None], sin[dim // 2], -sin[dim // 2])
    rope = np.stack([own, -cos[dim // 2]], axis=1).astype(np.float32)
    fill = np.zeros((2, B * XH * SK), np.uint16)
    fill[1] = 0x3F80
    return {"ident": np.eye(P, dtype=np.float32), "causal": causal, "rope": rope, "fill": fill,
            "iota": np.arange(E, dtype=np.float32)[None, :]}


def kernel(**inputs):
    import numpy as np
    import concourse.bacc as bacc
    from concourse.bass_utils import run_bass_kernel_spmd

    nc = bacc.Bacc("TRN2", target_bir_lowering=False, num_devices=1)
    arrays, args = {}, []

    def give(name, a):
        a = np.ascontiguousarray(a)
        arrays[name] = a
        args.append(nc.dram_tensor(name, a.shape, mybir.dt.from_np(a.dtype), kind="ExternalInput").ap())

    for name in _INS:
        give(f"in_{name}", inputs[name])
    for name, a in _constants().items():
        give(f"const_{name}", a)
        if name == "fill":
            args[-1] = args[-1].bitcast(BF16)
    args.append(nc.dram_tensor("out_0", (B, S, D), F32, kind="ExternalOutput").ap())
    build(nc, *args)
    r = run_bass_kernel_spmd(nc, [arrays], core_ids=[0])
    return r.results[0]["out_0"]
```
